# Optimizing a Trainium2 kernel written in Bass

```python
import numpy as np
import jax
import jax.numpy as jnp

def _softmax(x, axis=-1):
    return jax.nn.softmax(x, axis=axis)

def _gelu(x):
    return jax.nn.gelu(x, approximate=True)

def _silu(x):
    return jax.nn.silu(x)

def _sigmoid(x):
    return jax.nn.sigmoid(x)

def _layernorm(x, axis=-1, eps=1e-05):
    m = jnp.mean(x, axis=axis, keepdims=True)
    v = jnp.var(x, axis=axis, keepdims=True)
    return (x - m) / jnp.sqrt(v + eps)

def _scatter_add(tgt, idx, src, axis=0):
    return tgt.at[idx].add(src)

def _segment_sum(src, seg, n):
    return jax.ops.segment_sum(src, seg, n)
kernel_name = 'mk_adaln_attn_ffn_d1_seqx_r4_8f3e18'

def setup_inputs(seed: int=0):
    np.random.seed(seed)
    _w = jnp.asarray

    def _rec_inputs():
        import jax
        import jax.numpy as jnp
        _rk = jax.random.key(seed)
        x = -0.0002928 + 1 * jax.random.normal(jax.random.fold_in(_rk, 1), (2, 1024, 256), jnp.float32)
        _lenS = 1024 - jax.random.randint(jax.random.fold_in(_rk, 7), (2,), 0, max(1, 1024 // 4) + 1, jnp.int32)
        _lenS2 = 1024 - jax.random.randint(jax.random.fold_in(_rk, 8), (2,), 0, max(1, 1024 // 4) + 1, jnp.int32)
        itok_Sx32_0_1023 = jax.random.randint(jax.random.fold_in(_rk, 12), (1024, 32), 0, 256, jnp.int32)
        condB_uprev = -0.456674 + 0.753242 * jax.random.normal(jax.random.fold_in(_rk, 14), (2,), jnp.float32)
        condB_tauraws = -5.74692 + 0.777674 * jax.random.normal(jax.random.fold_in(_rk, 15), (2,), jnp.float32)
        cond_256 = -0.000235209 + 0.019331 * jax.random.normal(jax.random.fold_in(_rk, 16), (2, 64), jnp.float32)
        condB_bn2 = jnp.zeros((2,), jnp.float32)
        cond_1024 = -4.10585e-05 + 0.0199478 * jax.random.normal(jax.random.fold_in(_rk, 18), (2, 256), jnp.float32)
        _validS = jnp.arange(1024)[None, :] < _lenS[:, None]
        _validS2 = jnp.arange(1024)[None, :] < _lenS2[:, None]
        _causal = jnp.tril(jnp.ones((1024, 1024), dtype=bool))
        mask_SxS_bk0 = jnp.logical_not(jnp.broadcast_to(_validS[0:1, :], (1024, 1024)))
        mask_Sx32_bk1 = jnp.ones((1024, 32), dtype=bool)
        return (x, itok_Sx32_0_1023, condB_uprev, condB_tauraws, cond_256, condB_bn2, cond_1024, mask_SxS_bk0, mask_Sx32_bk1)
    x, itok_Sx32_0_1023, condB_uprev, condB_tauraws, cond_256, condB_bn2, cond_1024, mask_SxS_bk0, mask_Sx32_bk1 = _rec_inputs()

    def _L0_cond_setup():
        import jax, jax.numpy as jnp
        import numpy as np
        B, S, D, H = (4, 256, 256, 16)
        DH = D // H
        K_SPARSE = 32
        LAMBDA_MAX, ALPHA = (10.0, 5.0)
        SPARSE_THRESHOLD = 1.0
        key = jax.random.key(seed)
        ks = jax.random.split(key, 12)
        x = jax.random.normal(ks[0], (B, S, D), dtype=jnp.float32)
        prior_mask = jax.random.bernoulli(ks[1], 0.1, (S, S))
        prior_indices = jax.random.randint(ks[2], (S, K_SPARSE), 0, S)
        prior_index_mask = jax.random.bernoulli(ks[3], 0.9, (S, K_SPARSE))
        prior_index_mask = prior_index_mask.at[:, 0].set(True)
        u_prev = jax.random.normal(ks[4], (B, 1), dtype=jnp.float32)
        sc = 1.0 / np.sqrt(D)
        Wq = jax.random.normal(ks[5], (D, D), dtype=jnp.float32) * sc
        Wk = jax.random.normal(ks[6], (D, D), dtype=jnp.float32) * sc
        Wv = jax.random.normal(ks[7], (D, D), dtype=jnp.float32) * sc
        Wo = jax.random.normal(ks[8], (D, D), dtype=jnp.float32) * sc
        bq = jnp.zeros((D,), jnp.float32)
        bk = jnp.zeros((D,), jnp.float32)
        bv = jnp.zeros((D,), jnp.float32)
        bo = jnp.zeros((D,), jnp.float32)
        return {'x': x, 'prior_mask': prior_mask, 'prior_indices': prior_indices, 'prior_index_mask': prior_index_mask, 'u_prev': u_prev, 'Wq': Wq, 'bq': bq, 'Wk': Wk, 'bk': bk, 'Wv': Wv, 'bv': bv, 'Wo': Wo, 'bo': bo}
    _L0_cond_all = _L0_cond_setup()
    _L0_cond_in = {k: v for k, v in _L0_cond_all.items() if k in ('Wq', 'bq', 'Wk', 'bk', 'Wv', 'bv', 'Wo', 'bo')}
    del _L0_cond_all

    def _L0_attn_setup():
        import jax, jax.numpy as jnp
        import numpy as np
        N_EMBED = 256
        N_HEAD = 16
        HEAD_DIM = N_EMBED // N_HEAD
        key = jax.random.key(seed)
        ks = jax.random.split(key, 5)
        s = 1.0 / np.sqrt(N_EMBED)
        return {'x': jax.random.normal(ks[0], (4, 512, N_EMBED), dtype=jnp.float32), 'W_kqv': jax.random.normal(ks[1], (3 * N_EMBED, N_EMBED), dtype=jnp.float32) * s, 'b_kqv': jax.random.normal(ks[2], (3 * N_EMBED,), dtype=jnp.float32) * s, 'W_proj': jax.random.normal(ks[3], (N_EMBED, N_EMBED), dtype=jnp.float32) * s, 'b_proj': jax.random.normal(ks[4], (N_EMBED,), dtype=jnp.float32) * s}
    _L0_attn_all = _L0_attn_setup()
    _L0_attn_in = {k: v for k, v in _L0_attn_all.items() if k in ('W_kqv', 'b_kqv', 'W_proj', 'b_proj')}
    del _L0_attn_all

    def _L0_cond2_setup():
        import jax, jax.numpy as jnp
        import numpy as np
        import math
        B, T, E, D = (4, 512, 256, 4)

        def _tau_init(t):
            a = 0.1 ** (1.0 / max(t - 1, 1))
            tt = -math.log(max(a, 1e-10))
            return math.log(math.exp(tt) - 1 + 1e-10)

        def causal_ema(b, tau_raw):
            alpha = jnp.exp(-jax.nn.softplus(tau_raw)).astype(b.dtype)

            def step(h, bt):
                h = alpha * h + bt
                return (h, h)
            h0 = jnp.zeros((b.shape[0], b.shape[2]), b.dtype)
            _, hs = jax.lax.scan(step, h0, jnp.swapaxes(b, 0, 1))
            return jnp.swapaxes(hs, 0, 1)
        key = jax.random.key(seed)
        ks = jax.random.split(key, 10)
        s = 0.02
        return {'x': jax.random.normal(ks[0], (B, T, E), jnp.float32), 'tau_ctx': jnp.float32(_tau_init(max(T // 2, 4))), 'tau_raws': jnp.array([_tau_init(max(T // 2 ** i, 2)) for i in range(D)], jnp.float32), 'Wg': jax.random.normal(ks[1], (E, 2 * E), jnp.float32) * s, 'bg': jnp.full((E,), -0.5, jnp.float32), 'Wn1': jax.random.normal(ks[2], (E // 4, E), jnp.float32) * s, 'bn1': jnp.zeros((E // 4,), jnp.float32), 'Wn2': jax.random.normal(ks[3], (D, E // 4), jnp.float32) * s, 'bn2': jnp.zeros((D,), jnp.float32), 'blend': jax.random.normal(ks[4], (D, E), jnp.float32) * s, 'Wsoma': jax.random.normal(ks[5], (E, E), jnp.float32) * s, 'bsoma': jnp.zeros((E,), jnp.float32), 'Wtemp': jax.random.normal(ks[6], (E, E), jnp.float32) * s, 'btemp': jnp.zeros((E,), jnp.float32), 'Wout': jax.random.normal(ks[7], (E, E), jnp.float32) * s, 'gamma': jnp.ones((E,), jnp.float32), 'beta': jnp.zeros((E,), jnp.float32)}
    _L0_cond2_all = _L0_cond2_setup()
    _L0_cond2_in = {k: v for k, v in _L0_cond2_all.items() if k in ('tau_ctx', 'Wg', 'bg', 'Wn1', 'bn1', 'Wsoma', 'bsoma', 'Wtemp', 'btemp', 'Wout', 'gamma', 'beta')}
    del _L0_cond2_all

    def _L0_ffn_setup():
        import jax, jax.numpy as jnp
        import numpy as np
        B, S, H = (4, 512, 256)
        E, K = (8, 2)
        I_R, I_S = (4 * H, 8 * H)
        CAP_FACTOR = 1.25
        SCALE = 1.0
        key = jax.random.key(seed)
        ks = jax.random.split(key, 9)
        std = 0.02
        return {'x': jax.random.normal(ks[0], (B, S, H), jnp.float32), 'router_w': std * jax.random.normal(ks[1], (E, H), jnp.float32), 'rg': std * jax.random.normal(ks[2], (E, H, I_R), jnp.float32), 'ru': std * jax.random.normal(ks[3], (E, H, I_R), jnp.float32), 'rd': std * jax.random.normal(ks[4], (E, I_R, H), jnp.float32), 'sg': std * jax.random.normal(ks[5], (H, I_S), jnp.float32), 'su': std * jax.random.normal(ks[6], (H, I_S), jnp.float32), 'sd': std * jax.random.normal(ks[7], (I_S, H), jnp.float32)}
    _L0_ffn_all = _L0_ffn_setup()
    _L0_ffn_in = {k: v for k, v in _L0_ffn_all.items() if k in ('router_w', 'rg', 'ru', 'rd', 'sg', 'su', 'sd')}
    del _L0_ffn_all
    return {'x': x, 'itok_Sx32_0_1023': itok_Sx32_0_1023, 'condB_uprev': condB_uprev, 'condB_tauraws': condB_tauraws, 'cond_256': cond_256, 'condB_bn2': condB_bn2, 'cond_1024': cond_1024, 'mask_SxS_bk0': mask_SxS_bk0, 'mask_Sx32_bk1': mask_Sx32_bk1, 'L0_cond_Wq': _L0_cond_in['Wq'], 'L0_cond_bq': _L0_cond_in['bq'], 'L0_cond_Wk': _L0_cond_in['Wk'], 'L0_cond_bk': _L0_cond_in['bk'], 'L0_cond_Wv': _L0_cond_in['Wv'], 'L0_cond_bv': _L0_cond_in['bv'], 'L0_cond_Wo': _L0_cond_in['Wo'], 'L0_cond_bo': _L0_cond_in['bo'], 'L0_attn_W_kqv': _L0_attn_in['W_kqv'], 'L0_attn_b_kqv': _L0_attn_in['b_kqv'], 'L0_attn_W_proj': _L0_attn_in['W_proj'], 'L0_attn_b_proj': _L0_attn_in['b_proj'], 'L0_cond2_tau_ctx': _L0_cond2_in['tau_ctx'], 'L0_cond2_Wg': _L0_cond2_in['Wg'], 'L0_cond2_bg': _L0_cond2_in['bg'], 'L0_cond2_Wn1': _L0_cond2_in['Wn1'], 'L0_cond2_bn1': _L0_cond2_in['bn1'], 'L0_cond2_Wsoma': _L0_cond2_in['Wsoma'], 'L0_cond2_bsoma': _L0_cond2_in['bsoma'], 'L0_cond2_Wtemp': _L0_cond2_in['Wtemp'], 'L0_cond2_btemp': _L0_cond2_in['btemp'], 'L0_cond2_Wout': _L0_cond2_in['Wout'], 'L0_cond2_gamma': _L0_cond2_in['gamma'], 'L0_cond2_beta': _L0_cond2_in['beta'], 'L0_ffn_router_w': _L0_ffn_in['router_w'], 'L0_ffn_rg': _L0_ffn_in['rg'], 'L0_ffn_ru': _L0_ffn_in['ru'], 'L0_ffn_rd': _L0_ffn_in['rd'], 'L0_ffn_sg': _L0_ffn_in['sg'], 'L0_ffn_su': _L0_ffn_in['su'], 'L0_ffn_sd': _L0_ffn_in['sd']}

def reference(x, itok_Sx32_0_1023, condB_uprev, condB_tauraws, cond_256, condB_bn2, cond_1024, mask_SxS_bk0, mask_Sx32_bk1, L0_cond_Wq, L0_cond_bq, L0_cond_Wk, L0_cond_bk, L0_cond_Wv, L0_cond_bv, L0_cond_Wo, L0_cond_bo, L0_attn_W_kqv, L0_attn_b_kqv, L0_attn_W_proj, L0_attn_b_proj, L0_cond2_tau_ctx, L0_cond2_Wg, L0_cond2_bg, L0_cond2_Wn1, L0_cond2_bn1, L0_cond2_Wsoma, L0_cond2_bsoma, L0_cond2_Wtemp, L0_cond2_btemp, L0_cond2_Wout, L0_cond2_gamma, L0_cond2_beta, L0_ffn_router_w, L0_ffn_rg, L0_ffn_ru, L0_ffn_rd, L0_ffn_sg, L0_ffn_su, L0_ffn_sd):
    import jax
    import jax.numpy as jnp

    def _L0_cond_ref(x, prior_mask, prior_indices, prior_index_mask, u_prev, Wq, bq, Wk, bk, Wv, bv, Wo, bo):
        import jax, jax.numpy as jnp
        import numpy as np
        B, S, D, H = (4, 256, 256, 16)
        DH = D // H
        K_SPARSE = 32
        LAMBDA_MAX, ALPHA = (10.0, 5.0)
        SPARSE_THRESHOLD = 1.0
        Bb, Ss, Dd = x.shape
        scale = 1.0 / jnp.sqrt(jnp.asarray(DH, x.dtype))

        def proj(W, b):
            return (x @ W.T + b).reshape(Bb, Ss, H, DH).transpose(0, 2, 1, 3)
        Q, K, V = (proj(Wq, bq), proj(Wk, bk), proj(Wv, bv))
        lam = LAMBDA_MAX * jnp.exp(-ALPHA * u_prev.reshape(Bb))
        use_sparse = lam >= SPARSE_THRESHOLD
        scores = jnp.einsum('bhqd,bhkd->bhqk', Q, K) * scale
        prior_bias = jnp.where(prior_mask[:Ss, :Ss], 0.0, -1.0).astype(x.dtype)
        bias = lam[:, None, None, None] * prior_bias[None, None]
        dense_out = jnp.einsum('bhqk,bhkd->bhqd', jax.nn.softmax(scores + bias, axis=-1), V)
        idx = prior_indices[:Ss]
        Kg = K[:, :, idx]
        Vg = V[:, :, idx]
        s_scores = jnp.einsum('bhsd,bhskd->bhsk', Q, Kg) * scale
        s_scores = jnp.where(prior_index_mask[:Ss][None, None], s_scores, jnp.asarray(-jnp.inf, x.dtype))
        sparse_out = jnp.einsum('bhsk,bhskd->bhsd', jax.nn.softmax(s_scores, axis=-1), Vg)
        out = jnp.where(use_sparse[:, None, None, None], sparse_out, dense_out)
        out = out.transpose(0, 2, 1, 3).reshape(Bb, Ss, Dd)
        return out @ Wo.T + bo

    def _L0_attn_ref(x, W_kqv, b_kqv, W_proj, b_proj):
        import jax, jax.numpy as jnp
        import numpy as np
        N_EMBED = 256
        N_HEAD = 16
        HEAD_DIM = N_EMBED // N_HEAD
        B, S, E = x.shape
        H, D = (N_HEAD, E // N_HEAD)
        kqv = x @ W_kqv.T + b_kqv
        k, q, v = jnp.split(kqv, 3, axis=-1)
        to_heads = lambda t: t.reshape(B, S, H, D).transpose(0, 2, 1, 3)
        k, q, v = (to_heads(k), to_heads(q), to_heads(v))
        scale = 1.0 / np.sqrt(D).astype(np.float32)
        attn = jnp.einsum('bhqd,bhkd->bhqk', q, k) * scale
        causal = jnp.tril(jnp.ones((S, S), dtype=bool))
        attn = jnp.where(causal, attn, -jnp.inf)
        attn = jax.nn.softmax(attn, axis=-1)
        y = jnp.einsum('bhqk,bhkd->bhqd', attn, v)
        y = y.transpose(0, 2, 1, 3).reshape(B, S, E)
        return y @ W_proj.T + b_proj

    def _L0_cond2_ref(x, tau_ctx, tau_raws, Wg, bg, Wn1, bn1, Wn2, bn2, blend, Wsoma, bsoma, Wtemp, btemp, Wout, gamma, beta):
        import jax, jax.numpy as jnp
        import numpy as np
        import math
        B, T, E, D = (4, 512, 256, 4)

        def _tau_init(t):
            a = 0.1 ** (1.0 / max(t - 1, 1))
            tt = -math.log(max(a, 1e-10))
            return math.log(math.exp(tt) - 1 + 1e-10)

        def causal_ema(b, tau_raw):
            alpha = jnp.exp(-jax.nn.softplus(tau_raw)).astype(b.dtype)

            def step(h, bt):
                h = alpha * h + bt
                return (h, h)
            h0 = jnp.zeros((b.shape[0], b.shape[2]), b.dtype)
            _, hs = jax.lax.scan(step, h0, jnp.swapaxes(b, 0, 1))
            return jnp.swapaxes(hs, 0, 1)
        ctx = causal_ema(x, tau_ctx)
        gate_in = jnp.concatenate([x, ctx], axis=-1)
        wg = jax.nn.sigmoid(jnp.einsum('btc,ec->bte', gate_in, Wg) + bg)
        gated = x * wg
        h1 = jax.nn.gelu(jnp.einsum('btc,hc->bth', x, Wn1) + bn1, approximate=False)
        mod = 0.5 + jax.nn.sigmoid(jnp.einsum('bth,dh->btd', h1, Wn2) + bn2)
        traces = jax.vmap(lambda tau, m: causal_ema(gated * m[..., None], tau))(tau_raws, jnp.moveaxis(mod, -1, 0))
        blend_w = jax.nn.softmax(blend, axis=0)
        temporal = jnp.einsum('dbtc,dc->btc', traces, blend_w)
        gate = jax.nn.sigmoid(jnp.einsum('btc,ec->bte', temporal, Wtemp) + btemp)
        soma = jax.nn.gelu(jnp.einsum('btc,ec->bte', x, Wsoma) + bsoma, approximate=False)
        out = jnp.einsum('btc,ec->bte', soma * gate, Wout)
        mu = out.mean(-1, keepdims=True)
        var = out.var(-1, keepdims=True)
        return (out - mu) / jnp.sqrt(var + 1e-05) * gamma + beta

    def _L0_ffn_ref(x, router_w, rg, ru, rd, sg, su, sd):
        import jax, jax.numpy as jnp
        import numpy as np
        B, S, H = (4, 512, 256)
        E, K = (8, 2)
        I_R, I_S = (4 * H, 8 * H)
        CAP_FACTOR = 1.25
        SCALE = 1.0
        b, s, h = x.shape
        T = b * s
        capacity = max(int(CAP_FACTOR * T / E), 1)
        xf = x.reshape(T, h)
        eps = jnp.finfo(x.dtype).eps
        xn = xf * jax.lax.rsqrt(jnp.mean(xf * xf, axis=-1, keepdims=True) + eps)
        logits = xn @ router_w.T
        probs = jax.nn.softmax(logits, axis=-1)
        topk_p, topk_i = jax.lax.top_k(probs, K)
        rw = topk_p / jnp.sum(topk_p, axis=-1, keepdims=True)
        one_hot = jax.nn.one_hot(topk_i, E, dtype=x.dtype)
        mask = one_hot.sum(1)
        wdense = (one_hot * rw[..., None]).sum(1)
        sel = mask.T.astype(bool)
        order = jnp.argsort(~sel, axis=1, stable=True)
        dispatch = order[:, :capacity]
        count = sel.sum(axis=1)
        valid = (jnp.arange(capacity)[None, :] < count[:, None]).astype(x.dtype)
        xg = xf[dispatch]
        gate = jax.nn.silu(jnp.einsum('ech,ehi->eci', xg, rg))
        up = jnp.einsum('ech,ehi->eci', xg, ru)
        eout = jnp.einsum('eci,eih->ech', gate * up, rd)
        w = jnp.take_along_axis(wdense.T, dispatch, axis=1)
        contrib = eout * (w * valid)[..., None]
        routed = jnp.zeros_like(xf).at[dispatch.reshape(-1)].add(contrib.reshape(-1, h))
        shared = jax.nn.silu(x @ sg) * (x @ su) @ sd
        return shared + SCALE * routed.reshape(b, s, h)
    x = x + _L0_attn_ref(_L0_cond_ref(x, mask_SxS_bk0, itok_Sx32_0_1023, mask_Sx32_bk1, condB_uprev[:, None], L0_cond_Wq, L0_cond_bq, L0_cond_Wk, L0_cond_bk, L0_cond_Wv, L0_cond_bv, L0_cond_Wo, L0_cond_bo), L0_attn_W_kqv, L0_attn_b_kqv, L0_attn_W_proj, L0_attn_b_proj)
    x = x + _L0_ffn_ref(_L0_cond2_ref(x, L0_cond2_tau_ctx, condB_tauraws, L0_cond2_Wg, L0_cond2_bg, L0_cond2_Wn1, L0_cond2_bn1, cond_256, condB_bn2, cond_1024, L0_cond2_Wsoma, L0_cond2_bsoma, L0_cond2_Wtemp, L0_cond2_btemp, L0_cond2_Wout, L0_cond2_gamma, L0_cond2_beta), L0_ffn_router_w, L0_ffn_rg, L0_ffn_ru, L0_ffn_rd, L0_ffn_sg, L0_ffn_su, L0_ffn_sd)
    return x

_drawn_inputs = setup_inputs


def setup_inputs(seed=0):
    import zlib

    import numpy as np

    out = dict(_drawn_inputs(seed))
    spreads = {'condB_bn2': (0.0, 0.8),
     'L0_cond_bq': (0.0, 0.8),
     'L0_cond_bk': (0.0, 0.8),
     'L0_cond_bv': (0.0, 0.1),
     'L0_cond_bo': (0.0, 0.1),
     'L0_cond2_bg': (-0.5, 0.6),
     'L0_cond2_bn1': (0.0, 0.8),
     'L0_cond2_bsoma': (0.0, 0.313),
     'L0_cond2_btemp': (0.0, 0.8),
     'L0_cond2_gamma': (1.0, 0.6),
     'L0_cond2_beta': (0.0, 0.8)}
    factors = {'condB_tauraws': 8.0,
     'cond_256': 8.0,
     'cond_1024': 8.0,
     'L0_cond_Wq': 2.877,
     'L0_cond2_Wn1': 8.0,
     'L0_ffn_router_w': 3.16,
     'L0_ffn_rg': 2.852,
     'L0_ffn_ru': 2.815,
     'L0_ffn_rd': 2.812}
    for name, (base, spread) in spreads.items():
        noise = np.random.default_rng([zlib.crc32(name.encode()), seed]).standard_normal(out[name].shape)
        drawn = base * np.exp(spread * noise) if base else spread * noise
        out[name] = jnp.asarray(drawn.astype(out[name].dtype))
    for name, factor in factors.items():
        out[name] = (out[name] * factor).astype(out[name].dtype)
    return out
```

```python
from contextlib import ExitStack

import concourse.bass as bass
from concourse import mybir

ALU = mybir.AluOpType
ACT = mybir.ActivationFunctionType
AX = mybir.AxisListType
F32 = mybir.dt.float32
BF16 = mybir.dt.bfloat16
FP16 = mybir.dt.float16
U8 = mybir.dt.uint8
I32 = mybir.dt.int32
U32 = mybir.dt.uint32

P = 128
B, S, D, H = 2, 1024, 256, 16
DH = D // H
T = B * S
DC = D // P
NT = S // P
HALF = 512
NH = S // HALF
QUAD = 4
NQ = H // QUAD
HB = P // QUAD
K_SPARSE = 32
LAMBDA_MAX, ALPHA, SPARSE_THRESHOLD = 10.0, 5.0, 1.0
SCALE = 1.0 / DH ** 0.5
PARTS = 3
Q_PART = [0, 1, 2, 0, 1, 0]
K_PART = [0, 0, 0, 1, 1, 2]
ROWS = DH * len(Q_PART)
ROWS_M = ROWS + PARTS
NEG = -1e30
HUGE = 1e30
HN = D // 4
ND = 2
E, TOPK = 8, 2
I_R, I_S = 4 * D, 8 * D
CAP = max(int(1.25 * T / E), 1)
SLOTS = E * CAP
FAR = 1e5
LN_EPS = 1e-5
RMS_EPS = 1.1920928955078125e-07

CF = dict(ident=(0, P), sel_num=(P, 2 * P), sel_den=(3 * P, 2 * P), iota_e=(5 * P, E), slot_e=(5 * P + E, E))
CF_W = 5 * P + 2 * E
CB = dict(ident=(0, P), neg_qk=(P, P), neg_kq=(2 * P, P), before=(3 * P, P), ones=(4 * P, P))
CB_W = 5 * P


class Sem:

    def __init__(self, handle):
        self.handle, self.value = handle, 0


class Queue:

    def __init__(self):
        self.items, self.seen = [], {}

    def add(self, fn, after, sem, step):
        waits = []
        for m in after:
            if m is not None and self.seen.get(m[0], 0) < m[1]:
                self.seen[m[0]] = m[1]
                waits = [w for w in waits if w[0] is not m[0]] + [m]
        mark = None
        if sem is not None:
            sem.value += step
            mark = (sem, sem.value)
        self.items.append((waits, fn, sem, step))
        return mark

    def emit(self, engine):
        for waits, fn, sem, step in self.items:
            for s, v in waits:
                engine.wait_ge(s.handle, v)
            ins = fn and fn(engine)
            if sem is not None:
                ins.then_inc(sem.handle, step)


class Ring:

    def __init__(self, bufs):
        self.bufs, self.users, self.n = bufs, [[] for _ in bufs], 0

    def take(self):
        i = self.n % len(self.bufs)
        self.n += 1
        users, self.users[i] = self.users[i], []
        return i, self.bufs[i], users

    def hold(self, i, *marks):
        self.users[i] += marks


def build(nc, A, out):
    ctx = ExitStack()
    with ctx:
        all_sems = []

        def sem(name):
            all_sems.append(Sem(ctx.enter_context(nc.semaphore(name))))
            return all_sems[-1]

        def sb(name, shape, dt=F32, scope=None):
            return (scope or ctx).enter_context(nc.sbuf_tensor("sb_" + name, shape, dt))

        def dram(name, shape, dt):
            return nc.dram_tensor(name, shape, dt, kind="Internal").ap()

        pe, dve, act, pool, sp = (Queue() for _ in range(5))

        def do(queue, fn, after=(), sem=None):
            return queue.add(fn, after, sem, 1)

        def dma(queue, dst, src, after=(), sem=None):
            return queue.add(lambda e: e.dma_start(dst, src), after, sem, 16)

        s_pe = {k: sem(f"pe_{k}") for k in (
            "count", "countT", "proj", "vproj", "max", "maxT", "score", "pv", "sel", "out",
            "mix", "tok", "hT", "logit", "pos", "xT", "gu", "down")}
        s_dve = {k: sem(f"dve_{k}") for k in (
            "const", "index", "onehot", "flag", "bias", "weight", "split", "v", "rowmax", "maxpart",
            "weigh", "norm", "resid", "mix", "scan", "stat", "ln", "route", "act", "comb", "copy")}
        s_act = {k: sem(f"act_{k}") for k in (
            "flag", "count", "split", "exp", "o", "mrow", "y", "gate", "stat", "route", "copy", "silu")}
        s_pool = {k: sem(f"pool_{k}") for k in ("const", "zero")}

        parts = dram("parts", [2, B, 2, PARTS, D, S], BF16)
        count_d = dram("count_qk", [NT, P, S], BF16)
        countT_d = dram("count_kq", [NT, P, S], BF16)
        slots_in = dram("slots_in", [SLOTS, D], F32)
        slots_out = dram("slots_out", [SLOTS + 1, D], F32)

        wide = [ctx.enter_context(nc.psum_tensor(f"wide{i}", [P, 2 * HALF], F32)) for i in range(3)]
        bank = [ctx.enter_context(nc.psum_tensor(f"bank{i}", [P, HALF], F32)) for i in range(2)]
        score_ring = Ring(wide[:2])
        pv_ring = Ring(wide[2:])
        bank_ring = Ring(bank)

        cf = sb("const_f32", [P, CF_W])
        cb = sb("const_bf16", [P, CB_W], BF16)
        F = {k: cf[:, a:a + n] for k, (a, n) in CF.items()}
        C = {k: cb[:, a:a + n] for k, (a, n) in CB.items()}
        xT = sb("xT", [P, DC, T])
        small = sb("small", [P, 64])

        s_load = {}

        def load(name, dst, src, queue=None, after=()):
            if name not in s_load:
                s_load[name] = sem(f"load_{name}")
            return dma(queue or sp, dst, src, after, s_load[name])

        def chunks(ap):
            return ap.rearrange("(c p) m -> p c m", p=P)

        m_cb = load("cb", cb[:], A["const_bf16"])
        m_cf = load("cf", cf[:], A["const_f32"])

        ph1 = ExitStack()

        def s1(name, shape, dt=F32):
            return sb(name, shape, dt, ph1)

        w1 = s1("w_prior", [P, DC, 3 * D])
        w2 = s1("w_causal", [P, DC, 3 * D])
        wo = s1("w_o", [P, DC, D])
        wp = s1("w_proj", [P, DC, D])
        bcol = s1("bias_cols", [P, 6, DC])
        bv = s1("bias_v", [P, 2, D])
        idx_i = s1("index_i", [P, NT, K_SPARSE], I32)
        msk_u = s1("index_mask_u8", [P, NT, K_SPARSE], U8)
        idx_f = s1("index_f", [P, NT, K_SPARSE])
        idx_t = s1("index_t", [P, NT, K_SPARSE])
        msk_f = s1("index_mask", [P, NT, K_SPARSE])
        iota = s1("iota", [P, S], FP16)
        flags = s1("flags", [P, 8, B])
        stack_q = s1("stack_q", [P, 3, QUAD, S], BF16)
        stack_k = s1("stack_k", [P, 3, QUAD, S], BF16)
        weight = s1("weight", [P, NT, S])
        bias = s1("bias", [P, NT, S], BF16)
        prob = s1("prob", [P, 7, S])
        v_aug = s1("v_aug", [P, NT, H, HB])
        o_raw = s1("o_raw", [P, 2, S])
        o_norm = s1("o_norm", [P, DC, S])
        tab = s1("tables", [P, 1, S], BF16)
        tab8 = s1("tables8", [P, 1, S], U8)
        junk_ring = Ring([iota[:, i * HALF:(i + 1) * HALF].bitcast(BF16) for i in range(2)])
        rowmax = s1("rowmax", [P, 2, QUAD, NT, 2])
        mneg = s1("mneg", [P, 4, QUAD, NT])
        mpart = s1("mpart", [P, 2, NT, QUAD, PARTS], BF16)
        mrow = s1("mrow", [PARTS * QUAD, 1, S], BF16)

        m_iota = load("iota", iota[:], A["iota"], act)
        m_idx = load("idx", idx_i[:], A["idx"].rearrange("(n p) j -> p n j", p=P), act)
        m_idx = load("idx", msk_u[:], A["idx_mask"].bitcast(U8).rearrange("(n p) j -> p n j", p=P), act)
        m_x = [load(f"x{b}", xT[:, :, b * S:(b + 1) * S], chunks(A["xT"])[:, :, b * S:(b + 1) * S])
               for b in range(B)]
        m_w1 = load("w1", w1[:], chunks(A["w_prior"]))
        load("small", bcol[:], A["bias_cols"], act)
        load("small", bv[:], A["bias_v"].partition_broadcast(P), act)
        m_small = load("small", flags[:, 0, :], A["u_prev"].partition_broadcast(P), act)
        m_w2 = load("w2", w2[:], chunks(A["w_causal"]))
        load("wo", wo[:], chunks(A["w_o"]))
        m_wo = load("wo", wp[:], chunks(A["w_proj"]))

        m_ones = do(pool, lambda e: e.memset(v_aug[:, :, :, DH:HB], 1.0), (), s_pool["const"])
        for r in range(3):
            m_krows = do(pool, lambda e, r=r: e.memset(stack_k[ROWS:ROWS_M, r], 1.0),
                         [m_ones if r == 0 else m_krows], s_pool["const"])
        m_rowmax0 = do(pool, lambda e: e.memset(rowmax[:], -3e38), [m_krows], s_pool["const"])

        zeros = o_norm[:].rearrange("p c t -> p (c t)")
        m = do(pool, lambda e: e.memset(o_norm[:], 0.0), [m_rowmax0], s_pool["zero"])
        s_zero = sem("zero_slots")
        for r in range(0, SLOTS, P * S * DC // D):
            n = min(P * S * DC // D, SLOTS - r)
            dma(act, slots_in[r:r + n, :].rearrange("(p k) n -> p (k n)", p=P), zeros[:, 0:n * D // P], [m], s_zero)
        m_zero = dma(act, slots_out[SLOTS:SLOTS + 1, :], zeros[0:1, 0:D], [m], s_zero)

        fl = [flags[:, i, :] for i in range(8)]
        m = do(act, lambda e: e.activation(fl[1], fl[0], ACT.Exp, scale=-ALPHA), [m_small], s_act["flag"])
        sf = s_dve["flag"]
        m = do(dve, lambda e: e.tensor_scalar(fl[2], fl[1], LAMBDA_MAX, None, ALU.mult), [m], sf)
        m = do(dve, lambda e: e.tensor_scalar(fl[3], fl[2], SPARSE_THRESHOLD, None, ALU.is_ge), [m], sf)
        m = do(dve, lambda e: e.tensor_scalar(fl[4], fl[3], -1.0, 1.0, ALU.mult, ALU.add), [m], sf)
        m = do(dve, lambda e: e.tensor_scalar(fl[5], fl[3], NEG, None, ALU.mult), [m], sf)
        m = do(dve, lambda e: e.tensor_scalar(fl[2], fl[2], SPARSE_THRESHOLD, None, ALU.min), [m], sf)
        m = do(dve, lambda e: e.scalar_tensor_tensor(out=fl[6], in0=fl[2], scalar=-1.0, in1=fl[4],
                                                     op0=ALU.mult, op1=ALU.mult), [m], sf)
        m = do(act, lambda e: e.activation(fl[1], fl[2], ACT.Exp, scale=-1.0), [m], s_act["flag"])
        m_flag = do(dve, lambda e: e.scalar_tensor_tensor(out=fl[7], in0=fl[1], scalar=-1.0, in1=fl[4],
                                                          op0=ALU.add, op1=ALU.mult), [m], sf)

        si = s_dve["index"]
        m1 = do(dve, lambda e: e.tensor_copy(idx_f[:], idx_i[:]), [m_idx], si)
        m2 = do(dve, lambda e: e.tensor_copy(msk_f[:], msk_u[:]), [m_idx], si)
        m1 = do(dve, lambda e: e.tensor_scalar(idx_t[:], idx_f[:], 0.0, float(S), ALU.is_lt, ALU.mult), [m1], si)
        m1 = do(dve, lambda e: e.tensor_tensor(idx_f[:], idx_f[:], idx_t[:], ALU.add), [m1], si)
        m_index = do(dve, lambda e: e.tensor_scalar(idx_f[:], idx_f[:], 0.0, float(S - 1), ALU.max, ALU.min),
                     [m1], si)

        prob_ring = Ring([prob[:, i, :] for i in range(7)])
        hot_ring = Ring([prob[:, i, 0:HALF].bitcast(BF16) for i in range(4)])
        cnt_sb = Ring([prob[:, 4 + i, 0:HALF].bitcast(BF16) for i in range(2)])
        s_cnt = [sem("count_store0"), sem("count_store1")]
        m_tables = []
        for qt in range(NT):
            i, acc, free = score_ring.take()
            for j in range(K_SPARSE):
                k, hot, hfree = hot_ring.take()
                m = do(dve, lambda e, hot=hot, qt=qt, j=j: e.tensor_scalar(
                    hot, iota[:], idx_f[:, qt, j:j + 1], msk_f[:, qt, j:j + 1], ALU.is_equal, ALU.mult),
                    [m_iota, m_index, *hfree], s_dve["onehot"])
                for h in range(NH):
                    mm = do(pe, lambda e, hot=hot, acc=acc, h=h, j=j: e.matmul(
                        acc[:, h * HALF:(h + 1) * HALF], C["ident"], hot[:, h * HALF:(h + 1) * HALF],
                        start=(j == 0), stop=(j == K_SPARSE - 1)), [m, m_cb, *free],
                        s_pe["count"] if h == NH - 1 else None)
                hot_ring.hold(k, mm)
            c, cnt, cfree = cnt_sb.take()
            m = do(act, lambda e, cnt=cnt, acc=acc: e.activation(cnt, acc[:], ACT.Copy), [mm, *cfree], s_act["count"])
            score_ring.hold(i, m)
            st = dma(sp, count_d[qt], cnt, [m], s_cnt[0])
            bi, bk, bfree = bank_ring.take()
            bkT = bk[:].bitcast(BF16)
            for kb in range(NT):
                mm = do(pe, lambda e, kb=kb, cnt=cnt, bkT=bkT: e.transpose(
                    bkT[:, kb * P:(kb + 1) * P], cnt[:, kb * P:(kb + 1) * P], C["ident"]), [m, *bfree],
                    s_pe["countT"])
            cnt_sb.hold(c, st, mm)
            c, cnt, cfree = cnt_sb.take()
            m = do(act, lambda e, cnt=cnt, bkT=bkT: e.activation(cnt, bkT, ACT.Copy), [mm, *cfree], s_act["count"])
            bank_ring.hold(bi, m)
            st2 = dma(sp, countT_d[:, :, qt * P:(qt + 1) * P].rearrange("k p q -> p k q"),
                      cnt.rearrange("p (k q) -> p k q", k=NT), [m], s_cnt[1])
            cnt_sb.hold(c, st2)
        m_tables = [st, st2]
        for i in range(2):
            junk_ring.hold(i, (s_dve["onehot"], s_dve["onehot"].value))
        m_counted = [st, st2, mm]
        for i in range(7):
            prob_ring.hold(i, *m_counted)

        s_store = [sem(f"parts_store{k}") for k in range(2)]
        split_ring = Ring([
            (prob[:, 0, :], prob[:, 1, :], prob[:, 2, 0:HALF].bitcast(BF16), prob[:, 2, HALF:S].bitcast(BF16),
             prob[:, 3, 0:HALF].bitcast(BF16)),
            (prob[:, 4, :], prob[:, 5, :], prob[:, 6, 0:HALF].bitcast(BF16), prob[:, 6, HALF:S].bitcast(BF16),
             prob[:, 3, HALF:S].bitcast(BF16))])

        def project_qk(att, b, src, ready, w, q_col, k_col):
            marks = []
            for i in range(2):
                split_ring.hold(i, *[u for us in prob_ring.users for u in us])
            for qk, col, scale in ((0, q_col, SCALE), (1, k_col, 1.0)):
                for mc in range(DC):
                    i, acc, free = score_ring.take()
                    for h in range(NH):
                        for c in range(DC):
                            mm = do(pe, lambda e, acc=acc, h=h, c=c, o=col * D + mc * P: e.matmul(
                                acc[:, h * HALF:(h + 1) * HALF], w[:, c, o:o + P],
                                src[:, c, h * HALF:(h + 1) * HALF], start=(c == 0), stop=(c == DC - 1)),
                                [*ready, *free], s_pe["proj"] if (h, c) == (NH - 1, DC - 1) else None)
                    k, (val, rem, hi, mid, lo), sfree = split_ring.take()
                    bc = bcol[:, 2 * att + qk, mc:mc + 1]
                    m0 = do(dve, lambda e, val=val, acc=acc, bc=bc, scale=scale: e.tensor_scalar(
                        val, acc[:], bc, scale, ALU.add, ALU.mult), [mm, m_small, *sfree], s_dve["split"])
                    score_ring.hold(i, m0)
                    m1 = do(act, lambda e, val=val, hi=hi: e.activation(hi, val, ACT.Copy), [m0], s_act["split"])
                    m2 = do(dve, lambda e, val=val, hi=hi, rem=rem: e.tensor_tensor(rem, val, hi, ALU.subtract),
                            [m1], s_dve["split"])
                    m3 = do(act, lambda e, rem=rem, mid=mid: e.activation(mid, rem, ACT.Copy), [m2], s_act["split"])
                    m4 = do(dve, lambda e, rem=rem, mid=mid, lo=lo: e.tensor_tensor(lo, rem, mid, ALU.subtract),
                            [m3], s_dve["split"])
                    for part, (t, mk) in enumerate(((hi, m1), (mid, m3), (lo, m4))):
                        st = dma(sp, parts[att, b, qk, part, mc * P:(mc + 1) * P, :], t, [mk], s_store[k])
                    split_ring.hold(k, st)
                    marks.append(st)
            for i in range(7):
                prob_ring.hold(i, *marks[-2:])
            return marks[-2:]

        v_ring = Ring([v_aug])

        def project_v(att, src, ready, w, col):
            _, _, vfree = v_ring.take()
            for kt in range(NT):
                i, bk, free = bank_ring.take()
                for c in range(DC):
                    mm = do(pe, lambda e, bk=bk, c=c, kt=kt: e.matmul(
                        bk[:, 0:D], src[:, c, kt * P:(kt + 1) * P], w[:, c, col * D:(col + 1) * D],
                        start=(c == 0), stop=(c == DC - 1)), [*ready, *free],
                        s_pe["vproj"] if c == DC - 1 else None)
                m = do(dve, lambda e, bk=bk, kt=kt: e.tensor_tensor(
                    v_aug[:, kt, :, 0:DH], bk[:, 0:D].rearrange("p (h d) -> p h d", h=H),
                    bv[:, att, :].rearrange("p (h d) -> p h d", h=H), ALU.add),
                    [mm, m_small, m_ones, *vfree], s_dve["v"])
                bank_ring.hold(i, m)
            return m

        s_tab = sem("load_tables")
        tab_ring = Ring([(tab[:, 0, :], tab8[:, 0, :])])
        key_users = {"bias": [], "weight": []}

        def key_weights(b):
            for qt in range(NT):
                i, (t, t8), free = tab_ring.take()
                dma(sp, t, count_d[qt], [*m_tables, *free], s_tab)
                m = dma(sp, t8, A["prior"].bitcast(U8)[qt * P:(qt + 1) * P, :], [], s_tab)
                m = do(dve, lambda e, t=t: e.tensor_scalar(t, t, 0.0, fl[5][:, b:b + 1], ALU.is_equal, ALU.mult),
                       [m, m_flag], s_dve["bias"])
                o = bias[:, qt, :]
                m2 = do(dve, lambda e, t8=t8, o=o: e.tensor_scalar(
                    o, t8, 0.0, fl[6][:, b:b + 1], ALU.is_equal, ALU.mult), key_users["bias"], s_dve["bias"])
                m_b = do(dve, lambda e, t=t, o=o: e.tensor_tensor(o, o, t, ALU.add), [m, m2], s_dve["bias"])
                tab_ring.hold(i, m_b)
            for kt in range(NT):
                i, (t, t8), free = tab_ring.take()
                dma(sp, t, countT_d[kt], free, s_tab)
                m = dma(sp, t8, A["priorT"].bitcast(U8)[kt * P:(kt + 1) * P, :], [], s_tab)
                m = do(dve, lambda e, t=t: e.tensor_scalar(t, t, fl[3][:, b:b + 1], fl[4][:, b:b + 1],
                                                           ALU.mult, ALU.add), [m, m_flag], s_dve["weight"])
                o = weight[:, kt, :]
                m2 = do(dve, lambda e, t8=t8, o=o: e.tensor_scalar(
                    o, t8, 0.0, fl[7][:, b:b + 1], ALU.is_equal, ALU.mult), key_users["weight"], s_dve["weight"])
                m_w = do(dve, lambda e, t=t, o=o: e.tensor_tensor(o, o, t, ALU.add), [m, m2], s_dve["weight"])
                tab_ring.hold(i, m_w)
            return m_b, m_w

        stack_ring = Ring([0, 1, 2])
        s_stack = [sem(f"load_stack{r}") for r in range(3)]
        s_mrow = sem("store_mrow")
        rowmax_ring = Ring([0, 1])
        mrow_ring = Ring([0])
        mpart_ring = Ring([0, 1])
        o_ring = Ring([0, 1])
        onorm_ring = Ring([o_norm])
        onorm_ring.hold(0, m_zero)

        def load_stack(att, b, q, stored):
            r, _, free = stack_ring.take()
            for qk, (dst, which) in enumerate(((stack_q, Q_PART), (stack_k, K_PART))):
                for blk, part in enumerate(which):
                    src = parts[att, b, qk, part, q * QUAD * DH:(q + 1) * QUAD * DH, :]
                    m = dma(sp, dst[blk * DH:(blk + 1) * DH, r], src.rearrange("(h d) t -> d h t", d=DH),
                            [*stored, *free], s_stack[r])
            return r, m

        def max_units(att, q, r, loaded, m_bias):
            causal = att == 1
            mi, _, free_mx = rowmax_ring.take()
            m_last = {}

            def unit(h, qt, half):
                lo, hi = half * HALF, min((half + 1) * HALF, (qt + 1) * P if causal else S)
                diag = causal and hi == (qt + 1) * P
                i, bk, free = bank_ring.take()
                mm = do(pe, lambda e: e.matmul(
                    bk[:, 0:hi - lo], stack_q[0:ROWS, r, h, qt * P:(qt + 1) * P], stack_k[0:ROWS, r, h, lo:hi],
                    start=True, stop=not diag), [loaded, *free], None if diag else s_pe["max"])
                if diag:
                    mm = do(pe, lambda e: e.matmul(bk[:, hi - lo - P:hi - lo], C["ident"], C["neg_qk"],
                                                   start=False, stop=True), [m_cb], s_pe["max"])
                acc = rowmax[:, mi, h, qt, half:half + 1]
                if causal:
                    m = do(dve, lambda e: e.tensor_reduce(acc, bk[:, 0:hi - lo], AX.X, ALU.max),
                           [mm, *free_mx, m_rowmax0], s_dve["rowmax"])
                else:
                    ji, scrap, jfree = junk_ring.take()
                    m = do(dve, lambda e: e.tensor_tensor_reduce(
                        out=scrap, in0=bk[:], in1=bias[:, qt, lo:hi], scale=1.0, scalar=-3e38,
                        op0=ALU.add, op1=ALU.max, accum_out=acc), [mm, m_bias, *free_mx, m_rowmax0, *jfree],
                        s_dve["rowmax"])
                    junk_ring.hold(ji, m)
                bank_ring.hold(i, m)
                m_last["max"] = m

            def finish():
                sm = s_dve["maxpart"]
                pi, _, pfree = mpart_ring.take()
                top, neg, rem, rem2 = (mneg[:, k] for k in range(4))

                def part(k):
                    return mpart[:, pi, :, :, k].rearrange("p n h -> p h n")

                if causal:
                    m = do(dve, lambda e: e.tensor_reduce(
                        top[:, :, 0:NT // 2], rowmax[:, mi, :, 0:NT // 2, 0:1], AX.X, ALU.max),
                        [m_last["max"], *pfree], sm)
                    m = do(dve, lambda e: e.tensor_reduce(
                        top[:, :, NT // 2:NT], rowmax[:, mi, :, NT // 2:NT, :], AX.X, ALU.max), [m], sm)
                else:
                    m = do(dve, lambda e: e.tensor_reduce(top, rowmax[:, mi], AX.X, ALU.max),
                           [m_last["max"], *pfree], sm)
                rowmax_ring.hold(mi, m)
                m = do(dve, lambda e: e.tensor_scalar(neg, top, -1.0, None, ALU.mult), [m], sm)
                m = do(dve, lambda e: e.tensor_copy(part(0), neg), [m], sm)
                m = do(dve, lambda e: e.tensor_tensor(rem, neg, part(0), ALU.subtract), [m], sm)
                m = do(dve, lambda e: e.tensor_copy(part(1), rem), [m], sm)
                m = do(dve, lambda e: e.tensor_tensor(rem2, rem, part(1), ALU.subtract), [m], sm)
                m = do(dve, lambda e: e.tensor_copy(part(2), rem2), [m], sm)
                i, bk, free = bank_ring.take()
                rows = bk[0:PARTS * QUAD].bitcast(BF16)
                for qt in range(NT):
                    mm = do(pe, lambda e, qt=qt: e.transpose(
                        rows[:, qt * P:(qt + 1) * P], mpart[:, pi, qt].rearrange("p h k -> p (h k)"), C["ident"]),
                        [m, *free], s_pe["maxT"] if qt == NT - 1 else None)
                mpart_ring.hold(pi, mm)
                ri, _, rfree = mrow_ring.take()
                m = do(act, lambda e: e.activation(mrow[:, ri], rows, ACT.Copy), [mm, *rfree], s_act["mrow"])
                bank_ring.hold(i, m)
                for h in range(QUAD):
                    md = dma(sp, stack_q[ROWS:ROWS_M, r, h], mrow[h * PARTS:(h + 1) * PARTS, ri], [m], s_mrow)
                mrow_ring.hold(ri, md)
                m_last["rows"] = md

            steps = []
            for h in range(QUAD):
                for qt in range(NT):
                    for half in range(NH):
                        if not causal or half * HALF < (qt + 1) * P:
                            steps.append(lambda h=h, qt=qt, half=half: unit(h, qt, half))
            steps.append(finish)
            return steps, m_last

        def attend(att, b, stored, m_keys, make_v, prefetch=None):
            causal = att == 1
            m_bias, m_weight = m_keys
            stacks = [load_stack(att, b, q, stored) for q in range(2)]
            _, _, norm_free = onorm_ring.take()
            steps, m_max = max_units(att, 0, *stacks[0], m_bias)
            for st in steps:
                st()
            m_v = make_v()
            o_pair = []
            for q in range(NQ):
                r, loaded = stacks[q]
                m_rows = m_max["rows"]
                if q + 2 < NQ:
                    stacks.append(load_stack(att, b, q + 2, stored))
                if q + 1 < NQ:
                    steps, m_max = max_units(att, q + 1, *stacks[q + 1], m_bias)
                else:
                    steps = []
                n_steps, done, total = len(steps), 0, QUAD * NT
                _, pv, pvfree = pv_ring.take()

                def values(kt, ps):
                    for half in range(NH):
                        lo = max(half * HALF, kt * P) if causal else half * HALF
                        hi = (half + 1) * HALF
                        if lo >= hi:
                            continue
                        last = kt == (hi // P - 1 if causal else NT - 1)
                        for g, (i, p, m) in enumerate(ps):
                            mm = do(pe, lambda e, g=g, p=p, lo=lo, hi=hi, last=last, q=q, pv=pv: e.matmul(
                                pv[g * HB:(g + 1) * HB, lo:hi], v_aug[:, kt, q * QUAD + g, :], p[:, lo:hi],
                                start=(kt == 0), stop=last), [m, m_v, *pvfree], s_pe["pv"])
                    for i, _, _ in ps:
                        prob_ring.hold(i, mm)
                    return mm

                waiting = None
                for kt in range(NT):
                    ps = []
                    for g in range(QUAD):
                        first = kt * P if causal else 0
                        i, sc, free = score_ring.take()
                        for half in range(NH):
                            lo, hi = max(half * HALF, first), (half + 1) * HALF
                            if lo >= hi:
                                continue
                            diag = causal and lo == first
                            mm = do(pe, lambda e, sc=sc, lo=lo, hi=hi, g=g, kt=kt, diag=diag, r=r: e.matmul(
                                sc[:, lo:hi], stack_k[0:ROWS_M, r, g, kt * P:(kt + 1) * P],
                                stack_q[0:ROWS_M, r, g, lo:hi], start=True, stop=not diag),
                                [m_rows, m_krows, loaded, *free], s_pe["score"])
                            if diag:
                                mm = do(pe, lambda e, sc=sc, lo=lo: e.matmul(
                                    sc[:, lo:lo + P], C["ident"], C["neg_kq"], start=False, stop=True),
                                    [], s_pe["score"])
                        k, p, pfree = prob_ring.take()
                        m = do(act, lambda e, p=p, sc=sc, first=first: e.activation(
                            p[:, first:S], sc[:, first:S], ACT.Exp), [mm, *pfree], s_act["exp"])
                        score_ring.hold(i, m)
                        if not causal:
                            m = do(dve, lambda e, p=p, kt=kt: e.scalar_tensor_tensor(
                                out=p, in0=p, scalar=HUGE, in1=weight[:, kt, :], op0=ALU.min, op1=ALU.mult),
                                [m, m_weight], s_dve["weigh"])
                            m_weighed = m
                        ps.append((k, p, m))
                        due = (kt * QUAD + g + 1) * n_steps // total
                        while done < due:
                            steps[done]()
                            done += 1
                        if g == 1 and waiting is not None:
                            values(*waiting)
                            waiting = None
                    waiting = (kt, ps)
                mm = values(*waiting)
                stack_ring.hold(r, mm)
                oi, _, ofree = o_ring.take()
                m = do(act, lambda e, oi=oi, pv=pv: e.activation(o_raw[:, oi], pv[:], ACT.Copy), [mm, *ofree], s_act["o"])
                pv_ring.hold(0, m)
                o_pair.append((oi, m))
                if len(o_pair) == 2:
                    c = q // 2
                    for half in range(NH):
                        cols = slice(half * HALF, (half + 1) * HALF)
                        outs = []
                        for which in ("sel_den", "sel_num"):
                            i, bk, free = bank_ring.take()
                            for par, (oi, m) in enumerate(o_pair):
                                mm = do(pe, lambda e, bk=bk, par=par, oi=oi, which=which, cols=cols: e.matmul(
                                    bk[:], F[which][:, par * P:(par + 1) * P], o_raw[:, oi, cols],
                                    start=(par == 0), stop=(par == 1)), [m, m_cf, *free], s_pe["sel"])
                            outs.append((i, bk, mm))
                        (i0, den, md), (i1, num, mn) = outs
                        on = o_norm[:, c, cols]
                        m = do(dve, lambda e, on=on, den=den: e.reciprocal(on, den[:]), [md, *norm_free], s_dve["norm"])
                        bank_ring.hold(i0, m)
                        m = do(dve, lambda e, on=on, num=num: e.tensor_tensor(on, on, num[:], ALU.mult),
                               [m, mn], s_dve["norm"])
                        bank_ring.hold(i1, m)
                    for oi, _ in o_pair:
                        o_ring.hold(oi, mm)
                    o_pair = []
            v_ring.hold(0, mm)
            if not causal:
                key_users["bias"] = [m_max_last(s_dve["rowmax"])]
                key_users["weight"] = [m_weighed]
            return m

        def m_max_last(s):
            return (s, s.value)

        def xs(b):
            return xT[:, :, b * S:(b + 1) * S]

        stored = [project_qk(0, b, xs(b), [m_x[b], m_w1], w1, 0, 1) for b in range(B)]
        m_resid = []
        for b in range(B):
            keys = key_weights(b)
            m_o = attend(0, b, stored[b], keys,
                         lambda b=b: project_v(0, xs(b), [m_x[b], m_w1], w1, 2))
            y1 = o_raw
            yfree = [u for us in o_ring.users for u in us]
            for mc in range(DC):
                i, acc, free = score_ring.take()
                for h in range(NH):
                    for c in range(DC):
                        mm = do(pe, lambda e, acc=acc, h=h, c=c, mc=mc: e.matmul(
                            acc[:, h * HALF:(h + 1) * HALF], wo[:, c, mc * P:(mc + 1) * P],
                            o_norm[:, c, h * HALF:(h + 1) * HALF], start=(c == 0), stop=(c == DC - 1)),
                            [m_o, m_wo, *free], s_pe["out"])
                m_y = do(act, lambda e, acc=acc, mc=mc: e.activation(
                    y1[:, mc, :], acc[:], ACT.Identity, bias=bcol[:, 4, mc:mc + 1]), [mm, *yfree], s_act["y"])
                score_ring.hold(i, m_y)
            onorm_ring.hold(0, mm)
            st2 = project_qk(1, b, y1, [m_y, m_w2], w2, 1, 0)
            m_v2 = project_v(1, y1, [m_y, m_w2], w2, 2)
            for i in range(2):
                o_ring.hold(i, (s_pe["vproj"], s_pe["vproj"].value), (s_pe["proj"], s_pe["proj"].value))
            m_o = attend(1, b, st2, (None, None), lambda m=m_v2: m)
            for mc in range(DC):
                i, acc, free = score_ring.take()
                for h in range(NH):
                    for c in range(DC):
                        mm = do(pe, lambda e, acc=acc, h=h, c=c, mc=mc: e.matmul(
                            acc[:, h * HALF:(h + 1) * HALF], wp[:, c, mc * P:(mc + 1) * P],
                            o_norm[:, c, h * HALF:(h + 1) * HALF], start=(c == 0), stop=(c == DC - 1)),
                            [m_o, m_wo, *free], s_pe["out"])
                m = do(dve, lambda e, acc=acc, mc=mc, b=b: e.scalar_tensor_tensor(
                    out=xs(b)[:, mc, :], in0=acc[:], scalar=bcol[:, 5, mc:mc + 1], in1=xs(b)[:, mc, :],
                    op0=ALU.add, op1=ALU.add), [mm], s_dve["resid"])
                score_ring.hold(i, m)
            onorm_ring.hold(0, mm)
            m_resid.append(m)
        ph1.close()
        end1 = [(s, s.value) for s in all_sems if s.value]
        ph2 = ExitStack()

        def s2(name, shape, dt=F32):
            return sb(name, shape, dt, ph2)

        w_g = s2("w_g", [P, 2 * DC, D])
        w_n1 = s2("w_n1", [P, DC, HN])
        w_n2 = s2("w_n2", [HN, ND, P])
        w_soma = s2("w_soma", [P, DC, D])
        w_temp = s2("w_temp", [P, DC, D])
        w_out = s2("w_out", [P, DC, D])
        w_rt = s2("w_router", [P, DC, E])
        mcol = s2("mix_cols", [P, 3, DC])
        b_n1 = s2("b_n1", [HN, 1])
        b_n2 = s2("b_n2", [P, ND])
        blend = s2("blend", [P, ND, DC])
        ln_rows = s2("ln_rows", [P, 2, D])
        taus = s2("taus", [P, 1 + ND])
        tiny = s2("tiny", [P, 8, 8])
        wsg = s2("sg", [P, DC, I_S])
        wsu = s2("su", [P, DC, I_S])
        wsd = s2("sd", [P, I_S // P, D])
        h_tok = s2("h_tok", [P, B * NT, D])
        y = h_tok
        hT = s2("hT", [P, DC, T])
        big = s2("big", [P, 15 * S])

        def big_at(k, n):
            return big[:, k * S:(k + n) * S]

        ctxT, gated, tr0, tr1, soma, gate = (
            big_at(2 * k, 2).rearrange("p (c t) -> p c t", c=DC) for k in range(6))
        mod = big_at(12, 2).rearrange("p (c t) -> p c t", c=ND)
        h1 = big_at(14, 1)[0:HN]
        WE = 2 * DC * I_R + (I_R // P) * D
        stats = s2("stats", [P, 4, 6])
        mean_var = s2("mean_var", [P, B * NT, 2])
        rstd = s2("rstd", [P, B * NT])
        ssq = s2("ssq", [P, B * NT])
        rms = s2("rms", [P, B * NT])
        logit = s2("logit", [P, B * NT, E])
        top8 = s2("top8", [P, B * NT, 8])
        best = s2("best", [P, B * NT, 8], U32)
        best_f = s2("best_f", [P, B * NT, TOPK])
        lmax = s2("lmax", [P, B * NT])
        pick = s2("pick", [P, TOPK, B * NT, E])
        mask = s2("mask", [P, B * NT, E], BF16)
        before = s2("before", [P, B * NT + 1, E], BF16)
        slot_map = s2("slot_map", [P, B * NT, E])
        far = s2("far", [P, B * NT, E])
        slot = s2("slot", [P, TOPK, B * NT])
        slot_w = s2("slot_w", [P, TOPK, B * NT], U32)
        slot_r = s2("slot_r", [P, TOPK, B * NT], U32)
        gain = s2("gain", [P, TOPK, B * NT])
        gsum = s2("gsum", [P, B * NT])
        sil = s2("sil", [P, 2, HALF])
        act_s = s2("act_s", [P, 3, HALF])
        xg = s2("xg", [P, 2, 3, D])
        xgT = s2("xgT", [P, 2, DC, CAP])
        act_e = big_at(12, 3)[:, 0:I_R // P * CAP].rearrange("p (i n) -> p i n", n=CAP)
        e_out = s2("e_out", [P, 2, 3, D])
        got = [w[:, c] for w in (w_soma, w_temp) for c in range(DC)]

        load("mix", w_g[:], chunks(A["w_g"]), after=end1)
        load("mix", w_n1[:], chunks(A["w_n1"]))
        load("mix", w_n2[:], A["w_n2"])
        load("mix", w_soma[:], chunks(A["w_soma"]))
        load("mix", w_temp[:], chunks(A["w_temp"]))
        load("mix", w_out[:], chunks(A["w_out"]))
        load("mix", w_rt[:], chunks(A["w_router"]))
        load("mix", mcol[:], A["mix_cols"])
        load("mix", b_n1[:], A["b_n1"])
        load("mix", blend[:], A["blend"])
        load("mix", ln_rows[:], A["ln_rows"].partition_broadcast(P))
        load("mix", b_n2[:], A["b_n2"].partition_broadcast(P))
        m_mw = load("mix", taus[:], A["taus"].partition_broadcast(P))
        m_sg = load("sg", wsg[:], chunks(A["sg"]))
        m_su = load("su", wsu[:], chunks(A["su"]))
        m_sd = load("sd", wsd[:], chunks(A["sd"]))

        sx = s_dve["mix"]
        alpha, ex, bmax, bw, bsum = (tiny[:, k] for k in range(5))
        m = do(act, lambda e: e.activation(ex[:, 0:3], taus[:], ACT.Exp), [m_mw, *end1], s_act["gate"])
        m = do(dve, lambda e: e.tensor_scalar(ex[:, 0:3], ex[:, 0:3], 1.0, None, ALU.add), [m, *end1], sx)
        m_alpha = do(dve, lambda e: e.reciprocal(alpha[:, 0:3], ex[:, 0:3]), [m], sx)
        m = do(dve, lambda e: e.tensor_tensor(bmax[:, 0:DC], blend[:, 0], blend[:, 1], ALU.max), [m_mw], sx)
        for d in range(ND):
            m = do(dve, lambda e, d=d: e.tensor_tensor(bw[:, d * DC:(d + 1) * DC], blend[:, d], bmax[:, 0:DC],
                                                       ALU.subtract), [m], sx)
        m = do(act, lambda e: e.activation(bw[:, 0:4], bw[:, 0:4], ACT.Exp), [m], s_act["gate"])
        m = do(dve, lambda e: e.tensor_tensor(bsum[:, 0:DC], bw[:, 0:DC], bw[:, DC:2 * DC], ALU.add), [m], sx)
        m = do(dve, lambda e: e.reciprocal(bmax[:, 0:DC], bsum[:, 0:DC]), [m], sx)
        for d in range(ND):
            m_bw = do(dve, lambda e, d=d: e.tensor_tensor(bw[:, d * DC:(d + 1) * DC], bw[:, d * DC:(d + 1) * DC],
                                                          bmax[:, 0:DC], ALU.mult), [m], sx)
            m = m_bw

        m_before = do(dve, lambda e: e.memset(before[:, 0, :], 0.0), [], s_dve["route"])

        wide_ring = Ring(wide)
        bank_ring = Ring(bank)

        def matvec(dst_ring, K, wt, srcs, after, sem_, rows=P):
            i, acc, free = dst_ring.take()
            for h in range(NH):
                for k in range(K):
                    mm = do(pe, lambda e, h=h, k=k: e.matmul(
                        acc[0:rows, h * HALF:(h + 1) * HALF], wt(k), srcs(k)[:, h * HALF:(h + 1) * HALF],
                        start=(k == 0), stop=(k == K - 1)), [*after, *free],
                        sem_ if (h, k) == (NH - 1, K - 1) else None)
            return i, acc, mm

        def feature_cols(w, mc):
            return lambda k: w[:, k, mc * P:(mc + 1) * P]

        mix_free = []
        logit_bank = {}

        def mix(b):
            x = xs(b)
            sp_, sa, sd_ = s_pe["mix"], s_act["gate"], s_dve["mix"]
            ready = [m_resid[b], m_mw]
            m_ctx = [do(dve, lambda e, c=c: e.tensor_tensor_scan(
                ctxT[:, c], alpha[:, 0:1].broadcast_to([P, S]), x[:, c], 0.0, ALU.mult, ALU.add),
                [*ready, m_alpha, *mix_free], s_dve["scan"]) for c in range(DC)][-1]
            i, acc, mm = matvec(wide_ring, DC, lambda k: w_n1[:, k], lambda k: x[:, k], ready, sp_, HN)
            m_h1 = do(act, lambda e, acc=acc: e.activation(h1, acc[0:HN], ACT.Gelu, bias=b_n1[:]), [mm, *mix_free], sa)
            wide_ring.hold(i, m_h1)
            m_soma = []
            for mc in range(DC):
                i, acc, mm = matvec(wide_ring, DC, feature_cols(w_soma, mc), lambda k: x[:, k], ready, sp_)
                m_soma.append(do(act, lambda e, acc=acc, mc=mc: e.activation(
                    soma[:, mc], acc[:], ACT.Gelu, bias=mcol[:, 1, mc:mc + 1]), [mm], sa))
                wide_ring.hold(i, m_soma[-1])
            m_mod = []
            for d in range(ND):
                i, acc, mm = matvec(wide_ring, 1, lambda k, d=d: w_n2[:, d], lambda k: h1, [m_h1], sp_)
                m_mod.append(do(act, lambda e, acc=acc, d=d: e.activation(
                    mod[:, d], acc[:], ACT.Sigmoid, bias=b_n2[:, d:d + 1]), [mm], sa))
                wide_ring.hold(i, m_mod[-1])
            m_gated = []
            for mc in range(DC):
                i, acc, mm = matvec(wide_ring, 2 * DC, feature_cols(w_g, mc),
                                    lambda k: x[:, k] if k < DC else ctxT[:, k - DC], [*ready, m_ctx], sp_)
                m = do(act, lambda e, acc=acc, mc=mc: e.activation(
                    gate[:, mc], acc[:], ACT.Sigmoid, bias=mcol[:, 0, mc:mc + 1]), [mm], sa)
                wide_ring.hold(i, m)
                m_gated.append(do(dve, lambda e, mc=mc: e.tensor_tensor(gated[:, mc], x[:, mc], gate[:, mc],
                                                                        ALU.mult), [m], sd_))
            m_temporal = []
            for c in range(DC):
                for d, tr in enumerate((tr0, tr1)):
                    m = do(dve, lambda e, c=c, d=d, tr=tr: e.scalar_tensor_tensor(
                        out=tr[:, c], in0=mod[:, d], scalar=0.5, in1=gated[:, c], op0=ALU.add, op1=ALU.mult),
                        [m_mod[d], m_gated[c]], sd_)
                    m = do(dve, lambda e, c=c, d=d, tr=tr: e.tensor_tensor_scan(
                        tr[:, c], alpha[:, 1 + d:2 + d].broadcast_to([P, S]), tr[:, c], 0.0, ALU.mult, ALU.add),
                        [m], s_dve["scan"])
                    if d == 0:
                        m0 = do(dve, lambda e, c=c: e.tensor_scalar(tr0[:, c], tr0[:, c], bw[:, c:c + 1], None,
                                                                    ALU.mult), [m, m_bw], sd_)
                m_temporal.append(do(dve, lambda e, c=c: e.scalar_tensor_tensor(
                    out=tr0[:, c], in0=tr1[:, c], scalar=bw[:, DC + c:DC + c + 1], in1=tr0[:, c],
                    op0=ALU.mult, op1=ALU.add), [m, m0], sd_))
            m_in = []
            for mc in range(DC):
                i, acc, mm = matvec(wide_ring, DC, feature_cols(w_temp, mc), lambda k: tr0[:, k], m_temporal, sp_)
                m = do(act, lambda e, acc=acc, mc=mc: e.activation(
                    gate[:, mc], acc[:], ACT.Sigmoid, bias=mcol[:, 2, mc:mc + 1]), [mm, m_gated[mc]], sa)
                wide_ring.hold(i, m)
                m_in.append(do(dve, lambda e, mc=mc: e.tensor_tensor(soma[:, mc], soma[:, mc], gate[:, mc],
                                                                     ALU.mult), [m, m_soma[mc]], sd_))
            return m_in

        def normalise(b, m_in):
            sl = s_dve["ln"]
            ts = slice(b * NT, (b + 1) * NT)
            stat_ring = Ring(list(range(4)))
            marks = []
            for t in range(NT):
                i, bk, free = bank_ring.take()
                for c in range(DC):
                    mm = do(pe, lambda e, bk=bk, c=c, t=t: e.matmul(
                        bk[:, 0:D], soma[:, c, t * P:(t + 1) * P], w_out[:, c], start=(c == 0), stop=(c == DC - 1)),
                        [*m_in, *free], s_pe["tok"] if c == DC - 1 else None)
                si_, _, sfree = stat_ring.take()
                m3 = do(act, lambda e, bk=bk, t=t: e.activation(h_tok[:, b * NT + t], bk[:, 0:D], ACT.Copy),
                        [mm], s_act["copy"])
                m1 = do(dve, lambda e, t=t, si_=si_: e.bn_stats(stats[:, si_], h_tok[:, b * NT + t]),
                        [m3, *sfree], sl)
                m2 = do(dve, lambda e, si_=si_, t=t: e.bn_aggr(mean_var[:, b * NT + t], stats[:, si_]), [m1], sl)
                stat_ring.hold(si_, m2)
                bank_ring.hold(i, m3)
            mix_free.clear()
            mix_free.append(mm)
            m = do(dve, lambda e: e.tensor_scalar(rstd[:, ts], mean_var[:, ts, 1], LN_EPS, None, ALU.add), [m2], sl)
            m = do(act, lambda e: e.activation(rstd[:, ts], rstd[:, ts], ACT.Sqrt), [m, m2], s_act["stat"])
            m = do(dve, lambda e: e.reciprocal(rstd[:, ts], rstd[:, ts]), [m], sl)
            for t in range(b * NT, (b + 1) * NT):
                mn = do(dve, lambda e, t=t: e.tensor_scalar(h_tok[:, t], h_tok[:, t], mean_var[:, t, 0:1],
                                                            rstd[:, t:t + 1], ALU.subtract, ALU.mult), [m, m3], sl)
            ht = h_tok[:, ts]
            m = do(dve, lambda e: e.tensor_tensor(ht, ht, ln_rows[:, 0:1].broadcast_to([P, NT, D]), ALU.mult),
                   [mn], sl)
            m_h = do(dve, lambda e: e.tensor_tensor(ht, ht, ln_rows[:, 1:2].broadcast_to([P, NT, D]), ALU.add),
                     [m], sl)
            for g in range(NT // 4):
                for c in range(DC):
                    i, bk, free = bank_ring.take()
                    for k in range(4):
                        mm = do(pe, lambda e, bk=bk, c=c, k=k, t=b * NT + 4 * g + k: e.transpose(
                            bk[:, k * P:(k + 1) * P], h_tok[:, t, c * P:(c + 1) * P], F["ident"]),
                            [m_h, *free], s_pe["hT"] if k == 3 else None)
                    m_hT = do(act, lambda e, bk=bk, c=c, o=b * S + g * HALF: e.activation(
                        hT[:, c, o:o + HALF], bk[:], ACT.Copy), [mm], s_act["copy"])
                    bank_ring.hold(i, m_hT)
            scrap_ring = Ring([sil[:, 0, 0:D], sil[:, 1, 0:D]])
            for t in range(b * NT, (b + 1) * NT):
                k, sc, free = scrap_ring.take()
                m = do(act, lambda e, sc=sc, t=t: e.activation(sc, h_tok[:, t], ACT.Square,
                                                               accum_out=ssq[:, t:t + 1]), [m_h, *free], s_act["stat"])
                scrap_ring.hold(k, m)
            m = do(dve, lambda e: e.tensor_scalar(rms[:, ts], ssq[:, ts], 1.0 / D, RMS_EPS, ALU.mult, ALU.add), [m], sl)
            m = do(act, lambda e: e.activation(rms[:, ts], rms[:, ts], ACT.Sqrt), [m], s_act["stat"])
            m_rms = do(dve, lambda e: e.reciprocal(rms[:, ts], rms[:, ts]), [m], sl)
            return m_h, m_hT, m_rms

        def route(b, m_h, m_hT, m_rms, last_before):
            sr = s_dve["route"]
            ts = slice(b * NT, (b + 1) * NT)
            i, bk, free = bank_ring.take()
            for t in range(NT):
                for c in range(DC):
                    mm = do(pe, lambda e, t=t, c=c: e.matmul(
                        bk[:, t * E:(t + 1) * E], hT[:, c, b * S + t * P:b * S + (t + 1) * P], w_rt[:, c],
                        start=(c == 0), stop=(c == DC - 1)), [m_hT, *free],
                        s_pe["logit"] if (t, c) == (NT - 1, DC - 1) else None)
            lg = logit[:, ts]
            m = do(dve, lambda e: e.tensor_tensor(lg, bk[:, 0:NT * E].rearrange("p (t x) -> p t x", t=NT),
                                                  rms[:, ts].unsqueeze(2).broadcast_to([P, NT, E]), ALU.mult),
                   [mm, m_rms], sr)
            bank_ring.hold(i, m)
            m = do(dve, lambda e: e.tensor_reduce(lmax[:, ts], lg, AX.X, ALU.max), [m], sr)
            m = do(dve, lambda e: e.tensor_tensor(lg, lg, lmax[:, ts].unsqueeze(2).broadcast_to([P, NT, E]),
                                                  ALU.subtract), [m], sr)
            m = do(act, lambda e: e.activation(lg, lg, ACT.Exp), [m], s_act["route"])
            for t in range(b * NT, (b + 1) * NT):
                m1 = do(dve, lambda e, t=t: e.max(out=top8[:, t], in_=logit[:, t]), [m], sr)
            m_top = m1
            for t in range(b * NT, (b + 1) * NT):
                m1 = do(dve, lambda e, t=t: e.max_index(out=best[:, t], in_max=top8[:, t], in_values=logit[:, t]),
                        [m_top], sr)
            m = do(dve, lambda e: e.tensor_copy(best_f[:, ts], best[:, ts, 0:TOPK]), [m1], sr)
            m2 = do(dve, lambda e: e.tensor_reduce(gsum[:, ts], top8[:, ts, 0:TOPK], AX.X, ALU.add), [m_top], sr)
            m2 = do(dve, lambda e: e.reciprocal(gsum[:, ts], gsum[:, ts]), [m2], sr)
            for k in range(TOPK):
                m_gain = do(dve, lambda e, k=k: e.tensor_tensor(gain[:, k, ts], top8[:, ts, k], gsum[:, ts],
                                                                ALU.mult), [m2], sr)
            marks = []
            for k in range(TOPK):
                marks.append(do(dve, lambda e, k=k: e.tensor_tensor(
                    pick[:, k, ts], F["iota_e"].unsqueeze(1).broadcast_to([P, NT, E]),
                    best_f[:, ts, k:k + 1].broadcast_to([P, NT, E]), ALU.is_equal), [m], sr))
            m = do(dve, lambda e: e.tensor_tensor(mask[:, ts], pick[:, 0, ts], pick[:, 1, ts], ALU.add), marks, sr)
            for t in range(b * NT, (b + 1) * NT):
                last_before = do(dve, lambda e, t=t: e.tensor_tensor(before[:, t + 1], before[:, t], mask[:, t],
                                                                     ALU.add), [m, last_before], sr)
            i, bk, free = bank_ring.take()
            for t in range(NT):
                do(pe, lambda e, t=t: e.matmul(bk[:, t * E:(t + 1) * E], C["ones"], before[:, b * NT + t],
                                               start=True, stop=False), [last_before, *free])
                mm = do(pe, lambda e, t=t: e.matmul(bk[:, t * E:(t + 1) * E], C["before"], mask[:, b * NT + t],
                                                    start=False, stop=True), [], s_pe["pos"])
            pos = bk[:, 0:NT * E].rearrange("p (t x) -> p t x", t=NT)
            m = do(dve, lambda e: e.tensor_scalar(far[:, ts], pos, float(CAP), FAR, ALU.is_ge, ALU.mult), [mm], sr)
            m1 = do(dve, lambda e: e.tensor_tensor(slot_map[:, ts], pos,
                                                   F["slot_e"].unsqueeze(1).broadcast_to([P, NT, E]), ALU.add), [mm], sr)
            bank_ring.hold(i, m1)
            m = do(dve, lambda e: e.tensor_tensor(slot_map[:, ts], slot_map[:, ts], far[:, ts], ALU.add), [m, m1], sr)
            for k in range(TOPK):
                m1 = do(dve, lambda e, k=k: e.tensor_tensor(pick[:, k, ts], pick[:, k, ts], slot_map[:, ts], ALU.mult),
                        [m], sr)
                m1 = do(dve, lambda e, k=k: e.tensor_reduce(slot[:, k, ts], pick[:, k, ts], AX.X, ALU.add), [m1], sr)
                m_w = do(dve, lambda e, k=k: e.tensor_copy(slot_w[:, k, ts], slot[:, k, ts]), [m1], sr)
                m_r = do(dve, lambda e, k=k: e.tensor_scalar(slot_r[:, k, ts], slot[:, k, ts], float(SLOTS), None,
                                                             ALU.min), [m1], sr)
            for t in range(b * NT, (b + 1) * NT):
                for k in range(TOPK):
                    m_sent = pool.add(lambda e, t=t, k=k: e.indirect_dma_start(
                        out=slots_in, out_offset=bass.IndirectOffsetOnAxis(ap=slot_w[:, k, t:t + 1], axis=0),
                        in_=h_tok[:, t], in_offset=None, bounds_check=SLOTS - 1, oob_is_err=False),
                        [m_w, m_h, m_zero], s_sent, 16)
            return last_before, m_sent, m_r, m_gain

        s_sent = sem("tokens_sent")
        last_before = m_before
        for b in range(B):
            m_in = mix(b)
            m_h, m_hT, m_rms = normalise(b, m_in)
            last_before, m_sent, m_r, m_gain = route(b, m_h, m_hT, m_rms, last_before)

        def w_slot(k):
            o = 3 * 2 * S * k
            g, u, dn = (big[:, o + j * 2 * S:o + (j + 1) * 2 * S] for j in range(3))
            return (g.rearrange("p (c m) -> p c m", c=DC), u.rearrange("p (c m) -> p c m", c=DC),
                    dn.rearrange("p (i n) -> p i n", i=I_R // P))

        expert_ring = Ring([w_slot(0), w_slot(1)])
        s_we = [sem("load_expert0"), sem("load_expert1")]
        mixed = [(s_pe["tok"], s_pe["tok"].value), (s_pe["mix"], s_pe["mix"].value), (s_dve["mix"], s_dve["mix"].value)]
        expert_w = {}

        def load_expert(x):
            k, (g, u, dn), free = expert_ring.take()
            for dst, src in ((g, chunks(A["rg"][x])), (u, chunks(A["ru"][x])), (dn, chunks(A["rd"][x]))):
                m = dma(sp, dst, src, [*mixed, *free], s_we[k])
            expert_w[x] = (k, g, u, dn, m)

        gu_ring = Ring(wide[:2])
        acc_ring = Ring(wide[2:])
        sil_ring = Ring([sil[:, 0], sil[:, 1]])
        for k in range(2):
            sil_ring.hold(k, (s_act["stat"], s_act["stat"].value))
        act_ring = Ring([act_s[:, k] for k in range(3)])
        wides = [u for us in wide_ring.users for u in us]
        for i in range(2):
            gu_ring.hold(i, *wides)
        acc_ring.hold(0, *wides)

        def gate_up(n, wg_, wu_, col, src, ready, dst, dst_free):
            i, gu, free = gu_ring.take()
            for o, wt in ((0, wg_), (HALF, wu_)):
                for c in range(DC):
                    mm = do(pe, lambda e, o=o, wt=wt, c=c: e.matmul(
                        gu[:, o:o + n], wt[:, c, col:col + P], src(c), start=(c == 0), stop=(c == DC - 1)),
                        [*ready, *free], s_pe["gu"] if c == DC - 1 and o else None)
            k, sl_, sfree = sil_ring.take()
            m = do(act, lambda e: e.activation(sl_[:, 0:n], gu[:, 0:n], ACT.Silu), [mm, *sfree], s_act["silu"])
            m = do(dve, lambda e: e.tensor_tensor(dst, sl_[:, 0:n], gu[:, HALF:HALF + n], ALU.mult),
                   [m, *dst_free], s_dve["act"])
            gu_ring.hold(i, m)
            sil_ring.hold(k, m)
            return m

        def shared(tc):
            n_i, tiles = I_S // P, HALF // P
            ai, acc, afree = acc_ring.take()
            def down(i, k, a, m):
                for t in range(tiles):
                    mm = do(pe, lambda e, t=t: e.matmul(
                        acc[:, t * D:(t + 1) * D], a[:, t * P:(t + 1) * P], wsd[:, i],
                        start=(i == 0 and t % 2 == 0), stop=False, skip_group_check=True),
                        [m, m_sd, *afree], s_pe["down"])
                act_ring.hold(k, mm)
            late = None
            for i in range(n_i):
                k, a, free = act_ring.take()
                m = gate_up(HALF, wsg, wsu, i * P, lambda c: hT[:, c, tc * HALF:(tc + 1) * HALF],
                            [m_hT, m_sg, m_su], a, free)
                if late:
                    down(*late)
                late = (i, k, a, m)
            down(*late)
            for t in range(tiles):
                for c in range(DC):
                    mm = do(pe, lambda e, t=t, c=c: e.matmul(
                        acc[:, t * D + c * P:t * D + (c + 1) * P],
                        xT[:, c, tc * HALF + t * P:tc * HALF + (t + 1) * P], F["ident"],
                        start=False, stop=True, skip_group_check=True), [], s_pe["down"])
            yt = y[:, tc * tiles:(tc + 1) * tiles]
            m = do(act, lambda e: e.activation(yt.rearrange("p t n -> p (t n)"), acc[:], ACT.Copy),
                   [mm, m_sent], s_act["copy"])
            acc_ring.hold(ai, m)
            return m

        load_expert(0)
        load_expert(1)
        m_shared = {0: shared(0), 1: shared(1)}

        xg_ring, xgT_ring, eo_ring = (Ring([0, 1]) for _ in range(3))
        s_xg = [sem("load_tokens0"), sem("load_tokens1")]
        s_eo = [sem("store_expert0"), sem("store_expert1")]
        act_e_ring = Ring([act_e])
        act_e_ring.hold(0, *mixed)
        TILES = [(0, P), (P, P), (2 * P, CAP - 2 * P)]

        def fetch(x):
            k, _, free = xg_ring.take()
            rows = slots_in[x * CAP:(x + 1) * CAP, :]
            dma(sp, xg[:, k, 0:2], rows[0:2 * P, :].rearrange("(t p) n -> p t n", p=P), [m_sent, *free], s_xg[k])
            m = dma(sp, xg[0:CAP - 2 * P, k, 2], rows[2 * P:CAP, :], [], s_xg[k])
            kt, _, tfree = xgT_ring.take()
            for c in range(DC):
                i, bk, bfree = bank_ring.take()
                for t, (o, n) in enumerate(TILES):
                    mm = do(pe, lambda e, c=c, t=t, o=o, n=n, bk=bk: e.transpose(
                        bk[:, o:o + n], xg[0:n, k, t, c * P:(c + 1) * P], F["ident"][0:n, 0:n]), [m, *bfree],
                        s_pe["xT"] if t == 2 else None)
                m2 = do(act, lambda e, c=c, bk=bk: e.activation(xgT[:, kt, c], bk[:, 0:CAP], ACT.Copy),
                        [mm, *tfree], s_act["copy"])
                bank_ring.hold(i, m2)
            xg_ring.hold(k, mm)
            return kt, m2

        fetched = {0: fetch(0)}
        stored_e = []
        for x in range(E):
            k, wg_, wu_, wd_, m_w = expert_w[x]
            kt, m_x_ = fetched[x]
            _, _, ae_free = act_e_ring.take()
            ms = []
            for i in range(I_R // P):
                ms.append(gate_up(CAP, wg_, wu_, i * P, lambda c, kt=kt: xgT[:, kt, c], [m_w, m_x_],
                                  act_e[:, i], ae_free))
                if i == 3 and x + 1 < E:
                    fetched[x + 1] = fetch(x + 1)
            xgT_ring.hold(kt, (s_pe["gu"], s_pe["gu"].value))
            ai, acc, afree = acc_ring.take()
            for t, (o, n) in enumerate(TILES):
                for i in range(I_R // P):
                    mm = do(pe, lambda e, t=t, o=o, n=n, i=i, wd_=wd_, acc=acc: e.matmul(
                        acc[0:n, t * D:(t + 1) * D], act_e[:, i, o:o + n], wd_[:, i],
                        start=(i == 0), stop=(i == I_R // P - 1)), [ms[i], *afree], s_pe["down"])
            act_e_ring.hold(0, mm)
            expert_ring.hold(k, mm)
            if x + 2 < E:
                load_expert(x + 2)
            ko, _, ofree = eo_ring.take()
            do(dve, lambda e, ko=ko, acc=acc: e.tensor_copy(
                e_out[:, ko, 0:2], acc[:, 0:2 * D].rearrange("p (t n) -> p t n", t=2)), [mm, *ofree], s_dve["copy"])
            m = do(dve, lambda e, ko=ko, acc=acc: e.tensor_copy(e_out[0:CAP - 2 * P, ko, 2],
                                                                acc[0:CAP - 2 * P, 2 * D:3 * D]), [], s_dve["copy"])
            acc_ring.hold(ai, m)
            rows = slots_out[x * CAP:(x + 1) * CAP, :]
            dma(sp, rows[0:2 * P, :].rearrange("(t p) n -> p t n", p=P), e_out[:, ko, 0:2], [m], s_eo[ko])
            m = dma(sp, rows[2 * P:CAP, :], e_out[0:CAP - 2 * P, ko, 2], [], s_eo[ko])
            eo_ring.hold(ko, m)
            stored_e = (stored_e + [m])[-2:]

        for tc in range(2, T // HALF):
            m_shared[tc] = shared(tc)

        got_ring = Ring(list(range(4)))
        for k in range(4):
            got_ring.hold(k, *mixed)
        s_got = [sem(f"gather{k}") for k in range(4)]
        s_done = sem("store_out")
        for t in range(B * NT):
            m = m_shared[t * P // HALF]
            for k in range(TOPK):
                g, _, free = got_ring.take()
                mg = pool.add(lambda e, g=g, k=k, t=t: e.indirect_dma_start(
                    out=got[g], out_offset=None, in_=slots_out,
                    in_offset=bass.IndirectOffsetOnAxis(ap=slot_r[:, k, t:t + 1], axis=0)),
                    [*stored_e, m_r, m_zero, *free], s_got[g], 16)
                m = do(dve, lambda e, g=g, k=k, t=t: e.scalar_tensor_tensor(
                    out=y[:, t], in0=got[g], scalar=gain[:, k, t:t + 1], in1=y[:, t],
                    op0=ALU.mult, op1=ALU.add), [mg, m, m_gain], s_dve["comb"])
                got_ring.hold(g, m)
            md = dma(sp, out[t * P:(t + 1) * P, :], y[:, t], [m], s_done)
        ph2.close()
        sp.items.append(([md], None, None, 0))

        block = ctx.enter_context(nc.Block())

        @block.sync
        def _(e):
            sp.emit(e)

        @block.gpsimd
        def _(e):
            pool.emit(e)

        @block.scalar
        def _(e):
            act.emit(e)

        @block.vector
        def _(e):
            dve.emit(e)

        @block.tensor
        def _(e):
            pe.emit(e)




def constants():
    import numpy as np

    f = np.zeros((P, CF_W), np.float32)
    f[:, :P] = np.eye(P)
    for par in range(2):
        for g in range(QUAD):
            for d in range(DH):
                col = par * P + par * (P // 2) + g * DH + d
                f[g * HB + d, CF["sel_num"][0] + col] = 1
                f[g * HB + DH, CF["sel_den"][0] + col] = 1
    a = CF["iota_e"][0]
    f[:, a:a + E] = np.arange(E)
    f[:, a + E:a + 2 * E] = np.arange(E) * CAP
    r, c = np.arange(P)[:, None], np.arange(P)[None, :]
    b = np.concatenate([np.eye(P), np.where(c > r, NEG, 0), np.where(r > c, NEG, 0), r < c, np.ones((P, P))], 1)
    return {"const_f32": f, "const_bf16": b.astype(mybir.dt.np(BF16)),
            "iota": np.broadcast_to(np.arange(S, dtype=np.float16), (P, S)).copy()}


def layout(inputs):
    import numpy as np

    i = {k: np.asarray(v) for k, v in inputs.items()}
    a = constants()
    a["xT"] = i["x"].reshape(T, D).T
    a["idx"] = i["itok_Sx32_0_1023"]
    a["idx_mask"] = i["mask_Sx32_bk1"].view(np.int32)
    a["prior"] = i["mask_SxS_bk0"].view(np.int32)
    a["priorT"] = i["mask_SxS_bk0"].T.copy().view(np.int32)
    a["u_prev"] = i["condB_uprev"]
    a["w_prior"] = np.concatenate([i[f"L0_cond_W{n}"].T for n in "qkv"], 1)
    a["w_causal"] = i["L0_attn_W_kqv"].T
    a["w_o"] = i["L0_cond_Wo"].T
    a["w_proj"] = i["L0_attn_W_proj"].T
    bk = i["L0_attn_b_kqv"]
    a["bias_cols"] = np.stack([i["L0_cond_bq"], i["L0_cond_bk"], bk[D:2 * D], bk[:D], i["L0_cond_bo"],
                               i["L0_attn_b_proj"]])
    a["bias_v"] = np.stack([i["L0_cond_bv"], bk[2 * D:]])
    c2 = "L0_cond2_"
    a["taus"] = np.concatenate([i[c2 + "tau_ctx"].reshape(1), i["condB_tauraws"]])
    a["w_g"] = i[c2 + "Wg"].T
    a["w_n1"] = i[c2 + "Wn1"].T
    a["w_n2"] = np.repeat(i["cond_256"].T[:, :, None], P, 2)
    a["b_n2"] = i["condB_bn2"]
    a["b_n1"] = i[c2 + "bn1"].reshape(HN, 1)
    a["blend"] = i["cond_1024"]
    a["w_soma"] = i[c2 + "Wsoma"].T
    a["w_temp"] = i[c2 + "Wtemp"].T
    a["w_out"] = i[c2 + "Wout"].T
    a["mix_cols"] = np.stack([i[c2 + "bg"], i[c2 + "bsoma"], i[c2 + "btemp"]])
    a["ln_rows"] = np.stack([i[c2 + "gamma"], i[c2 + "beta"]])
    a["w_router"] = i["L0_ffn_router_w"].T
    for n in ("rg", "ru", "rd", "sg", "su", "sd"):
        a[n] = i["L0_ffn_" + n]
    for n in ("bias_cols", "mix_cols", "blend"):
        a[n] = a[n].reshape(-1, DC, P).transpose(2, 0, 1)
    return {k: np.ascontiguousarray(v) for k, v in a.items()}


def kernel(**inputs):
    import concourse.bacc as bacc
    import numpy as np
    from concourse.bass_utils import run_bass_kernel_spmd

    arrays = layout(inputs)
    nc = bacc.Bacc("TRN2", target_bir_lowering=False, num_devices=1)
    A = {k: nc.dram_tensor(k, v.shape, mybir.dt.from_np(v.dtype), kind="ExternalInput").ap()
         for k, v in arrays.items()}
    out = nc.dram_tensor("out", (T, D), F32, kind="ExternalOutput").ap()
    build(nc, A, out)
    r = run_bass_kernel_spmd(nc, [arrays], core_ids=[0])
    return np.asarray(r.results[0]["out"]).reshape(B, S, D)
```

```python
from contextlib import ExitStack

import concourse.bass as bass
from concourse import mybir

ALU = mybir.AluOpType
ACT = mybir.ActivationFunctionType
AX = mybir.AxisListType
F32 = mybir.dt.float32
BF16 = mybir.dt.bfloat16
FP16 = mybir.dt.float16
U8 = mybir.dt.uint8
I32 = mybir.dt.int32
U32 = mybir.dt.uint32

P = 128
B, S, D, H = 2, 1024, 256, 16
DH = D // H
T = B * S
DC = D // P
NT = S // P
HALF = 512
NH = S // HALF
QUAD = 4
NQ = H // QUAD
HB = P // QUAD
K_SPARSE = 32
LAMBDA_MAX, ALPHA, SPARSE_THRESHOLD = 10.0, 5.0, 1.0
SCALE = 1.0 / DH ** 0.5
SPANS = P // K_SPARSE
SPAN = S // SPANS
N_PROB = 7
PARTS = 3
Q_PART = [0, 1, 2, 0, 1, 0]
K_PART = [0, 0, 0, 1, 1, 2]
ROWS = DH * len(Q_PART)
ROWS_M = ROWS + PARTS
NEG = -1e30
HUGE = 1e30
HN = D // 4
ND = 2
E, TOPK = 8, 2
I_R, I_S = 4 * D, 8 * D
CAP = max(int(1.25 * T / E), 1)
SLOTS = E * CAP
VALUES_LAG = 2
FAR = 1e5
LN_EPS = 1e-5
RMS_EPS = 1.1920928955078125e-07

CF = dict(ident=(0, P), sel_num=(P, 2 * P), sel_den=(3 * P, 2 * P), iota_e=(5 * P, E), slot_e=(5 * P + E, E))
CF_W = 5 * P + 2 * E
CB = dict(ident=(0, P), neg_qk=(P, P), neg_kq=(2 * P, P), before=(3 * P, P), ones=(4 * P, P), iota=(5 * P, P))
CB_W = 6 * P


class Sem:

    def __init__(self, handle):
        self.handle, self.value = handle, 0


class Queue:

    def __init__(self):
        self.items, self.seen = [], {}

    def add(self, fn, after, sem, step):
        waits = []
        for m in after:
            if m is not None and self.seen.get(m[0], 0) < m[1]:
                self.seen[m[0]] = m[1]
                waits = [w for w in waits if w[0] is not m[0]] + [m]
        mark = None
        if sem is not None:
            sem.value += step
            mark = (sem, sem.value)
        self.items.append((waits, fn, sem, step))
        return mark

    def emit(self, engine):
        for waits, fn, sem, step in self.items:
            for s, v in waits:
                engine.wait_ge(s.handle, v)
            ins = fn and fn(engine)
            if sem is not None:
                ins.then_inc(sem.handle, step)


class Ring:

    def __init__(self, bufs):
        self.bufs, self.users, self.n = bufs, [[] for _ in bufs], 0

    def take(self):
        i = self.n % len(self.bufs)
        self.n += 1
        users, self.users[i] = self.users[i], []
        return i, self.bufs[i], users

    def hold(self, i, *marks):
        self.users[i] += marks


def build(nc, A, out):
    ctx = ExitStack()
    with ctx:
        all_sems = []

        def sem(name):
            all_sems.append(Sem(ctx.enter_context(nc.semaphore(name))))
            return all_sems[-1]

        def sb(name, shape, dt=F32, scope=None):
            return (scope or ctx).enter_context(nc.sbuf_tensor("sb_" + name, shape, dt))

        def dram(name, shape, dt):
            return nc.dram_tensor(name, shape, dt, kind="Internal").ap()

        pe, dve, act, pool, sp = (Queue() for _ in range(5))

        def do(queue, fn, after=(), sem=None):
            return queue.add(fn, after, sem, 1)

        def dma(queue, dst, src, after=(), sem=None):
            return queue.add(lambda e: e.dma_start(dst, src), after, sem, 16)

        s_pe = {k: sem(f"pe_{k}") for k in (
            "count", "countT", "proj", "vproj", "max", "maxT", "score", "pv", "sel", "out",
            "mix", "tok", "hT", "logit", "pos", "xT", "gu", "down")}
        s_dve = {k: sem(f"dve_{k}") for k in (
            "const", "index", "onehot", "flag", "bias", "weight", "split", "v", "rowmax", "maxpart",
            "weigh", "norm", "resid", "mix", "scan", "stat", "ln", "route", "act", "comb", "copy")}
        s_act = {k: sem(f"act_{k}") for k in (
            "flag", "count", "split", "exp", "o", "mrow", "y", "gate", "stat", "route", "copy", "silu")}
        s_pool = {k: sem(f"pool_{k}") for k in ("const", "zero")}

        parts = dram("parts", [2, B, 2, PARTS, D, S], BF16)
        count_d = dram("count_qk", [NT, P, S], BF16)
        y_d = dram("y_prior", [B, DC, P, S], F32)
        countT_d = dram("count_kq", [NT, P, S], BF16)
        slots_in = dram("slots_in", [SLOTS, D], F32)
        slots_out = dram("slots_out", [SLOTS + 1, D], F32)

        wide = [ctx.enter_context(nc.psum_tensor(f"wide{i}", [P, 2 * HALF], F32)) for i in range(3)]
        bank = [ctx.enter_context(nc.psum_tensor(f"bank{i}", [P, HALF], F32)) for i in range(2)]
        score_ring = Ring(wide[:2])
        pv_ring = Ring(wide[2:])
        bank_ring = Ring(bank)

        cf = sb("const_f32", [P, CF_W])
        cb = sb("const_bf16", [P, CB_W], BF16)
        F = {k: cf[:, a:a + n] for k, (a, n) in CF.items()}
        C = {k: cb[:, a:a + n] for k, (a, n) in CB.items()}
        xT = sb("xT", [P, DC, T])

        s_load = {}

        def load(name, dst, src, queue=None, after=()):
            if name not in s_load:
                s_load[name] = sem(f"load_{name}")
            return dma(queue or sp, dst, src, after, s_load[name])

        def chunks(ap):
            return ap.rearrange("(c p) m -> p c m", p=P)

        m_cb = load("cb", cb[:], A["const_bf16"])
        m_cf = load("cf", cf[:], A["const_f32"])

        ph1 = ExitStack()

        def s1(name, shape, dt=F32):
            return sb(name, shape, dt, ph1)

        w1 = s1("w_prior", [P, DC, 3 * D])
        w2 = s1("w_causal", [P, DC, 3 * D])
        wo = s1("w_o", [P, DC, D])
        wp = s1("w_proj", [P, DC, D])
        bcol = s1("bias_cols", [P, 6, DC])
        bv = s1("bias_v", [P, 2, D])
        spans = s1("span_iota", [P, SPANS * NT], BF16)
        flags = s1("flags", [P, 10, B])
        stack_q = s1("stack_q", [P, 3, QUAD, S], BF16)
        stack_k = s1("stack_k", [P, 3, QUAD, S], BF16)
        weight = s1("weight", [P, NT, S])
        bias = s1("bias", [P, NT, S], BF16)
        prob = s1("prob", [P, 7, S])
        v_aug = s1("v_aug", [P, NT, H, HB])
        o_raw = s1("o_raw", [P, 2, S])
        o_norm = s1("o_norm", [P, DC, S])
        tab = s1("tables", [P, 2, S], BF16)
        tab8 = s1("tables8", [P, 2, S], U8)
        junk = s1("junk", [P, 2, HALF], BF16)
        junk_ring = Ring([junk[:, i] for i in range(2)])
        lo16 = junk[:, 0, 0:SPAN]
        hi16 = junk[:, 1, 0:SPAN]
        rowmax = s1("rowmax", [P, 2, QUAD, NT, 2])
        mneg = s1("mneg", [P, 4, QUAD, NT])
        mpart = s1("mpart", [P, 2, NT, QUAD, PARTS], BF16)
        mrow = s1("mrow", [PARTS * QUAD, 1, S], BF16)

        idx_i = o_raw[:, 0, 0:SPAN].bitcast(I32)
        key_lo, key_hi = o_raw[:, 0, SPAN:2 * SPAN], o_raw[:, 0, 2 * SPAN:3 * SPAN]
        key, wrap = o_raw[:, 1, 0:SPAN], o_raw[:, 1, SPAN:2 * SPAN]
        listed = o_raw[:, 1, 2 * SPAN:3 * SPAN]
        msk_u = o_raw[:, 1, 3 * SPAN:3 * SPAN + SPAN // 4].bitcast(U8)
        m_idx = load("idx", idx_i, A["idx"], act)
        m_idx = load("idx", spans[:], A["span_iota"], act)
        m_idx = load("idx", msk_u, A["idx_mask"].bitcast(U8), act)
        m_x = [load(f"x{b}", xT[:, :, b * S:(b + 1) * S], chunks(A["xT"])[:, :, b * S:(b + 1) * S])
               for b in range(B)]
        m_w1 = load("w1", w1[:], chunks(A["w_prior"]))
        load("small", bcol[:], A["bias_cols"], act)
        load("small", bv[:], A["bias_v"].partition_broadcast(P), act)
        m_small = load("small", flags[:, 0, :], A["u_prev"].partition_broadcast(P), act)
        m_w2 = load("w2", w2[:], chunks(A["w_causal"]))
        load("wo", wo[:], chunks(A["w_o"]))
        m_wo = load("wo", wp[:], chunks(A["w_proj"]))

        m_ones = do(pool, lambda e: e.memset(v_aug[:, :, :, DH:HB], 1.0), (), s_pool["const"])
        for r in range(3):
            m_krows = do(pool, lambda e, r=r: e.memset(stack_k[ROWS:ROWS_M, r], 1.0),
                         [m_ones if r == 0 else m_krows], s_pool["const"])
        m_rowmax0 = do(pool, lambda e: e.memset(rowmax[:], -3e38), [m_krows], s_pool["const"])

        zeros = o_norm[:].rearrange("p c t -> p (c t)")
        m = do(pool, lambda e: e.memset(o_norm[:], 0.0), [m_rowmax0], s_pool["zero"])
        s_zero = sem("zero_slots")
        for r in range(0, SLOTS, P * S * DC // D):
            n = min(P * S * DC // D, SLOTS - r)
            dma(act, slots_in[r:r + n, :].rearrange("(p k) n -> p (k n)", p=P), zeros[:, 0:n * D // P], [m], s_zero)
        m_zero = dma(act, slots_out[SLOTS:SLOTS + 1, :], zeros[0:1, 0:D], [m], s_zero)

        fl = [flags[:, i, :] for i in range(10)]
        m = do(act, lambda e: e.activation(fl[1], fl[0], ACT.Exp, scale=-ALPHA), [m_small], s_act["flag"])
        sf = s_dve["flag"]
        m = do(dve, lambda e: e.tensor_scalar(fl[2], fl[1], LAMBDA_MAX, None, ALU.mult), [m], sf)
        m = do(dve, lambda e: e.tensor_scalar(fl[3], fl[2], SPARSE_THRESHOLD, None, ALU.is_ge), [m], sf)
        m = do(dve, lambda e: e.tensor_scalar(fl[4], fl[3], -1.0, 1.0, ALU.mult, ALU.add), [m], sf)
        m = do(dve, lambda e: e.tensor_scalar(fl[5], fl[3], NEG, None, ALU.mult), [m], sf)
        m = do(dve, lambda e: e.tensor_scalar(fl[2], fl[2], SPARSE_THRESHOLD, None, ALU.min), [m], sf)
        m = do(dve, lambda e: e.tensor_tensor(fl[7], fl[2], fl[4], ALU.mult), [m], sf)
        m = do(dve, lambda e: e.tensor_scalar(fl[6], fl[7], -1.0, None, ALU.mult), [m], sf)
        m = do(act, lambda e: e.activation(fl[1], fl[2], ACT.Exp, scale=-1.0), [m], s_act["flag"])
        m = do(dve, lambda e: e.tensor_tensor(fl[8], fl[1], fl[4], ALU.mult), [m], sf)
        m_flag = do(dve, lambda e: e.tensor_tensor(fl[9], fl[4], fl[8], ALU.subtract), [m], sf)

        si = s_dve["index"]
        m = do(dve, lambda e: e.tensor_copy(key, idx_i), [m_idx], si)
        m = do(dve, lambda e: e.tensor_scalar(wrap, key, 0.0, float(S), ALU.is_lt, ALU.mult), [m], si)
        m = do(dve, lambda e: e.tensor_tensor(key, key, wrap, ALU.add), [m], si)
        m = do(dve, lambda e: e.tensor_scalar(key, key, 0.0, float(S - 1), ALU.max, ALU.min), [m], si)
        m = do(dve, lambda e: e.tensor_scalar(key_hi, key, float(P), None, ALU.is_ge), [m], si)
        for n in range(2, NT):
            m = do(dve, lambda e, n=n: e.scalar_tensor_tensor(
                out=key_hi, in0=key, scalar=float(n * P), in1=key_hi, op0=ALU.is_ge, op1=ALU.add), [m], si)
        m = do(dve, lambda e: e.scalar_tensor_tensor(out=key_lo, in0=key_hi, scalar=-float(P), in1=key,
                                                     op0=ALU.mult, op1=ALU.add), [m], si)
        m = do(dve, lambda e: e.tensor_copy(listed, msk_u), [m], si)
        m = do(dve, lambda e: e.tensor_scalar(listed, listed, -float(NT), float(NT), ALU.mult, ALU.add), [m], si)
        m = do(dve, lambda e: e.tensor_tensor(key_hi, key_hi, listed, ALU.add), [m], si)
        m_lo = do(dve, lambda e: e.tensor_copy(lo16, key_lo), [m], si)
        m_hi = do(dve, lambda e: e.tensor_copy(hi16, key_hi), [m_lo], si)

        prob_ring = Ring([prob[:, i, :] for i in range(N_PROB)])
        counts = prob[:, 0:4, :].rearrange("p a b -> p (a b)").bitcast(BF16).rearrange("p (k q) -> p k q", k=NT)
        hot_hi = bias[:].rearrange("p a b -> p (a b)").rearrange("p (t c) -> p t c", c=SPANS * NT)
        GROUP = 32
        hot_ring = Ring([weight[:, 2 * i:2 * i + 2].rearrange("p a b -> p (a b)").bitcast(BF16)
                         .rearrange("p (t r) -> p t r", r=P) for i in range(NT // 2)])
        for g in range(SPAN // GROUP):
            ts = slice(g * GROUP, (g + 1) * GROUP)
            mh = do(dve, lambda e, ts=ts: e.tensor_tensor(
                hot_hi[:, ts], spans[:].unsqueeze(1).broadcast_to([P, GROUP, SPANS * NT]),
                hi16[:, ts].unsqueeze(2).broadcast_to([P, GROUP, SPANS * NT]), ALU.is_equal), [m_hi], s_dve["onehot"])
            k, hot, hfree = hot_ring.take()
            m = do(dve, lambda e, hot=hot, ts=ts: e.tensor_tensor(
                hot, C["iota"].unsqueeze(1).broadcast_to([P, GROUP, P]),
                lo16[:, ts].unsqueeze(2).broadcast_to([P, GROUP, P]), ALU.is_equal), [m_cb, m_lo, *hfree],
                s_dve["onehot"])
            i, acc, free = score_ring.take()
            for t in range(GROUP):
                mm = do(pe, lambda e, hot=hot, acc=acc, t=t, g=g: e.matmul(
                    acc[:, t * SPANS * NT:(t + 1) * SPANS * NT], hot[:, t], hot_hi[:, g * GROUP + t],
                    start=True, stop=True), [m, mh, *free], s_pe["count"] if t == GROUP - 1 else None)
            hot_ring.hold(k, mm)
            m_count = do(act, lambda e, acc=acc, g=g: e.activation(
                counts.rearrange("p k (s t) -> p s k t", s=SPANS)[:, :, :, g * GROUP:(g + 1) * GROUP],
                acc[:].rearrange("p (t s k) -> p s k t", s=SPANS, k=NT), ACT.Copy), [mm], s_act["count"])
            score_ring.hold(i, m_count)
        m_counted = mm
        s_cnt = [sem("count_store0"), sem("count_store1")]
        m_tables = [dma(sp, countT_d.rearrange("k p q -> p k q"), counts, [m_count], s_cnt[0])]

        s_store = [sem(f"parts_store{k}") for k in range(2)]
        idle = [stack_q[:, 2].rearrange("p h t -> p (h t)"),
                prob[:, 4:6].rearrange("p a t -> p (a t)").bitcast(BF16)]
        start_sets = [(z[:, 0:2 * HALF].bitcast(F32), *(z[:, (2 + j) * HALF:(3 + j) * HALF] for j in range(PARTS)))
                      for z in idle]
        tabs = tab[:].rearrange("p a t -> p (a t)")
        tabs8 = tab8[:].rearrange("p a t -> p (a t)").bitcast(BF16)
        late_sets = [(w1[:, 0, 0:HALF], *(tabs[:, j * HALF:(j + 1) * HALF] for j in range(PARTS))),
                     (w1[:, 1, 0:HALF], tabs[:, 3 * HALF:4 * HALF], tabs8[:, 0:HALF], tabs8[:, HALF:2 * HALF])]
        split_ring = Ring(start_sets)
        late_ring = Ring(late_sets)

        def project_qk(att, b, src, ready, w, q_col, k_col, ring):
            steps, stored = [], {}

            def chain(qk, col, scale, mc, h):
                st = {}

                def product():
                    cols = slice(h * HALF, (h + 1) * HALF)
                    i, acc, free = bank_ring.take()
                    for c in range(DC):
                        mm = do(pe, lambda e, c=c, o=col * D + mc * P: e.matmul(
                            acc[:], w[:, c, o:o + P], src[:, c, cols], start=(c == 0), stop=(c == DC - 1)),
                            [*ready(), *free], s_pe["proj"] if c == DC - 1 else None)
                    st["k"], (val, hi, mid, lo), sfree = ring.take()
                    m0 = do(dve, lambda e: e.tensor_scalar(val, acc[:], bcol[:, 2 * att + qk, mc:mc + 1], scale,
                                                           ALU.add, ALU.mult), [mm, m_small, *sfree], s_dve["split"])
                    bank_ring.hold(i, m0)
                    st["hi"] = do(act, lambda e: e.activation(hi, val, ACT.Copy), [m0], s_act["split"])
                    st["bufs"] = (val, hi, mid, lo)

                def second():
                    val, hi, mid, lo = st["bufs"]
                    m = do(dve, lambda e: e.tensor_tensor(val, val, hi, ALU.subtract), [st["hi"]], s_dve["split"])
                    st["mid"] = do(act, lambda e: e.activation(mid, val, ACT.Copy), [m], s_act["split"])

                def third():
                    val, hi, mid, lo = st["bufs"]
                    k = st["k"]
                    m = do(dve, lambda e: e.tensor_tensor(lo, val, mid, ALU.subtract), [st["mid"]], s_dve["split"])
                    for part, (t, mk) in enumerate(((hi, st["hi"]), (mid, st["mid"]), (lo, m))):
                        ms = dma(sp, parts[att, b, qk, part, mc * P:(mc + 1) * P, h * HALF:(h + 1) * HALF], t, [mk],
                                 s_store[k])
                    ring.hold(k, ms)
                    stored[k] = ms

                return [product, second, third]

            chains = [chain(qk, col, scale, mc, h) for qk, col, scale in ((0, q_col, SCALE), (1, k_col, 1.0))
                      for mc in range(DC) for h in range(NH)]
            for one, other in zip(chains[0::2], chains[1::2]):
                steps += [f for pair in zip(one, other) for f in pair]
            return steps, stored

        v_ring = Ring([v_aug])

        def project_v(att, src, ready, w, col):
            _, _, vfree = v_ring.take()
            marks = {}

            def tile(kt):
                i, bk, free = bank_ring.take()
                for c in range(DC):
                    mm = do(pe, lambda e, c=c: e.matmul(
                        bk[:, 0:D], src(c)[:, kt * P:(kt + 1) * P], w[:, c, col * D:(col + 1) * D],
                        start=(c == 0), stop=(c == DC - 1)), [*ready, *free],
                        s_pe["vproj"] if c == DC - 1 else None)
                m = do(dve, lambda e: e.tensor_tensor(
                    v_aug[:, kt, :, 0:DH], bk[:, 0:D].rearrange("p (h d) -> p h d", h=H),
                    bv[:, att, :].rearrange("p (h d) -> p h d", h=H), ALU.add),
                    [mm, m_small, m_ones, *vfree], s_dve["v"])
                bank_ring.hold(i, m)
                marks[kt], marks["read"] = m, mm

            return [lambda kt=kt: tile(kt) for kt in range(NT)], marks

        s_tab = [sem(f"load_tables{i}") for i in range(2)]
        tab_ring = Ring([(tab[:, i, :], tab8[:, i, :]) for i in range(2)])
        count_ring = Ring([prob[:, 6, i * HALF:(i + 1) * HALF].bitcast(BF16) for i in range(2)])

        def key_bias(b, qt, free_bias, mark):
            i, (t, t8), free = tab_ring.take()
            m_t8 = dma(sp, t8, A["prior"].bitcast(U8)[qt * P:(qt + 1) * P, :], free, s_tab[i])
            if b == 0:
                bi, bk, bfree = bank_ring.take()
                turned = bk[:].bitcast(BF16)
                for kb in range(NT):
                    m_n = do(pe, lambda e, kb=kb: e.transpose(
                        turned[:, kb * P:(kb + 1) * P], counts[:, kb, qt * P:(qt + 1) * P], C["ident"]),
                        [m_count, *bfree], s_pe["countT"])
                c, cnt, cfree = count_ring.take()
                mc = do(act, lambda e: e.activation(cnt, turned, ACT.Copy), [m_n, *cfree], s_act["count"])
                bank_ring.hold(bi, mc)
                m_st = dma(sp, count_d[qt], cnt, [mc], s_cnt[1])
                count_ring.hold(c, m_st)
                n, m_n = cnt, mc
                if qt == NT - 1:
                    m_tables.append(m_st)
            else:
                n = t
                m_n = m_t8 = dma(sp, t, count_d[qt], m_tables, s_tab[i])
            o = bias[:, qt, :]
            m1 = do(act, lambda e: e.activation(o, t8, ACT.Identity, bias=fl[6][:, b:b + 1], scale=fl[7][:, b:b + 1]),
                    [m_t8, m_flag, *free_bias], s_act["count"])
            m = do(dve, lambda e: e.tensor_scalar(t, n, 0.0, fl[5][:, b:b + 1], ALU.is_equal, ALU.mult),
                   [m_n, m_flag, *free], s_dve["bias"])
            m = do(dve, lambda e: e.tensor_tensor(o, o, t, ALU.add), [m, m1], s_dve["bias"])
            if b == 0:
                count_ring.hold(c, m)
            tab_ring.hold(i, m)
            mark[qt] = m

        def key_weight(b, kt, free_weight, mark):
            i, (t, t8), free = tab_ring.take()
            m_t = dma(sp, t8, A["priorT"].bitcast(U8)[kt * P:(kt + 1) * P, :], free, s_tab[i])
            if b == 0:
                n, m_n = counts[:, kt, :], m_count
            else:
                n = t
                m_n = m_t = dma(sp, t, countT_d[kt], m_tables, s_tab[i])
            o = weight[:, kt, :]
            m1 = do(act, lambda e: e.activation(o, t8, ACT.Identity, bias=fl[8][:, b:b + 1], scale=fl[9][:, b:b + 1]),
                    [m_t, m_flag, *free_weight], s_act["count"])
            m = do(dve, lambda e: e.scalar_tensor_tensor(out=o, in0=n, scalar=fl[3][:, b:b + 1], in1=o,
                                                         op0=ALU.mult, op1=ALU.add), [m1, m_n], s_dve["weight"])
            tab_ring.hold(i, m)
            mark[kt] = m

        stack_ring = Ring([0, 1, 2])
        s_stack = [sem(f"load_stack{r}") for r in range(3)]
        s_mrow = sem("store_mrow")
        rowmax_ring = Ring([0, 1])
        mrow_ring = Ring([0])
        mpart_ring = Ring([0, 1])
        o_ring = Ring([0, 1])

        def load_stack(att, b, q, stored):
            r, _, free = stack_ring.take()
            for qk, (dst, which) in enumerate(((stack_q, Q_PART), (stack_k, K_PART))):
                for blk, part in enumerate(which):
                    src = parts[att, b, qk, part, q * QUAD * DH:(q + 1) * QUAD * DH, :]
                    m = dma(sp, dst[blk * DH:(blk + 1) * DH, r], src.rearrange("(h d) t -> d h t", d=DH),
                            [*stored, *free], s_stack[r])
            return r, m

        def max_units(att, q, r, loaded, m_bias):
            causal = att == 1
            mi, _, free_mx = rowmax_ring.take()
            m_last = {}

            def unit(h, qt, half):
                lo, hi = half * HALF, min((half + 1) * HALF, (qt + 1) * P if causal else S)
                diag = causal and hi == (qt + 1) * P
                i, bk, free = bank_ring.take()
                mm = do(pe, lambda e: e.matmul(
                    bk[:, 0:hi - lo], stack_q[0:ROWS, r, h, qt * P:(qt + 1) * P], stack_k[0:ROWS, r, h, lo:hi],
                    start=True, stop=not diag), [loaded, *free], None if diag else s_pe["max"])
                if diag:
                    mm = do(pe, lambda e: e.matmul(bk[:, hi - lo - P:hi - lo], C["ident"], C["neg_qk"],
                                                   start=False, stop=True), [m_cb], s_pe["max"])
                acc = rowmax[:, mi, h, qt, half:half + 1]
                if causal:
                    m = do(dve, lambda e: e.tensor_reduce(acc, bk[:, 0:hi - lo], AX.X, ALU.max),
                           [mm, *free_mx, m_rowmax0], s_dve["rowmax"])
                else:
                    ji, scrap, jfree = junk_ring.take()
                    m = do(dve, lambda e: e.tensor_tensor_reduce(
                        out=scrap, in0=bk[:], in1=bias[:, qt, lo:hi], scale=1.0, scalar=-3e38,
                        op0=ALU.add, op1=ALU.max, accum_out=acc), [mm, m_bias[qt], *free_mx, m_rowmax0, *jfree],
                        s_dve["rowmax"])
                    junk_ring.hold(ji, m)
                bank_ring.hold(i, m)
                m_last["max"] = m

            def finish():
                sm = s_dve["maxpart"]
                pi, _, pfree = mpart_ring.take()
                top, neg, rem, rem2 = (mneg[:, k] for k in range(4))

                def part(k):
                    return mpart[:, pi, :, :, k].rearrange("p n h -> p h n")

                if causal:
                    m = do(dve, lambda e: e.tensor_reduce(
                        top[:, :, 0:NT // 2], rowmax[:, mi, :, 0:NT // 2, 0:1], AX.X, ALU.max),
                        [m_last["max"], *pfree], sm)
                    m = do(dve, lambda e: e.tensor_reduce(
                        top[:, :, NT // 2:NT], rowmax[:, mi, :, NT // 2:NT, :], AX.X, ALU.max), [m], sm)
                else:
                    m = do(dve, lambda e: e.tensor_reduce(top, rowmax[:, mi], AX.X, ALU.max),
                           [m_last["max"], *pfree], sm)
                rowmax_ring.hold(mi, m)
                m = do(dve, lambda e: e.tensor_scalar(neg, top, -1.0, None, ALU.mult), [m], sm)
                m = do(dve, lambda e: e.tensor_copy(part(0), neg), [m], sm)
                m = do(dve, lambda e: e.tensor_tensor(rem, neg, part(0), ALU.subtract), [m], sm)
                m = do(dve, lambda e: e.tensor_copy(part(1), rem), [m], sm)
                m = do(dve, lambda e: e.tensor_tensor(rem2, rem, part(1), ALU.subtract), [m], sm)
                m = do(dve, lambda e: e.tensor_copy(part(2), rem2), [m], sm)
                i, bk, free = bank_ring.take()
                rows = bk[0:PARTS * QUAD].bitcast(BF16)
                for qt in range(NT):
                    mm = do(pe, lambda e, qt=qt: e.transpose(
                        rows[:, qt * P:(qt + 1) * P], mpart[:, pi, qt].rearrange("p h k -> p (h k)"), C["ident"]),
                        [m, *free], s_pe["maxT"] if qt == NT - 1 else None)
                mpart_ring.hold(pi, mm)
                ri, _, rfree = mrow_ring.take()
                m = do(act, lambda e: e.activation(mrow[:, ri], rows, ACT.Copy), [mm, *rfree], s_act["mrow"])
                bank_ring.hold(i, m)
                for h in range(QUAD):
                    md = dma(sp, stack_q[ROWS:ROWS_M, r, h], mrow[h * PARTS:(h + 1) * PARTS, ri], [m], s_mrow)
                mrow_ring.hold(ri, md)
                m_last["rows"] = md

            steps = []
            for h in range(QUAD):
                for qt in range(NT):
                    for half in range(NH):
                        if not causal or half * HALF < (qt + 1) * P:
                            steps.append(lambda h=h, qt=qt, half=half: unit(h, qt, half))
            steps.append(finish)
            return steps, m_last

        def xs(b):
            return xT[:, :, b * S:(b + 1) * S]

        def weave(first, then, n):
            total = [(k / max(len(first), 1) * 0.9, 0, f) for k, f in enumerate(first)]
            total += [(k / max(len(then), 1), 1, f) for k, f in enumerate(then)]
            return [f for _, _, f in sorted(total, key=lambda z: z[:2])]

        y1 = o_raw
        s_y = sem("y_store")
        s_yload = [sem(f"y_load{i}") for i in range(2)]
        ATTENTIONS = [(0, 0), (0, 1), (1, 0), (1, 1)]
        JOBS = [(att, b, q) for att, b in ATTENTIONS for q in range(NQ)]
        m_bias, m_weight = [{}, {}], [{}, {}]
        m_norm, m_out = {}, {}
        qk_stored = {}
        m_resid = [None, None]

        def normalise_steps(c, o_pair, key):
            norm_free = [m for m in (m_zero, *m_out.values()) if m is not None]

            def step(half):
                cols = slice(half * HALF, (half + 1) * HALF)
                outs = []
                for which in ("sel_den", "sel_num"):
                    i, bk, free = bank_ring.take()
                    for par, (oi, m) in enumerate(o_pair):
                        mm = do(pe, lambda e, bk=bk, par=par, oi=oi, which=which: e.matmul(
                            bk[:], F[which][:, par * P:(par + 1) * P], o_raw[:, oi, cols],
                            start=(par == 0), stop=(par == 1)), [m, m_cf, *free], s_pe["sel"])
                    outs.append((i, bk, mm))
                (i0, den, md), (i1, num, mn) = outs
                on = o_norm[:, c, cols]
                m = do(dve, lambda e: e.reciprocal(on, den[:]), [md, *norm_free], s_dve["norm"])
                bank_ring.hold(i0, m)
                m = do(dve, lambda e: e.tensor_tensor(on, on, num[:], ALU.mult), [m, mn], s_dve["norm"])
                bank_ring.hold(i1, m)
                for oi, _ in o_pair:
                    o_ring.hold(oi, mn)
                m_norm[key] = m

            return [lambda half=half: step(half) for half in range(NH)]

        def project_out(w, key, mc, half):
            i, acc, free = bank_ring.take()
            for c in range(DC):
                mm = do(pe, lambda e, c=c: e.matmul(
                    acc[:], w[:, c, mc * P:(mc + 1) * P], o_norm[:, c, half * HALF:(half + 1) * HALF],
                    start=(c == 0), stop=(c == DC - 1)), [m_norm[key], m_wo, *free], s_pe["out"])
            m_out[key] = mm
            return i, acc, mm

        def between(b):
            state = {}

            def y_step(mc, half):
                i, acc, mm = project_out(wo, (0, b), mc, half)
                if "free" not in state:
                    state["free"] = [u for us in o_ring.users for u in us]
                m = do(act, lambda e: e.activation(
                    y1[:, mc, half * HALF:(half + 1) * HALF], acc[:], ACT.Identity, bias=bcol[:, 4, mc:mc + 1]),
                    [mm, *state["free"]], s_act["y"])
                bank_ring.hold(i, m)
                state["y"] = m
                if half == NH - 1:
                    state["store"] = dma(sp, y_d[b, mc], y1[:, mc, :], [m], s_y)

            ys = [lambda mc=mc, half=half: y_step(mc, half) for mc in range(DC) for half in range(NH)]
            for k in range(2):
                late_ring.hold(k, (s_pe["proj"], s_pe["proj"].value), *m_weight[1].values())
            steps, qk_stored[1, b] = project_qk(1, b, y1, lambda: [state["y"], m_w2], w2, 1, 0, late_ring)

            def release():
                for i in range(2):
                    o_ring.hold(i, state["store"], (s_pe["proj"], s_pe["proj"].value))
                state["done"] = True

            m_ystored[b] = state
            return ys + steps + [release]

        m_ystored = {}

        def add_residual(b):
            def step(mc, half):
                i, acc, mm = project_out(wp, (1, b), mc, half)
                o = xs(b)[:, mc, half * HALF:(half + 1) * HALF]
                m = do(dve, lambda e: e.scalar_tensor_tensor(
                    out=o, in0=acc[:], scalar=bcol[:, 5, mc:mc + 1], in1=o, op0=ALU.add, op1=ALU.add),
                    [mm], s_dve["resid"])
                bank_ring.hold(i, m)
                m_resid[b] = m

            return [lambda mc=mc, half=half: step(mc, half) for mc in range(DC) for half in range(NH)]

        def load_quad(n):
            att, b, q = JOBS[n]
            return load_stack(att, b, q, list(qk_stored[att, b].values()))

        def values_of(att, b):
            if att == 0:
                return project_v(0, lambda c: xs(b)[:, c], [m_x[b], m_w1], w1, 2)
            bufs = [prob_ring.take() for _ in range(DC)]
            loads = [dma(sp, buf, y_d[b, c], [m_ystored[b]["store"], *free], s_yload[c])
                     for c, (_, buf, free) in enumerate(bufs)]
            steps, marks = project_v(1, lambda c: bufs[c][1], [*loads, m_w2], w2, 2)

            def last():
                steps[-1]()
                for k, _, _ in bufs:
                    prob_ring.hold(k, marks["read"])

            return steps[:-1] + [last], marks

        projections = []
        for b in range(B):
            steps, qk_stored[0, b] = project_qk(0, b, xs(b), lambda b=b: [m_x[b], m_w1], w1, 0, 1, split_ring)
            projections += steps
            if b == 0:
                for f in projections:
                    f()
        after_splits = projections[len(projections) // 2:]
        quads = {0: load_quad(0)}
        for t in range(NT):
            key_bias(0, t, [m_counted], m_bias[0])
        for i in range(2):
            junk_ring.hold(i, m_hi, (s_dve["onehot"], s_dve["onehot"].value))
        max_steps, m_max = max_units(0, 0, *quads[0], m_bias[0])
        n_w = 0
        for k, f in enumerate(after_splits):
            f()
        quads[1] = load_quad(1)
        for k, f in enumerate(max_steps):
            f()
            if k % 8 == 4 and n_w < NT:
                key_weight(0, n_w, [m_counted], m_weight[0])
                n_w += 1
        for i in range(N_PROB):
            prob_ring.hold(i, *m_tables, *m_weight[0].values(), *[u for us in split_ring.users for u in us])
        stack_ring.hold(2, *[u for us in split_ring.users for u in us])

        o_pair, extras = [], []
        for n, (att, b, q) in enumerate(JOBS):
            causal = att == 1
            r, loaded = quads[n]
            m_rows = m_max["rows"]
            if n + 2 < len(JOBS):
                quads[n + 2] = load_quad(n + 2)
            if q == 0:
                v_steps, m_v = values_of(att, b)
            steps = []
            if n + 1 < len(JOBS):
                steps, m_max = max_units(JOBS[n + 1][0], JOBS[n + 1][2], *quads[n + 1], m_bias[JOBS[n + 1][1]])
            next_weights = (att, b, q) == (0, 0, NQ - 1)
            if next_weights:
                done_max = (s_dve["rowmax"], s_dve["rowmax"].value)
                steps = [lambda t=t: key_bias(1, t, [done_max], m_bias[1]) for t in range(NT)] + steps
            steps = weave(extras, steps, QUAD * NT)
            extras = []
            n_steps, done, total = len(steps), 0, QUAD * NT - 3
            _, pv, pvfree = pv_ring.take()

            def values(kt, ps):
                for half in range(NH):
                    lo = max(half * HALF, kt * P) if causal else half * HALF
                    hi = (half + 1) * HALF
                    if lo >= hi:
                        continue
                    last = kt == (hi // P - 1 if causal else NT - 1)
                    for g, (i, p, m) in enumerate(ps):
                        mm = do(pe, lambda e, g=g, p=p, lo=lo, hi=hi, last=last, q=q, pv=pv: e.matmul(
                            pv[g * HB:(g + 1) * HB, lo:hi], v_aug[:, kt, q * QUAD + g, :], p[:, lo:hi],
                            start=(kt == 0), stop=last), [m, m_v[kt], *pvfree], s_pe["pv"])
                for i, _, _ in ps:
                    prob_ring.hold(i, mm)
                return mm

            def weigh(kt, k, p, m):
                return do(dve, lambda e: e.scalar_tensor_tensor(
                    out=p, in0=p, scalar=HUGE, in1=weight[:, kt, :], op0=ALU.min, op1=ALU.mult),
                    [m, m_weight[b][kt]], s_dve["weigh"])

            waiting, ps, fresh, new = None, [], None, None
            for u in range(QUAD * NT + 1):
                kt, g = divmod(u, QUAD)
                for _ in range(2 if u else 0):
                    if v_steps:
                        v_steps.pop(0)()
                if u < QUAD * NT:
                    first = kt * P if causal else 0
                    i, sc, free = score_ring.take()
                    for half in range(NH):
                        lo, hi = max(half * HALF, first), (half + 1) * HALF
                        if lo >= hi:
                            continue
                        diag = causal and lo == first
                        mm = do(pe, lambda e, sc=sc, lo=lo, hi=hi, g=g, kt=kt, diag=diag, r=r: e.matmul(
                            sc[:, lo:hi], stack_k[0:ROWS_M, r, g, kt * P:(kt + 1) * P],
                            stack_q[0:ROWS_M, r, g, lo:hi], start=True, stop=not diag),
                            [m_rows, m_krows, loaded, *free], s_pe["score"])
                        if diag:
                            mm = do(pe, lambda e, sc=sc, lo=lo: e.matmul(
                                sc[:, lo:lo + P], C["ident"], C["neg_kq"], start=False, stop=True),
                                [], s_pe["score"])
                    k, p, pfree = prob_ring.take()
                    m = do(act, lambda e, p=p, sc=sc, first=first: e.activation(
                        p[:, first:S], sc[:, first:S], ACT.Exp), [mm, *pfree], s_act["exp"])
                    score_ring.hold(i, m)
                    new = (kt, k, p, m)
                due = (u + 1) * n_steps // total
                while done < min(due, n_steps):
                    steps[done]()
                    done += 1
                if fresh:
                    kt_f, k, p, m = fresh
                    if not causal:
                        m = weigh(*fresh)
                    ps.append((k, p, m))
                    if len(ps) == QUAD:
                        waiting, ps = (kt_f, ps), []
                        if next_weights:
                            key_weight(1, kt_f, [m], m_weight[1])
                fresh = new
                if waiting and (g == VALUES_LAG or u == QUAD * NT):
                    mm = values(*waiting)
                    waiting = None
            stack_ring.hold(r, mm)
            oi, _, ofree = o_ring.take()
            m = do(act, lambda e, oi=oi, pv=pv: e.activation(o_raw[:, oi], pv[:], ACT.Copy), [mm, *ofree], s_act["o"])
            pv_ring.hold(0, m)
            o_pair.append((oi, m))
            if len(o_pair) == 2:
                extras += normalise_steps(q // 2, o_pair, (att, b))
                o_pair = []
            if q == NQ - 1:
                v_ring.hold(0, mm)
                extras += add_residual(b) if causal else between(b)
        for f in extras:
            f()
        ph1.close()
        end1 = [(s, s.value) for s in all_sems if s.value]
        ph2 = ExitStack()

        def s2(name, shape, dt=F32):
            return sb(name, shape, dt, ph2)

        w_g = s2("w_g", [P, 2 * DC, D])
        w_n1 = s2("w_n1", [P, DC, HN])
        w_n2 = s2("w_n2", [HN, ND, P])
        w_soma = s2("w_soma", [P, DC, D])
        w_temp = s2("w_temp", [P, DC, D])
        w_out = s2("w_out", [P, DC, D])
        w_rt = s2("w_router", [P, DC, E])
        mcol = s2("mix_cols", [P, 3, DC])
        b_n1 = s2("b_n1", [HN, 1])
        b_n2 = s2("b_n2", [P, ND])
        blend = s2("blend", [P, ND, DC])
        ln_rows = s2("ln_rows", [P, 2, D])
        taus = s2("taus", [P, 1 + ND])
        tiny = s2("tiny", [P, 8, 8])
        wsg = s2("sg", [P, DC, I_S])
        wsu = s2("su", [P, DC, I_S])
        wsd = s2("sd", [P, I_S // P, D])
        h_tok = s2("h_tok", [P, B * NT, D])
        y = h_tok
        hT = s2("hT", [P, DC, T])
        big = s2("big", [P, 15 * S])

        def big_at(k, n):
            return big[:, k * S:(k + n) * S]

        ctxT, gated, tr0, tr1, soma, gate = (
            big_at(2 * k, 2).rearrange("p (c t) -> p c t", c=DC) for k in range(6))
        mod = big_at(12, 2).rearrange("p (c t) -> p c t", c=ND)
        h1 = big_at(14, 1)[0:HN]
        WE = 2 * DC * I_R + (I_R // P) * D
        stats = s2("stats", [P, 4, 6])
        mean_var = s2("mean_var", [P, B * NT, 2])
        rstd = s2("rstd", [P, B * NT])
        ssq = s2("ssq", [P, B * NT])
        rms = s2("rms", [P, B * NT])
        logit = s2("logit", [P, B * NT, E])
        top8 = s2("top8", [P, B * NT, 8])
        best = s2("best", [P, B * NT, 8], U32)
        best_f = s2("best_f", [P, B * NT, TOPK])
        lmax = s2("lmax", [P, B * NT])
        pick = s2("pick", [P, TOPK, B * NT, E])
        mask = s2("mask", [P, B * NT, E], BF16)
        before = s2("before", [P, B * NT + 1, E], BF16)
        slot_map = s2("slot_map", [P, B * NT, E])
        far = s2("far", [P, B * NT, E])
        slot = s2("slot", [P, TOPK, B * NT])
        slot_w = s2("slot_w", [P, TOPK, B * NT], U32)
        slot_r = s2("slot_r", [P, TOPK, B * NT], U32)
        gain = s2("gain", [P, TOPK, B * NT])
        gsum = s2("gsum", [P, B * NT])
        sil = s2("sil", [P, 2, HALF])
        act_s = s2("act_s", [P, 3, HALF])
        xg = s2("xg", [P, 2, 3, D])
        xgT = s2("xgT", [P, 2, DC, CAP])
        act_e = big_at(12, 3)[:, 0:I_R // P * CAP].rearrange("p (i n) -> p i n", n=CAP)
        e_out = s2("e_out", [P, 2, 3, D])
        got = [w[:, c] for w in (w_soma, w_temp) for c in range(DC)]

        load("mix", w_g[:], chunks(A["w_g"]), after=end1)
        load("mix", w_n1[:], chunks(A["w_n1"]))
        load("mix", w_n2[:], A["w_n2"])
        load("mix", w_soma[:], chunks(A["w_soma"]))
        load("mix", w_temp[:], chunks(A["w_temp"]))
        load("mix", w_out[:], chunks(A["w_out"]))
        load("mix", w_rt[:], chunks(A["w_router"]))
        load("mix", mcol[:], A["mix_cols"])
        load("mix", b_n1[:], A["b_n1"])
        load("mix", blend[:], A["blend"])
        load("mix", ln_rows[:], A["ln_rows"].partition_broadcast(P))
        load("mix", b_n2[:], A["b_n2"].partition_broadcast(P))
        m_mw = load("mix", taus[:], A["taus"].partition_broadcast(P))
        m_sg = load("sg", wsg[:], chunks(A["sg"]))
        m_su = load("su", wsu[:], chunks(A["su"]))
        m_sd = load("sd", wsd[:], chunks(A["sd"]))

        sx = s_dve["mix"]
        alpha, ex, bmax, bw, bsum = (tiny[:, k] for k in range(5))
        m = do(act, lambda e: e.activation(ex[:, 0:3], taus[:], ACT.Exp), [m_mw, *end1], s_act["gate"])
        m = do(dve, lambda e: e.tensor_scalar(ex[:, 0:3], ex[:, 0:3], 1.0, None, ALU.add), [m, *end1], sx)
        m_alpha = do(dve, lambda e: e.reciprocal(alpha[:, 0:3], ex[:, 0:3]), [m], sx)
        m = do(dve, lambda e: e.tensor_tensor(bmax[:, 0:DC], blend[:, 0], blend[:, 1], ALU.max), [m_mw], sx)
        for d in range(ND):
            m = do(dve, lambda e, d=d: e.tensor_tensor(bw[:, d * DC:(d + 1) * DC], blend[:, d], bmax[:, 0:DC],
                                                       ALU.subtract), [m], sx)
        m = do(act, lambda e: e.activation(bw[:, 0:4], bw[:, 0:4], ACT.Exp), [m], s_act["gate"])
        m = do(dve, lambda e: e.tensor_tensor(bsum[:, 0:DC], bw[:, 0:DC], bw[:, DC:2 * DC], ALU.add), [m], sx)
        m = do(dve, lambda e: e.reciprocal(bmax[:, 0:DC], bsum[:, 0:DC]), [m], sx)
        for d in range(ND):
            m_bw = do(dve, lambda e, d=d: e.tensor_tensor(bw[:, d * DC:(d + 1) * DC], bw[:, d * DC:(d + 1) * DC],
                                                          bmax[:, 0:DC], ALU.mult), [m], sx)
            m = m_bw

        m_before = do(dve, lambda e: e.memset(before[:, 0, :], 0.0), [], s_dve["route"])

        wide_ring = Ring(wide)
        bank_ring = Ring(bank)

        def matvec(dst_ring, K, wt, srcs, after, sem_, rows=P):
            i, acc, free = dst_ring.take()
            for h in range(NH):
                for k in range(K):
                    mm = do(pe, lambda e, h=h, k=k: e.matmul(
                        acc[0:rows, h * HALF:(h + 1) * HALF], wt(k), srcs(k)[:, h * HALF:(h + 1) * HALF],
                        start=(k == 0), stop=(k == K - 1)), [*after, *free],
                        sem_ if (h, k) == (NH - 1, K - 1) else None)
            return i, acc, mm

        def feature_cols(w, mc):
            return lambda k: w[:, k, mc * P:(mc + 1) * P]

        mix_free = []
        logit_bank = {}

        def mix(b):
            x = xs(b)
            sp_, sa, sd_ = s_pe["mix"], s_act["gate"], s_dve["mix"]
            ready = [m_resid[b], m_mw]
            m_ctx = [do(dve, lambda e, c=c: e.tensor_tensor_scan(
                ctxT[:, c], alpha[:, 0:1].broadcast_to([P, S]), x[:, c], 0.0, ALU.mult, ALU.add),
                [*ready, m_alpha, *mix_free], s_dve["scan"]) for c in range(DC)][-1]
            i, acc, mm = matvec(wide_ring, DC, lambda k: w_n1[:, k], lambda k: x[:, k], ready, sp_, HN)
            m_h1 = do(act, lambda e, acc=acc: e.activation(h1, acc[0:HN], ACT.Gelu, bias=b_n1[:]), [mm, *mix_free], sa)
            wide_ring.hold(i, m_h1)
            m_soma = []
            for mc in range(DC):
                i, acc, mm = matvec(wide_ring, DC, feature_cols(w_soma, mc), lambda k: x[:, k], ready, sp_)
                m_soma.append(do(act, lambda e, acc=acc, mc=mc: e.activation(
                    soma[:, mc], acc[:], ACT.Gelu, bias=mcol[:, 1, mc:mc + 1]), [mm], sa))
                wide_ring.hold(i, m_soma[-1])
            m_mod = []
            for d in range(ND):
                i, acc, mm = matvec(wide_ring, 1, lambda k, d=d: w_n2[:, d], lambda k: h1, [m_h1], sp_)
                m_mod.append(do(act, lambda e, acc=acc, d=d: e.activation(
                    mod[:, d], acc[:], ACT.Sigmoid, bias=b_n2[:, d:d + 1]), [mm], sa))
                wide_ring.hold(i, m_mod[-1])
            m_gated = []
            for mc in range(DC):
                i, acc, mm = matvec(wide_ring, 2 * DC, feature_cols(w_g, mc),
                                    lambda k: x[:, k] if k < DC else ctxT[:, k - DC], [*ready, m_ctx], sp_)
                m = do(act, lambda e, acc=acc, mc=mc: e.activation(
                    gate[:, mc], acc[:], ACT.Sigmoid, bias=mcol[:, 0, mc:mc + 1]), [mm], sa)
                wide_ring.hold(i, m)
                m_gated.append(do(dve, lambda e, mc=mc: e.tensor_tensor(gated[:, mc], x[:, mc], gate[:, mc],
                                                                        ALU.mult), [m], sd_))
            m_temporal = []
            for c in range(DC):
                for d, tr in enumerate((tr0, tr1)):
                    m = do(dve, lambda e, c=c, d=d, tr=tr: e.scalar_tensor_tensor(
                        out=tr[:, c], in0=mod[:, d], scalar=0.5, in1=gated[:, c], op0=ALU.add, op1=ALU.mult),
                        [m_mod[d], m_gated[c]], sd_)
                    m = do(dve, lambda e, c=c, d=d, tr=tr: e.tensor_tensor_scan(
                        tr[:, c], alpha[:, 1 + d:2 + d].broadcast_to([P, S]), tr[:, c], 0.0, ALU.mult, ALU.add),
                        [m], s_dve["scan"])
                    if d == 0:
                        m0 = do(dve, lambda e, c=c: e.tensor_scalar(tr0[:, c], tr0[:, c], bw[:, c:c + 1], None,
                                                                    ALU.mult), [m, m_bw], sd_)
                m_temporal.append(do(dve, lambda e, c=c: e.scalar_tensor_tensor(
                    out=tr0[:, c], in0=tr1[:, c], scalar=bw[:, DC + c:DC + c + 1], in1=tr0[:, c],
                    op0=ALU.mult, op1=ALU.add), [m, m0], sd_))
            m_in = []
            for mc in range(DC):
                i, acc, mm = matvec(wide_ring, DC, feature_cols(w_temp, mc), lambda k: tr0[:, k], m_temporal, sp_)
                m = do(act, lambda e, acc=acc, mc=mc: e.activation(
                    gate[:, mc], acc[:], ACT.Sigmoid, bias=mcol[:, 2, mc:mc + 1]), [mm, m_gated[mc]], sa)
                wide_ring.hold(i, m)
                m_in.append(do(dve, lambda e, mc=mc: e.tensor_tensor(soma[:, mc], soma[:, mc], gate[:, mc],
                                                                     ALU.mult), [m, m_soma[mc]], sd_))
            return m_in

        def normalise(b, m_in):
            sl = s_dve["ln"]
            ts = slice(b * NT, (b + 1) * NT)
            stat_ring = Ring(list(range(4)))
            marks = []
            for t in range(NT):
                i, bk, free = bank_ring.take()
                for c in range(DC):
                    mm = do(pe, lambda e, bk=bk, c=c, t=t: e.matmul(
                        bk[:, 0:D], soma[:, c, t * P:(t + 1) * P], w_out[:, c], start=(c == 0), stop=(c == DC - 1)),
                        [*m_in, *free], s_pe["tok"] if c == DC - 1 else None)
                si_, _, sfree = stat_ring.take()
                m3 = do(act, lambda e, bk=bk, t=t: e.activation(h_tok[:, b * NT + t], bk[:, 0:D], ACT.Copy),
                        [mm], s_act["copy"])
                m1 = do(dve, lambda e, t=t, si_=si_: e.bn_stats(stats[:, si_], h_tok[:, b * NT + t]),
                        [m3, *sfree], sl)
                m2 = do(dve, lambda e, si_=si_, t=t: e.bn_aggr(mean_var[:, b * NT + t], stats[:, si_]), [m1], sl)
                stat_ring.hold(si_, m2)
                bank_ring.hold(i, m3)
            mix_free.clear()
            mix_free.append(mm)
            m = do(dve, lambda e: e.tensor_scalar(rstd[:, ts], mean_var[:, ts, 1], LN_EPS, None, ALU.add), [m2], sl)
            m = do(act, lambda e: e.activation(rstd[:, ts], rstd[:, ts], ACT.Sqrt), [m, m2], s_act["stat"])
            m = do(dve, lambda e: e.reciprocal(rstd[:, ts], rstd[:, ts]), [m], sl)
            for t in range(b * NT, (b + 1) * NT):
                mn = do(dve, lambda e, t=t: e.tensor_scalar(h_tok[:, t], h_tok[:, t], mean_var[:, t, 0:1],
                                                            rstd[:, t:t + 1], ALU.subtract, ALU.mult), [m, m3], sl)
            ht = h_tok[:, ts]
            m = do(dve, lambda e: e.tensor_tensor(ht, ht, ln_rows[:, 0:1].broadcast_to([P, NT, D]), ALU.mult),
                   [mn], sl)
            m_h = do(dve, lambda e: e.tensor_tensor(ht, ht, ln_rows[:, 1:2].broadcast_to([P, NT, D]), ALU.add),
                     [m], sl)
            for g in range(NT // 4):
                for c in range(DC):
                    i, bk, free = bank_ring.take()
                    for k in range(4):
                        mm = do(pe, lambda e, bk=bk, c=c, k=k, t=b * NT + 4 * g + k: e.transpose(
                            bk[:, k * P:(k + 1) * P], h_tok[:, t, c * P:(c + 1) * P], F["ident"]),
                            [m_h, *free], s_pe["hT"] if k == 3 else None)
                    m_hT = do(act, lambda e, bk=bk, c=c, o=b * S + g * HALF: e.activation(
                        hT[:, c, o:o + HALF], bk[:], ACT.Copy), [mm], s_act["copy"])
                    bank_ring.hold(i, m_hT)
            scrap_ring = Ring([sil[:, 0, 0:D], sil[:, 1, 0:D]])
            for t in range(b * NT, (b + 1) * NT):
                k, sc, free = scrap_ring.take()
                m = do(act, lambda e, sc=sc, t=t: e.activation(sc, h_tok[:, t], ACT.Square,
                                                               accum_out=ssq[:, t:t + 1]), [m_h, *free], s_act["stat"])
                scrap_ring.hold(k, m)
            m = do(dve, lambda e: e.tensor_scalar(rms[:, ts], ssq[:, ts], 1.0 / D, RMS_EPS, ALU.mult, ALU.add), [m], sl)
            m = do(act, lambda e: e.activation(rms[:, ts], rms[:, ts], ACT.Sqrt), [m], s_act["stat"])
            m_rms = do(dve, lambda e: e.reciprocal(rms[:, ts], rms[:, ts]), [m], sl)
            return m_h, m_hT, m_rms

        def route(b, m_h, m_hT, m_rms, last_before):
            sr = s_dve["route"]
            ts = slice(b * NT, (b + 1) * NT)
            i, bk, free = bank_ring.take()
            for t in range(NT):
                for c in range(DC):
                    mm = do(pe, lambda e, t=t, c=c: e.matmul(
                        bk[:, t * E:(t + 1) * E], hT[:, c, b * S + t * P:b * S + (t + 1) * P], w_rt[:, c],
                        start=(c == 0), stop=(c == DC - 1)), [m_hT, *free],
                        s_pe["logit"] if (t, c) == (NT - 1, DC - 1) else None)
            lg = logit[:, ts]
            m = do(dve, lambda e: e.tensor_tensor(lg, bk[:, 0:NT * E].rearrange("p (t x) -> p t x", t=NT),
                                                  rms[:, ts].unsqueeze(2).broadcast_to([P, NT, E]), ALU.mult),
                   [mm, m_rms], sr)
            bank_ring.hold(i, m)
            m = do(dve, lambda e: e.tensor_reduce(lmax[:, ts], lg, AX.X, ALU.max), [m], sr)
            m = do(dve, lambda e: e.tensor_tensor(lg, lg, lmax[:, ts].unsqueeze(2).broadcast_to([P, NT, E]),
                                                  ALU.subtract), [m], sr)
            m = do(act, lambda e: e.activation(lg, lg, ACT.Exp), [m], s_act["route"])
            for t in range(b * NT, (b + 1) * NT):
                m1 = do(dve, lambda e, t=t: e.max(out=top8[:, t], in_=logit[:, t]), [m], sr)
            m_top = m1
            for t in range(b * NT, (b + 1) * NT):
                m1 = do(dve, lambda e, t=t: e.max_index(out=best[:, t], in_max=top8[:, t], in_values=logit[:, t]),
                        [m_top], sr)
            m = do(dve, lambda e: e.tensor_copy(best_f[:, ts], best[:, ts, 0:TOPK]), [m1], sr)
            m2 = do(dve, lambda e: e.tensor_reduce(gsum[:, ts], top8[:, ts, 0:TOPK], AX.X, ALU.add), [m_top], sr)
            m2 = do(dve, lambda e: e.reciprocal(gsum[:, ts], gsum[:, ts]), [m2], sr)
            for k in range(TOPK):
                m_gain = do(dve, lambda e, k=k: e.tensor_tensor(gain[:, k, ts], top8[:, ts, k], gsum[:, ts],
                                                                ALU.mult), [m2], sr)
            marks = []
            for k in range(TOPK):
                marks.append(do(dve, lambda e, k=k: e.tensor_tensor(
                    pick[:, k, ts], F["iota_e"].unsqueeze(1).broadcast_to([P, NT, E]),
                    best_f[:, ts, k:k + 1].broadcast_to([P, NT, E]), ALU.is_equal), [m], sr))
            m = do(dve, lambda e: e.tensor_tensor(mask[:, ts], pick[:, 0, ts], pick[:, 1, ts], ALU.add), marks, sr)
            for t in range(b * NT, (b + 1) * NT):
                last_before = do(dve, lambda e, t=t: e.tensor_tensor(before[:, t + 1], before[:, t], mask[:, t],
                                                                     ALU.add), [m, last_before], sr)
            i, bk, free = bank_ring.take()
            for t in range(NT):
                do(pe, lambda e, t=t: e.matmul(bk[:, t * E:(t + 1) * E], C["ones"], before[:, b * NT + t],
                                               start=True, stop=False), [last_before, *free])
                mm = do(pe, lambda e, t=t: e.matmul(bk[:, t * E:(t + 1) * E], C["before"], mask[:, b * NT + t],
                                                    start=False, stop=True), [], s_pe["pos"])
            pos = bk[:, 0:NT * E].rearrange("p (t x) -> p t x", t=NT)
            m = do(dve, lambda e: e.tensor_scalar(far[:, ts], pos, float(CAP), FAR, ALU.is_ge, ALU.mult), [mm], sr)
            m1 = do(dve, lambda e: e.tensor_tensor(slot_map[:, ts], pos,
                                                   F["slot_e"].unsqueeze(1).broadcast_to([P, NT, E]), ALU.add), [mm], sr)
            bank_ring.hold(i, m1)
            m = do(dve, lambda e: e.tensor_tensor(slot_map[:, ts], slot_map[:, ts], far[:, ts], ALU.add), [m, m1], sr)
            for k in range(TOPK):
                m1 = do(dve, lambda e, k=k: e.tensor_tensor(pick[:, k, ts], pick[:, k, ts], slot_map[:, ts], ALU.mult),
                        [m], sr)
                m1 = do(dve, lambda e, k=k: e.tensor_reduce(slot[:, k, ts], pick[:, k, ts], AX.X, ALU.add), [m1], sr)
                m_w = do(dve, lambda e, k=k: e.tensor_copy(slot_w[:, k, ts], slot[:, k, ts]), [m1], sr)
                m_r = do(dve, lambda e, k=k: e.tensor_scalar(slot_r[:, k, ts], slot[:, k, ts], float(SLOTS), None,
                                                             ALU.min), [m1], sr)
            for t in range(b * NT, (b + 1) * NT):
                for k in range(TOPK):
                    m_sent = pool.add(lambda e, t=t, k=k: e.indirect_dma_start(
                        out=slots_in, out_offset=bass.IndirectOffsetOnAxis(ap=slot_w[:, k, t:t + 1], axis=0),
                        in_=h_tok[:, t], in_offset=None, bounds_check=SLOTS - 1, oob_is_err=False),
                        [m_w, m_h, m_zero], s_sent, 16)
            return last_before, m_sent, m_r, m_gain

        s_sent = sem("tokens_sent")
        last_before = m_before
        for b in range(B):
            m_in = mix(b)
            m_h, m_hT, m_rms = normalise(b, m_in)
            last_before, m_sent, m_r, m_gain = route(b, m_h, m_hT, m_rms, last_before)

        def w_slot(k):
            o = 3 * 2 * S * k
            g, u, dn = (big[:, o + j * 2 * S:o + (j + 1) * 2 * S] for j in range(3))
            return (g.rearrange("p (c m) -> p c m", c=DC), u.rearrange("p (c m) -> p c m", c=DC),
                    dn.rearrange("p (i n) -> p i n", i=I_R // P))

        expert_ring = Ring([w_slot(0), w_slot(1)])
        s_we = [sem("load_expert0"), sem("load_expert1")]
        mixed = [(s_pe["tok"], s_pe["tok"].value), (s_pe["mix"], s_pe["mix"].value), (s_dve["mix"], s_dve["mix"].value)]
        expert_w = {}

        def load_expert(x):
            k, (g, u, dn), free = expert_ring.take()
            for dst, src in ((g, chunks(A["rg"][x])), (u, chunks(A["ru"][x])), (dn, chunks(A["rd"][x]))):
                m = dma(sp, dst, src, [*mixed, *free], s_we[k])
            expert_w[x] = (k, g, u, dn, m)

        gu_ring = Ring(wide[:2])
        acc_ring = Ring(wide[2:])
        sil_ring = Ring([sil[:, 0], sil[:, 1]])
        for k in range(2):
            sil_ring.hold(k, (s_act["stat"], s_act["stat"].value))
        act_ring = Ring([act_s[:, k] for k in range(3)])
        wides = [u for us in wide_ring.users for u in us]
        for i in range(2):
            gu_ring.hold(i, *wides)
        acc_ring.hold(0, *wides)

        def gate_up(n, wg_, wu_, col, src, ready, dst, dst_free):
            i, gu, free = gu_ring.take()
            for o, wt in ((0, wg_), (HALF, wu_)):
                for c in range(DC):
                    mm = do(pe, lambda e, o=o, wt=wt, c=c: e.matmul(
                        gu[:, o:o + n], wt[:, c, col:col + P], src(c), start=(c == 0), stop=(c == DC - 1)),
                        [*ready, *free], s_pe["gu"] if c == DC - 1 and o else None)
            k, sl_, sfree = sil_ring.take()
            m = do(act, lambda e: e.activation(sl_[:, 0:n], gu[:, 0:n], ACT.Silu), [mm, *sfree], s_act["silu"])
            m = do(dve, lambda e: e.tensor_tensor(dst, sl_[:, 0:n], gu[:, HALF:HALF + n], ALU.mult),
                   [m, *dst_free], s_dve["act"])
            gu_ring.hold(i, m)
            sil_ring.hold(k, m)
            return m

        def shared(tc):
            n_i, tiles = I_S // P, HALF // P
            ai, acc, afree = acc_ring.take()
            def down(i, k, a, m):
                for t in range(tiles):
                    mm = do(pe, lambda e, t=t: e.matmul(
                        acc[:, t * D:(t + 1) * D], a[:, t * P:(t + 1) * P], wsd[:, i],
                        start=(i == 0 and t % 2 == 0), stop=False, skip_group_check=True),
                        [m, m_sd, *afree], s_pe["down"])
                act_ring.hold(k, mm)
            late = None
            for i in range(n_i):
                k, a, free = act_ring.take()
                m = gate_up(HALF, wsg, wsu, i * P, lambda c: hT[:, c, tc * HALF:(tc + 1) * HALF],
                            [m_hT, m_sg, m_su], a, free)
                if late:
                    down(*late)
                late = (i, k, a, m)
            down(*late)
            for t in range(tiles):
                for c in range(DC):
                    mm = do(pe, lambda e, t=t, c=c: e.matmul(
                        acc[:, t * D + c * P:t * D + (c + 1) * P],
                        xT[:, c, tc * HALF + t * P:tc * HALF + (t + 1) * P], F["ident"],
                        start=False, stop=True, skip_group_check=True), [], s_pe["down"])
            yt = y[:, tc * tiles:(tc + 1) * tiles]
            m = do(act, lambda e: e.activation(yt.rearrange("p t n -> p (t n)"), acc[:], ACT.Copy),
                   [mm, m_sent], s_act["copy"])
            acc_ring.hold(ai, m)
            return m

        load_expert(0)
        load_expert(1)
        m_shared = {0: shared(0), 1: shared(1)}

        xg_ring, xgT_ring, eo_ring = (Ring([0, 1]) for _ in range(3))
        s_xg = [sem("load_tokens0"), sem("load_tokens1")]
        s_eo = [sem("store_expert0"), sem("store_expert1")]
        act_e_ring = Ring([act_e])
        act_e_ring.hold(0, *mixed)
        TILES = [(0, P), (P, P), (2 * P, CAP - 2 * P)]

        def fetch(x):
            k, _, free = xg_ring.take()
            rows = slots_in[x * CAP:(x + 1) * CAP, :]
            dma(sp, xg[:, k, 0:2], rows[0:2 * P, :].rearrange("(t p) n -> p t n", p=P), [m_sent, *free], s_xg[k])
            m = dma(sp, xg[0:CAP - 2 * P, k, 2], rows[2 * P:CAP, :], [], s_xg[k])
            kt, _, tfree = xgT_ring.take()
            for c in range(DC):
                i, bk, bfree = bank_ring.take()
                for t, (o, n) in enumerate(TILES):
                    mm = do(pe, lambda e, c=c, t=t, o=o, n=n, bk=bk: e.transpose(
                        bk[:, o:o + n], xg[0:n, k, t, c * P:(c + 1) * P], F["ident"][0:n, 0:n]), [m, *bfree],
                        s_pe["xT"] if t == 2 else None)
                m2 = do(act, lambda e, c=c, bk=bk: e.activation(xgT[:, kt, c], bk[:, 0:CAP], ACT.Copy),
                        [mm, *tfree], s_act["copy"])
                bank_ring.hold(i, m2)
            xg_ring.hold(k, mm)
            return kt, m2

        fetched = {0: fetch(0)}
        stored_e = []
        for x in range(E):
            k, wg_, wu_, wd_, m_w = expert_w[x]
            kt, m_x_ = fetched[x]
            _, _, ae_free = act_e_ring.take()
            ms = []
            for i in range(I_R // P):
                ms.append(gate_up(CAP, wg_, wu_, i * P, lambda c, kt=kt: xgT[:, kt, c], [m_w, m_x_],
                                  act_e[:, i], ae_free))
                if i == 3 and x + 1 < E:
                    fetched[x + 1] = fetch(x + 1)
            xgT_ring.hold(kt, (s_pe["gu"], s_pe["gu"].value))
            ai, acc, afree = acc_ring.take()
            for t, (o, n) in enumerate(TILES):
                for i in range(I_R // P):
                    mm = do(pe, lambda e, t=t, o=o, n=n, i=i, wd_=wd_, acc=acc: e.matmul(
                        acc[0:n, t * D:(t + 1) * D], act_e[:, i, o:o + n], wd_[:, i],
                        start=(i == 0), stop=(i == I_R // P - 1)), [ms[i], *afree], s_pe["down"])
            act_e_ring.hold(0, mm)
            expert_ring.hold(k, mm)
            if x + 2 < E:
                load_expert(x + 2)
            ko, _, ofree = eo_ring.take()
            do(dve, lambda e, ko=ko, acc=acc: e.tensor_copy(
                e_out[:, ko, 0:2], acc[:, 0:2 * D].rearrange("p (t n) -> p t n", t=2)), [mm, *ofree], s_dve["copy"])
            m = do(dve, lambda e, ko=ko, acc=acc: e.tensor_copy(e_out[0:CAP - 2 * P, ko, 2],
                                                                acc[0:CAP - 2 * P, 2 * D:3 * D]), [], s_dve["copy"])
            acc_ring.hold(ai, m)
            rows = slots_out[x * CAP:(x + 1) * CAP, :]
            dma(sp, rows[0:2 * P, :].rearrange("(t p) n -> p t n", p=P), e_out[:, ko, 0:2], [m], s_eo[ko])
            m = dma(sp, rows[2 * P:CAP, :], e_out[0:CAP - 2 * P, ko, 2], [], s_eo[ko])
            eo_ring.hold(ko, m)
            stored_e = (stored_e + [m])[-2:]

        for tc in range(2, T // HALF):
            m_shared[tc] = shared(tc)

        got_ring = Ring(list(range(4)))
        for k in range(4):
            got_ring.hold(k, *mixed)
        s_got = [sem(f"gather{k}") for k in range(4)]
        s_done = sem("store_out")
        for t in range(B * NT):
            m = m_shared[t * P // HALF]
            for k in range(TOPK):
                g, _, free = got_ring.take()
                mg = pool.add(lambda e, g=g, k=k, t=t: e.indirect_dma_start(
                    out=got[g], out_offset=None, in_=slots_out,
                    in_offset=bass.IndirectOffsetOnAxis(ap=slot_r[:, k, t:t + 1], axis=0)),
                    [*stored_e, m_r, m_zero, *free], s_got[g], 16)
                m = do(dve, lambda e, g=g, k=k, t=t: e.scalar_tensor_tensor(
                    out=y[:, t], in0=got[g], scalar=gain[:, k, t:t + 1], in1=y[:, t],
                    op0=ALU.mult, op1=ALU.add), [mg, m, m_gain], s_dve["comb"])
                got_ring.hold(g, m)
            md = dma(sp, out[t * P:(t + 1) * P, :], y[:, t], [m], s_done)
        ph2.close()
        sp.items.append(([md], None, None, 0))

        block = ctx.enter_context(nc.Block())

        @block.sync
        def _(e):
            sp.emit(e)

        @block.gpsimd
        def _(e):
            pool.emit(e)

        @block.scalar
        def _(e):
            act.emit(e)

        @block.vector
        def _(e):
            dve.emit(e)

        @block.tensor
        def _(e):
            pe.emit(e)




def constants():
    import numpy as np

    f = np.zeros((P, CF_W), np.float32)
    f[:, :P] = np.eye(P)
    for par in range(2):
        for g in range(QUAD):
            for d in range(DH):
                col = par * P + par * (P // 2) + g * DH + d
                f[g * HB + d, CF["sel_num"][0] + col] = 1
                f[g * HB + DH, CF["sel_den"][0] + col] = 1
    a = CF["iota_e"][0]
    f[:, a:a + E] = np.arange(E)
    f[:, a + E:a + 2 * E] = np.arange(E) * CAP
    r, c = np.arange(P)[:, None], np.arange(P)[None, :]
    b = np.concatenate([np.eye(P), np.where(c > r, NEG, 0), np.where(r > c, NEG, 0), r < c, np.ones((P, P)),
                        np.broadcast_to(c, (P, P))], 1)
    span = np.where(r // K_SPARSE == np.arange(SPANS * NT)[None, :] // NT, np.arange(SPANS * NT)[None, :] % NT, -1)
    return {"const_f32": f, "const_bf16": b.astype(mybir.dt.np(BF16)), "span_iota": span.astype(mybir.dt.np(BF16))}


def layout(inputs):
    import numpy as np

    i = {k: np.asarray(v) for k, v in inputs.items()}
    a = constants()
    a["xT"] = i["x"].reshape(T, D).T
    def by_span(m):
        return np.ascontiguousarray(m.reshape(SPANS, SPAN, K_SPARSE).transpose(0, 2, 1)).reshape(P, SPAN)

    a["idx"] = by_span(i["itok_Sx32_0_1023"])
    a["idx_mask"] = by_span(i["mask_Sx32_bk1"]).view(np.int32)
    a["prior"] = i["mask_SxS_bk0"].view(np.int32)
    a["priorT"] = i["mask_SxS_bk0"].T.copy().view(np.int32)
    a["u_prev"] = i["condB_uprev"]
    a["w_prior"] = np.concatenate([i[f"L0_cond_W{n}"].T for n in "qkv"], 1)
    a["w_causal"] = i["L0_attn_W_kqv"].T
    a["w_o"] = i["L0_cond_Wo"].T
    a["w_proj"] = i["L0_attn_W_proj"].T
    bk = i["L0_attn_b_kqv"]
    a["bias_cols"] = np.stack([i["L0_cond_bq"], i["L0_cond_bk"], bk[D:2 * D], bk[:D], i["L0_cond_bo"],
                               i["L0_attn_b_proj"]])
    a["bias_v"] = np.stack([i["L0_cond_bv"], bk[2 * D:]])
    c2 = "L0_cond2_"
    a["taus"] = np.concatenate([i[c2 + "tau_ctx"].reshape(1), i["condB_tauraws"]])
    a["w_g"] = i[c2 + "Wg"].T
    a["w_n1"] = i[c2 + "Wn1"].T
    a["w_n2"] = np.repeat(i["cond_256"].T[:, :, None], P, 2)
    a["b_n2"] = i["condB_bn2"]
    a["b_n1"] = i[c2 + "bn1"].reshape(HN, 1)
    a["blend"] = i["cond_1024"]
    a["w_soma"] = i[c2 + "Wsoma"].T
    a["w_temp"] = i[c2 + "Wtemp"].T
    a["w_out"] = i[c2 + "Wout"].T
    a["mix_cols"] = np.stack([i[c2 + "bg"], i[c2 + "bsoma"], i[c2 + "btemp"]])
    a["ln_rows"] = np.stack([i[c2 + "gamma"], i[c2 + "beta"]])
    a["w_router"] = i["L0_ffn_router_w"].T
    for n in ("rg", "ru", "rd", "sg", "su", "sd"):
        a[n] = i["L0_ffn_" + n]
    for n in ("bias_cols", "mix_cols", "blend"):
        a[n] = a[n].reshape(-1, DC, P).transpose(2, 0, 1)
    return {k: np.ascontiguousarray(v) for k, v in a.items()}


def kernel(**inputs):
    import concourse.bacc as bacc
    import numpy as np
    from concourse.bass_utils import run_bass_kernel_spmd

    arrays = layout(inputs)
    nc = bacc.Bacc("TRN2", target_bir_lowering=False, num_devices=1)
    A = {k: nc.dram_tensor(k, v.shape, mybir.dt.from_np(v.dtype), kind="ExternalInput").ap()
         for k, v in arrays.items()}
    out = nc.dram_tensor("out", (T, D), F32, kind="ExternalOutput").ap()
    build(nc, A, out)
    r = run_bass_kernel_spmd(nc, [arrays], core_ids=[0])
    return np.asarray(r.results[0]["out"]).reshape(B, S, D)
```

```python
from contextlib import ExitStack

import concourse.bass as bass
from concourse import mybir

ALU = mybir.AluOpType
ACT = mybir.ActivationFunctionType
AX = mybir.AxisListType
F32 = mybir.dt.float32
BF16 = mybir.dt.bfloat16
U8 = mybir.dt.uint8
I32 = mybir.dt.int32
U32 = mybir.dt.uint32

P = 128
B, S, D, H = 2, 1024, 256, 16
DH = D // H
T = B * S
DC = D // P
NT = S // P
HALF = 512
NH = S // HALF
QUAD = 4
NQ = H // QUAD
HB = P // QUAD
K_SPARSE = 32
LAMBDA_MAX, ALPHA, SPARSE_THRESHOLD = 10.0, 5.0, 1.0
SCALE = 1.0 / DH ** 0.5
SPANS = P // K_SPARSE
SPAN = S // SPANS
N_PROB = 8
PARTS = 3
Q_PART = [0, 1, 2, 0, 1, 0]
K_PART = [0, 0, 0, 1, 1, 2]
ROWS = DH * len(Q_PART)
ROWS_M = ROWS + PARTS
NEG = -1e30
HUGE = 1e30
HN = D // 4
ND = 2
E, TOPK = 8, 2
I_R, I_S = 4 * D, 8 * D
CAP = max(int(1.25 * T / E), 1)
SLOTS = E * CAP
PIECE = 256
PIECES_AT = (0, 1, 1, 1)
SLACK = (10, 3)
TURN = (9, 4)
POOL_HEADS = (0, 2)
STEPS_PER_COLUMN = 2

FAR = 1e5
LN_EPS = 1e-5
RMS_EPS = 1.1920928955078125e-07

CF = dict(ident=(0, P), sel_num=(P, 2 * P), sel_den=(3 * P, 2 * P), iota_e=(5 * P, E), slot_e=(5 * P + E, E))
CF_W = 5 * P + 2 * E
CB = dict(ident=(0, P), neg_qk=(P, P), neg_kq=(2 * P, P), before=(3 * P, P), ones=(4 * P, P), iota=(5 * P, P))
CB_W = 6 * P


class Sem:

    def __init__(self, handle):
        self.handle, self.value = handle, 0


class Queue:

    def __init__(self):
        self.items, self.seen = [], {}

    def add(self, fn, after, sem, step):
        waits = []
        for m in after:
            if m is not None and self.seen.get(m[0], 0) < m[1]:
                self.seen[m[0]] = m[1]
                waits = [w for w in waits if w[0] is not m[0]] + [m]
        mark = None
        if sem is not None:
            sem.value += step
            mark = (sem, sem.value)
        self.items.append((waits, fn, sem, step))
        return mark

    def emit(self, engine):
        for waits, fn, sem, step in self.items:
            for s, v in waits:
                engine.wait_ge(s.handle, v)
            ins = fn and fn(engine)
            if sem is not None:
                ins.then_inc(sem.handle, step)


class Ring:

    def __init__(self, bufs):
        self.bufs, self.users, self.n = bufs, [[] for _ in bufs], 0

    def take(self):
        i = self.n % len(self.bufs)
        self.n += 1
        users, self.users[i] = self.users[i], []
        return i, self.bufs[i], users

    def hold(self, i, *marks):
        self.users[i] += marks


def build(nc, A, out):
    ctx = ExitStack()
    with ctx:
        all_sems = []

        def sem(name):
            all_sems.append(Sem(ctx.enter_context(nc.semaphore(name))))
            return all_sems[-1]

        def sb(name, shape, dt=F32, scope=None):
            return (scope or ctx).enter_context(nc.sbuf_tensor("sb_" + name, shape, dt))

        def dram(name, shape, dt):
            return nc.dram_tensor(name, shape, dt, kind="Internal").ap()

        pe, dve, act, pool, sp = (Queue() for _ in range(5))

        def do(queue, fn, after=(), sem=None):
            return queue.add(fn, after, sem, 1)

        def dma(queue, dst, src, after=(), sem=None):
            return queue.add(lambda e: e.dma_start(dst, src), after, sem, 16)

        s_pe = {k: sem(f"pe_{k}") for k in (
            "count", "countT", "proj", "vproj", "max", "maxT", "score", "pv", "sel", "out",
            "mix", "tok", "hT", "logit", "pos", "xT", "gu", "down")}
        s_dve = {k: sem(f"dve_{k}") for k in (
            "index", "onehot", "flag", "bias", "weight", "split", "v", "rowmax", "maxpart",
            "weigh", "norm", "resid", "mix", "scan", "ln", "route", "act", "comb", "copy")}
        s_act = {k: sem(f"act_{k}") for k in (
            "flag", "count", "split", "exp", "o", "mrow", "y", "gate", "stat", "route", "copy", "silu")}
        s_pool = {k: sem(f"pool_{k}") for k in ("const", "zero", "weigh")}

        parts = dram("parts", [2, B, 2, PARTS, D, S], BF16)
        count_d = dram("count_qk", [NT, P, S], BF16)
        y_d = dram("y_prior", [B, DC, P, S], F32)
        countT_d = dram("count_kq", [NT, P, S], BF16)
        slots_in = dram("slots_in", [SLOTS, D], F32)
        slots_out = dram("slots_out", [SLOTS + 1, D], F32)

        wide = [ctx.enter_context(nc.psum_tensor(f"wide{i}", [P, 2 * HALF], F32)) for i in range(3)]
        bank = [ctx.enter_context(nc.psum_tensor(f"bank{i}", [P, HALF], F32)) for i in range(2)]
        score_ring = Ring(wide[:2])
        pv_ring = Ring(wide[2:])
        bank_ring = Ring(bank)

        cf = sb("const_f32", [P, CF_W])
        cb = sb("const_bf16", [P, CB_W], BF16)
        F = {k: cf[:, a:a + n] for k, (a, n) in CF.items()}
        C = {k: cb[:, a:a + n] for k, (a, n) in CB.items()}
        xT = sb("xT", [P, DC, T])
        weight = sb("weight", [P, NT, S])

        s_load = {}

        def load(name, dst, src, queue=None, after=()):
            if name not in s_load:
                s_load[name] = sem(f"load_{name}")
            return dma(queue or sp, dst, src, after, s_load[name])

        def chunks(ap):
            return ap.rearrange("(c p) m -> p c m", p=P)

        m_cb = load("cb", cb[:], A["const_bf16"])

        hT = weight[:, 0:DC * T // S].rearrange("p a t -> p (a t)").rearrange("p (c t) -> p c t", c=DC)
        pool_of_words = weight[:, DC * T // S:].rearrange("p a t -> p (a t)")
        carved = [0]

        def carve(*shape, rows=P):
            n = 1
            for k in shape:
                n *= k
            piece = pool_of_words[0:rows, carved[0]:carved[0] + n]
            carved[0] += n
            return piece.rearrange("p (a b) -> p a b", b=shape[1]) if len(shape) > 1 else piece

        w_g = carve(2 * DC, D)
        w_n1 = carve(DC, HN)
        w_n2 = carve(ND, P, rows=HN)
        w_soma, w_temp, w_out = (carve(DC, D) for _ in range(3))
        w_rt = carve(DC, E)
        ln_rows = carve(2, D)
        mcol = carve(3, DC)
        b_n1 = carve(1, rows=HN)
        b_n2 = carve(ND)
        blend = carve(ND, DC)
        taus = carve(1 + ND)
        logit = carve(B * NT, E)
        top8 = carve(B * NT, 8)
        best = carve(B * NT, 8).bitcast(U32)
        slot_map = carve(B * NT, E)
        assert carved[0] <= pool_of_words.shape[1]

        ph1 = ExitStack()

        def s1(name, shape, dt=F32):
            return sb(name, shape, dt, ph1)

        w1 = s1("w_prior", [P, DC, 3 * D])
        w2 = s1("w_causal", [P, DC, 3 * D])
        wo = s1("w_o", [P, DC, D])
        bcol = s1("bias_cols", [P, 6, DC])
        bv = s1("bias_v", [P, 2, D])
        spans = s1("span_iota", [P, SPANS * NT], BF16)
        flags = s1("flags", [P, 10, B])
        stack_q = s1("stack_q", [P, 3, QUAD, S], BF16)
        stack_k = s1("stack_k", [P, 3, QUAD, S], BF16)
        bias = s1("bias", [P, NT, S], BF16)
        prob = s1("prob", [P, N_PROB, S])
        v_aug = s1("v_aug", [P, NT, H, HB])
        o_raw = s1("o_raw", [P, 2, S])
        o_norm = s1("o_norm", [P, DC, S])
        tab = s1("tables", [P, 2, S], BF16)
        tab8 = s1("tables8", [P, 2, S], U8)
        junk = s1("junk", [P, 2, HALF], BF16)
        junk_ring = Ring([junk[:, i] for i in range(2)])
        lo16 = junk[:, 0, 0:SPAN]
        hi16 = junk[:, 1, 0:SPAN]
        rowmax = s1("rowmax", [P, 2, QUAD, NT, 2])
        mneg = s1("mneg", [P, 4, QUAD, NT])
        mpart = s1("mpart", [P, 2, NT, QUAD, PARTS], BF16)
        mrow = s1("mrow", [PARTS * QUAD, 1, S], BF16)

        idx_i = o_raw[:, 0, 0:SPAN].bitcast(I32)
        key_lo, key_hi = o_raw[:, 0, SPAN:2 * SPAN], o_raw[:, 0, 2 * SPAN:3 * SPAN]
        key, wrap = o_raw[:, 1, 0:SPAN], o_raw[:, 1, SPAN:2 * SPAN]
        listed = o_raw[:, 1, 2 * SPAN:3 * SPAN]
        msk_u = o_raw[:, 1, 3 * SPAN:3 * SPAN + SPAN // 4].bitcast(U8)
        m_idx = load("idx", idx_i, A["idx"])
        m_idx = load("idx", spans[:], A["span_iota"])
        m_idx = load("idx", msk_u, A["idx_mask"].bitcast(U8))
        m_cf = load("cf", cf[:], A["const_f32"])
        m_x = [load(f"x{b}", xT[:, :, b * S:(b + 1) * S], chunks(A["xT"])[:, :, b * S:(b + 1) * S],
                    after=[m_idx] if b else [])
               for b in range(B)]
        m_w1 = load("w1", w1[:], chunks(A["w_prior"]))
        load("small", bcol[:], A["bias_cols"], act)
        load("small", bv[:], A["bias_v"].partition_broadcast(P), act)
        m_small = load("small", flags[:, 0, :], A["u_prev"].partition_broadcast(P), act)
        m_w2 = load("w2", w2[:], chunks(A["w_causal"]))
        m_wo = load("wo", wo[:], chunks(A["w_o"]))

        m_ones = do(pool, lambda e: e.memset(v_aug[:, :, :, DH:HB], 1.0), (), s_pool["const"])
        for r in range(3):
            m_krows = do(pool, lambda e, r=r: e.memset(stack_k[ROWS:ROWS_M, r], 1.0),
                         [m_ones if r == 0 else m_krows], s_pool["const"])
        m_rowmax0 = do(pool, lambda e: e.memset(rowmax[:], -3e38), [m_krows], s_pool["const"])

        zeros = o_norm[:].rearrange("p c t -> p (c t)")
        m = do(pool, lambda e: e.memset(o_norm[:], 0.0), [m_rowmax0], s_pool["zero"])
        s_zero = sem("zero_slots")
        for r in range(0, SLOTS, P * S * DC // D):
            n = min(P * S * DC // D, SLOTS - r)
            dma(sp, slots_in[r:r + n, :].rearrange("(p k) n -> p (k n)", p=P), zeros[:, 0:n * D // P], [m], s_zero)
        m_zero = dma(sp, slots_out[SLOTS:SLOTS + 1, :], zeros[0:1, 0:D], [m], s_zero)

        fl = [flags[:, i, :] for i in range(10)]
        m = do(act, lambda e: e.activation(fl[1], fl[0], ACT.Exp, scale=-ALPHA), [m_small], s_act["flag"])
        sf = s_dve["flag"]
        m = do(dve, lambda e: e.tensor_scalar(fl[2], fl[1], LAMBDA_MAX, None, ALU.mult), [m], sf)
        m = do(dve, lambda e: e.tensor_scalar(fl[3], fl[2], SPARSE_THRESHOLD, None, ALU.is_ge), [m], sf)
        m = do(dve, lambda e: e.tensor_scalar(fl[4], fl[3], -1.0, 1.0, ALU.mult, ALU.add), [m], sf)
        m = do(dve, lambda e: e.tensor_scalar(fl[5], fl[3], NEG, None, ALU.mult), [m], sf)
        m = do(dve, lambda e: e.tensor_scalar(fl[2], fl[2], SPARSE_THRESHOLD, None, ALU.min), [m], sf)
        m = do(dve, lambda e: e.tensor_tensor(fl[7], fl[2], fl[4], ALU.mult), [m], sf)
        m = do(dve, lambda e: e.tensor_scalar(fl[6], fl[7], -1.0, None, ALU.mult), [m], sf)
        m = do(act, lambda e: e.activation(fl[1], fl[2], ACT.Exp, scale=-1.0), [m], s_act["flag"])
        m = do(dve, lambda e: e.tensor_tensor(fl[8], fl[1], fl[4], ALU.mult), [m], sf)
        m_flag = do(dve, lambda e: e.tensor_tensor(fl[9], fl[4], fl[8], ALU.subtract), [m], sf)

        si = s_dve["index"]
        m = do(dve, lambda e: e.tensor_copy(key, idx_i), [m_idx], si)
        m = do(dve, lambda e: e.tensor_scalar(wrap, key, 0.0, float(S), ALU.is_lt, ALU.mult), [m], si)
        m = do(dve, lambda e: e.tensor_tensor(key, key, wrap, ALU.add), [m], si)
        m = do(dve, lambda e: e.tensor_scalar(key, key, 0.0, float(S - 1), ALU.max, ALU.min), [m], si)
        m = do(dve, lambda e: e.tensor_scalar(key_hi, key, float(P), None, ALU.is_ge), [m], si)
        for n in range(2, NT):
            m = do(dve, lambda e, n=n: e.scalar_tensor_tensor(
                out=key_hi, in0=key, scalar=float(n * P), in1=key_hi, op0=ALU.is_ge, op1=ALU.add), [m], si)
        m = do(dve, lambda e: e.scalar_tensor_tensor(out=key_lo, in0=key_hi, scalar=-float(P), in1=key,
                                                     op0=ALU.mult, op1=ALU.add), [m], si)
        m = do(dve, lambda e: e.tensor_copy(listed, msk_u), [m], si)
        m = do(dve, lambda e: e.tensor_scalar(listed, listed, -float(NT), float(NT), ALU.mult, ALU.add), [m], si)
        m = do(dve, lambda e: e.tensor_tensor(key_hi, key_hi, listed, ALU.add), [m], si)
        m_lo = do(dve, lambda e: e.tensor_copy(lo16, key_lo), [m], si)
        m_hi = do(dve, lambda e: e.tensor_copy(hi16, key_hi), [m_lo], si)

        prob_ring = Ring([prob[:, i, :] for i in range(N_PROB)])
        counts = prob[:, 0:4, :].rearrange("p a b -> p (a b)").bitcast(BF16).rearrange("p (k q) -> p k q", k=NT)
        hot_hi = bias[:].rearrange("p a b -> p (a b)").rearrange("p (t c) -> p t c", c=SPANS * NT)
        GROUP = 32
        hot_ring = Ring([weight[:, 2 * i:2 * i + 2].rearrange("p a b -> p (a b)").bitcast(BF16)
                         .rearrange("p (t r) -> p t r", r=P) for i in range(NT // 2)])
        for g in range(SPAN // GROUP):
            ts = slice(g * GROUP, (g + 1) * GROUP)
            mh = do(dve, lambda e, ts=ts: e.tensor_tensor(
                hot_hi[:, ts], spans[:].unsqueeze(1).broadcast_to([P, GROUP, SPANS * NT]),
                hi16[:, ts].unsqueeze(2).broadcast_to([P, GROUP, SPANS * NT]), ALU.is_equal), [m_hi], s_dve["onehot"])
            k, hot, hfree = hot_ring.take()
            m = do(dve, lambda e, hot=hot, ts=ts: e.tensor_tensor(
                hot, C["iota"].unsqueeze(1).broadcast_to([P, GROUP, P]),
                lo16[:, ts].unsqueeze(2).broadcast_to([P, GROUP, P]), ALU.is_equal), [m_cb, m_lo, *hfree],
                s_dve["onehot"])
            i, acc, free = score_ring.take()
            for t in range(GROUP):
                mm = do(pe, lambda e, hot=hot, acc=acc, t=t, g=g: e.matmul(
                    acc[:, t * SPANS * NT:(t + 1) * SPANS * NT], hot[:, t], hot_hi[:, g * GROUP + t],
                    start=True, stop=True), [m, mh, *free], s_pe["count"] if t == GROUP - 1 else None)
            hot_ring.hold(k, mm)
            m_count = do(act, lambda e, acc=acc, g=g: e.activation(
                counts.rearrange("p k (s t) -> p s k t", s=SPANS)[:, :, :, g * GROUP:(g + 1) * GROUP],
                acc[:].rearrange("p (t s k) -> p s k t", s=SPANS, k=NT), ACT.Copy), [mm], s_act["count"])
            score_ring.hold(i, m_count)
        m_counted = mm
        s_cnt = [sem("count_store0"), sem("count_store1")]
        m_tables = [dma(sp, countT_d.rearrange("k p q -> p k q"), counts, [m_count], s_cnt[0])]

        s_store = [sem(f"parts_store{k}") for k in range(2)]
        idle = [stack_q[:, 2].rearrange("p h t -> p (h t)"),
                prob[:, 4:6].rearrange("p a t -> p (a t)").bitcast(BF16)]
        start_sets = [(z[:, 0:2 * HALF].bitcast(F32), *(z[:, (2 + j) * HALF:(3 + j) * HALF] for j in range(PARTS)))
                      for z in idle]
        tabs = tab[:].rearrange("p a t -> p (a t)")
        tabs8 = tab8[:].rearrange("p a t -> p (a t)").bitcast(BF16)
        late_sets = [(w1[:, 0, 0:HALF], *(tabs[:, j * HALF:(j + 1) * HALF] for j in range(PARTS))),
                     (w1[:, 1, 0:HALF], tabs[:, 3 * HALF:4 * HALF], tabs8[:, 0:HALF], tabs8[:, HALF:2 * HALF])]
        middle_sets = [(o_norm[:, 0, k * HALF:(k + 1) * HALF], *late_sets[k][1:]) for k in range(2)]
        split_ring = Ring(start_sets)
        middle_ring = Ring(middle_sets)
        late_ring = Ring(late_sets)

        def project_qk(att, b, src, ready, w, q_col, k_col, ring):
            steps, stored = [], {}

            def chain(qk, col, scale, mc, h):
                st = {}

                def product():
                    cols = slice(h * HALF, (h + 1) * HALF)
                    i, acc, free = bank_ring.take()
                    for c in range(DC):
                        mm = do(pe, lambda e, c=c, o=col * D + mc * P: e.matmul(
                            acc[:], w[:, c, o:o + P], src[:, c, cols], start=(c == 0), stop=(c == DC - 1)),
                            [*ready(), *free], s_pe["proj"] if c == DC - 1 else None)
                    st["k"], (val, hi, mid, lo), sfree = ring.take()
                    m0 = do(dve, lambda e: e.tensor_scalar(val, acc[:], bcol[:, 2 * att + qk, mc:mc + 1], scale,
                                                           ALU.add, ALU.mult), [mm, m_small, *sfree], s_dve["split"])
                    bank_ring.hold(i, m0)
                    st["hi"] = do(act, lambda e: e.activation(hi, val, ACT.Copy), [m0], s_act["split"])
                    st["bufs"] = (val, hi, mid, lo)

                def second():
                    val, hi, mid, lo = st["bufs"]
                    m = do(dve, lambda e: e.tensor_tensor(val, val, hi, ALU.subtract), [st["hi"]], s_dve["split"])
                    st["mid"] = do(act, lambda e: e.activation(mid, val, ACT.Copy), [m], s_act["split"])

                def third():
                    val, hi, mid, lo = st["bufs"]
                    k = st["k"]
                    m = do(dve, lambda e: e.tensor_tensor(lo, val, mid, ALU.subtract), [st["mid"]], s_dve["split"])
                    for part, (t, mk) in enumerate(((hi, st["hi"]), (mid, st["mid"]), (lo, m))):
                        ms = dma(sp, parts[att, b, qk, part, mc * P:(mc + 1) * P, h * HALF:(h + 1) * HALF], t, [mk],
                                 s_store[k])
                    ring.hold(k, ms)
                    stored[k] = ms

                return [product, second, third]

            chains = [chain(qk, col, scale, mc, h) for qk, col, scale in ((0, q_col, SCALE), (1, k_col, 1.0))
                      for mc in range(DC) for h in range(NH)]
            for one, other in zip(chains[0::2], chains[1::2]):
                steps += [f for pair in zip(one, other) for f in pair]
            return steps, stored

        v_ring = Ring([v_aug])

        def project_v(att, src, ready, w, col):
            _, _, vfree = v_ring.take()
            marks = {}

            def tile(kt):
                i, bk, free = bank_ring.take()
                for c in range(DC):
                    mm = do(pe, lambda e, c=c: e.matmul(
                        bk[:, 0:D], src(c)[:, kt * P:(kt + 1) * P], w[:, c, col * D:(col + 1) * D],
                        start=(c == 0), stop=(c == DC - 1)), [*ready, *free],
                        s_pe["vproj"] if c == DC - 1 else None)
                m = do(dve, lambda e: e.tensor_tensor(
                    v_aug[:, kt, :, 0:DH], bk[:, 0:D].rearrange("p (h d) -> p h d", h=H),
                    bv[:, att, :].rearrange("p (h d) -> p h d", h=H), ALU.add),
                    [mm, m_small, m_ones, *vfree], s_dve["v"])
                bank_ring.hold(i, m)
                marks[kt], marks["read"] = m, mm

            return [lambda kt=kt: tile(kt) for kt in range(NT)], marks

        s_tab = [sem(f"load_tables{i}") for i in range(2)]
        tab_ring = Ring([(tab[:, i, :], tab8[:, i, :]) for i in range(2)])
        spare = o_norm[:, 1, :]
        tab_w_ring = Ring([(spare[:, 0:HALF].bitcast(BF16), spare[:, HALF:HALF + S // 4].bitcast(U8))])
        s_tab_w = [sem("load_weight_tables")]
        count_ring = Ring([prob[:, 6, i * HALF:(i + 1) * HALF].bitcast(BF16) for i in range(2)])

        def key_bias(b, qt, free_bias, mark):
            i, (t, t8), free = tab_ring.take()
            m_t8 = dma(sp, t8, A["prior"].bitcast(U8)[qt * P:(qt + 1) * P, :], free, s_tab[i])
            if b == 0:
                bi, bk, bfree = score_ring.take()
                turned = bk[:, 0:HALF].bitcast(BF16)
                for kb in range(NT):
                    m_n = do(pe, lambda e, kb=kb: e.transpose(
                        turned[:, kb * P:(kb + 1) * P], counts[:, kb, qt * P:(qt + 1) * P], C["ident"]),
                        [m_count, *bfree], s_pe["countT"])
                c, cnt, cfree = count_ring.take()
                mc = do(act, lambda e: e.activation(cnt, turned, ACT.Copy), [m_n, *cfree], s_act["count"])
                score_ring.hold(bi, mc)
                m_st = dma(sp, count_d[qt], cnt, [mc], s_cnt[1])
                count_ring.hold(c, m_st)
                n, m_n = cnt, mc
                if qt == NT - 1:
                    m_tables.append(m_st)
            else:
                n = t
                m_n = m_t8 = dma(sp, t, count_d[qt], m_tables, s_tab[i])
            yield
            o = bias[:, qt, :]
            m1 = do(act, lambda e: e.activation(o, t8, ACT.Identity, bias=fl[6][:, b:b + 1], scale=fl[7][:, b:b + 1]),
                    [m_t8, m_flag, *free_bias], s_act["count"])
            m = do(dve, lambda e: e.tensor_scalar(t, n, 0.0, fl[5][:, b:b + 1], ALU.is_equal, ALU.mult),
                   [m_n, m_flag, *free], s_dve["bias"])
            m = do(dve, lambda e: e.tensor_tensor(o, o, t, ALU.add), [m, m1], s_dve["bias"])
            if b == 0:
                count_ring.hold(c, m)
            tab_ring.hold(i, m)
            mark[qt] = m

        def key_weight(b, kt, free_weight, mark):
            ring, sems = (tab_ring, s_tab) if b == 0 else (tab_w_ring, s_tab_w)
            i, (t, t8), free = ring.take()
            m_t = dma(sp, t8, A["priorT"].bitcast(U8)[kt * P:(kt + 1) * P, :], free, sems[i])
            if b == 0:
                n, m_n = counts[:, kt, :], m_count
            else:
                n = t
                m_n = m_t = dma(sp, t, countT_d[kt], m_tables, sems[i])
            yield
            o = weight[:, kt, :]
            m1 = do(act, lambda e: e.activation(o, t8, ACT.Identity, bias=fl[8][:, b:b + 1], scale=fl[9][:, b:b + 1]),
                    [m_t, m_flag, *free_weight], s_act["count"])
            m = do(dve, lambda e: e.scalar_tensor_tensor(out=o, in0=n, scalar=fl[3][:, b:b + 1], in1=o,
                                                         op0=ALU.mult, op1=ALU.add), [m1, m_n], s_dve["weight"])
            ring.hold(i, m)
            mark[kt] = m

        stack_ring = Ring([0, 1, 2])
        s_stack = [sem(f"load_stack{r}") for r in range(3)]
        s_mrow = sem("store_mrow")
        rowmax_ring = Ring([0, 1])
        mrow_ring = Ring([0])
        mpart_ring = Ring([0, 1])
        o_ring = Ring([0, 1])

        def load_stack(att, b, q, stored):
            r, _, free = stack_ring.take()
            for qk, (dst, which) in enumerate(((stack_q, Q_PART), (stack_k, K_PART))):
                for blk, part in enumerate(which):
                    src = parts[att, b, qk, part, q * QUAD * DH:(q + 1) * QUAD * DH, :]
                    m = dma(sp, dst[blk * DH:(blk + 1) * DH, r], src.rearrange("(h d) t -> d h t", d=DH),
                            [*stored, *free], s_stack[r])
            return r, m

        def max_units(att, q, r, loaded, m_bias):
            causal = att == 1
            mi, _, free_mx = rowmax_ring.take()
            m_last = {}

            def unit(h, qt, half):
                lo, hi = half * HALF, min((half + 1) * HALF, (qt + 1) * P if causal else S)
                diag = causal and hi == (qt + 1) * P
                i, bk, free = bank_ring.take()
                mm = do(pe, lambda e: e.matmul(
                    bk[:, 0:hi - lo], stack_q[0:ROWS, r, h, qt * P:(qt + 1) * P], stack_k[0:ROWS, r, h, lo:hi],
                    start=True, stop=not diag), [loaded, *free], None if diag else s_pe["max"])
                if diag:
                    mm = do(pe, lambda e: e.matmul(bk[:, hi - lo - P:hi - lo], C["ident"], C["neg_qk"],
                                                   start=False, stop=True), [m_cb], s_pe["max"])
                acc = rowmax[:, mi, h, qt, half:half + 1]
                if causal:
                    m = do(dve, lambda e: e.tensor_reduce(acc, bk[:, 0:hi - lo], AX.X, ALU.max),
                           [mm, *free_mx, m_rowmax0], s_dve["rowmax"])
                else:
                    ji, scrap, jfree = junk_ring.take()
                    m = do(dve, lambda e: e.tensor_tensor_reduce(
                        out=scrap, in0=bk[:], in1=bias[:, qt, lo:hi], scale=1.0, scalar=-3e38,
                        op0=ALU.add, op1=ALU.max, accum_out=acc), [mm, m_bias[qt], *free_mx, m_rowmax0, *jfree],
                        s_dve["rowmax"])
                    junk_ring.hold(ji, m)
                bank_ring.hold(i, m)
                m_last["max"] = m

            def finish():
                sm = s_dve["maxpart"]
                pi, _, pfree = mpart_ring.take()
                top, neg, rem, rem2 = (mneg[:, k] for k in range(4))

                def part(k):
                    return mpart[:, pi, :, :, k].rearrange("p n h -> p h n")

                if causal:
                    m = do(dve, lambda e: e.tensor_reduce(
                        top[:, :, 0:NT // 2], rowmax[:, mi, :, 0:NT // 2, 0:1], AX.X, ALU.max),
                        [m_last["max"], *pfree], sm)
                    m = do(dve, lambda e: e.tensor_reduce(
                        top[:, :, NT // 2:NT], rowmax[:, mi, :, NT // 2:NT, :], AX.X, ALU.max), [m], sm)
                else:
                    m = do(dve, lambda e: e.tensor_reduce(top, rowmax[:, mi], AX.X, ALU.max),
                           [m_last["max"], *pfree], sm)
                rowmax_ring.hold(mi, m)
                m = do(dve, lambda e: e.tensor_scalar(neg, top, -1.0, None, ALU.mult), [m], sm)
                m = do(dve, lambda e: e.tensor_copy(part(0), neg), [m], sm)
                m = do(dve, lambda e: e.tensor_tensor(rem, neg, part(0), ALU.subtract), [m], sm)
                m = do(dve, lambda e: e.tensor_copy(part(1), rem), [m], sm)
                m = do(dve, lambda e: e.tensor_tensor(rem2, rem, part(1), ALU.subtract), [m], sm)
                m = do(dve, lambda e: e.tensor_copy(part(2), rem2), [m], sm)
                m_last["parts"] = pi, m

            def turn():
                pi, m = m_last["parts"]
                i, bk, free = bank_ring.take()
                rows = bk[0:PARTS * QUAD].bitcast(BF16)
                for qt in range(NT):
                    mm = do(pe, lambda e, qt=qt: e.transpose(
                        rows[:, qt * P:(qt + 1) * P], mpart[:, pi, qt].rearrange("p h k -> p (h k)"), C["ident"]),
                        [m, *free], s_pe["maxT"] if qt == NT - 1 else None)
                mpart_ring.hold(pi, mm)
                ri, _, rfree = mrow_ring.take()
                m = do(act, lambda e: e.activation(mrow[:, ri], rows, ACT.Copy), [mm, *rfree], s_act["mrow"])
                bank_ring.hold(i, m)
                for h in range(QUAD):
                    md = dma(sp, stack_q[ROWS:ROWS_M, r, h], mrow[h * PARTS:(h + 1) * PARTS, ri], [m], s_mrow)
                mrow_ring.hold(ri, md)
                m_last["rows"] = md

            steps = []
            for h in range(QUAD):
                for qt in range(NT):
                    for half in range(NH):
                        if not causal or half * HALF < (qt + 1) * P:
                            steps.append(lambda h=h, qt=qt, half=half: unit(h, qt, half))
            steps += [finish, turn]
            return steps, m_last

        def xs(b):
            return xT[:, :, b * S:(b + 1) * S]

        def weave(first, then):
            total = [(k / max(len(first), 1) * 0.9, 0, f) for k, f in enumerate(first)]
            total += [(k / max(len(then), 1), 1, f) for k, f in enumerate(then)]
            return [f for _, _, f in sorted(total, key=lambda z: z[:2])]

        y1 = o_raw
        s_y = sem("y_store")
        s_yload = [sem(f"y_load{i}") for i in range(2)]
        ATTENTIONS = [(0, 0), (0, 1), (1, 0), (1, 1)]
        JOBS = [(att, b, q) for att, b in ATTENTIONS for q in range(NQ)]
        m_bias, m_weight = [{}, {}], [{}, {}]
        m_norm, m_out = {}, {}
        qk_stored = {}
        m_resid = [None, None]

        def normalise_steps(c, o_pair, key):
            norm_free = [m_zero, *m_out.values(), (s_dve["split"], s_dve["split"].value),
                         (s_act["split"], s_act["split"].value), *m_weight[1].values()]

            def step(half):
                cols = slice(half * HALF, (half + 1) * HALF)
                outs = []
                for which in ("sel_den", "sel_num"):
                    i, bk, free = bank_ring.take()
                    for par, (oi, m) in enumerate(o_pair):
                        mm = do(pe, lambda e, bk=bk, par=par, oi=oi, which=which: e.matmul(
                            bk[:], F[which][:, par * P:(par + 1) * P], o_raw[:, oi, cols],
                            start=(par == 0), stop=(par == 1)), [m, m_cf, *free],
                            s_pe["sel"] if par else None)
                    outs.append((i, bk, mm))
                (i0, den, md), (i1, num, mn) = outs
                on = o_norm[:, c, cols]
                m = do(dve, lambda e: e.reciprocal(on, den[:]), [md, *norm_free], s_dve["norm"])
                bank_ring.hold(i0, m)
                m = do(dve, lambda e: e.tensor_tensor(on, on, num[:], ALU.mult), [m, mn], s_dve["norm"])
                bank_ring.hold(i1, m)
                for oi, _ in o_pair:
                    o_ring.hold(oi, mn)
                m_norm[key] = m

            return [lambda half=half: step(half) for half in range(NH)]

        def project_out(w, key, mc, half):
            i, acc, free = bank_ring.take()
            for c in range(DC):
                mm = do(pe, lambda e, c=c: e.matmul(
                    acc[:], w[:, c, mc * P:(mc + 1) * P], o_norm[:, c, half * HALF:(half + 1) * HALF],
                    start=(c == 0), stop=(c == DC - 1)), [m_norm[key], m_wo, *free],
                    s_pe["out"] if c == DC - 1 else None)
            m_out[key] = mm
            return i, acc, mm

        def between(b):
            state = {}

            def y_step(mc, half):
                i, acc, mm = project_out(wo, (0, b), mc, half)
                if "free" not in state:
                    state["free"] = [u for us in o_ring.users for u in us]
                m = do(act, lambda e: e.activation(
                    y1[:, mc, half * HALF:(half + 1) * HALF], acc[:], ACT.Identity, bias=bcol[:, 4, mc:mc + 1]),
                    [mm, *state["free"]], s_act["y"])
                bank_ring.hold(i, m)
                state["y"] = m
                if half == NH - 1:
                    state["store"] = dma(sp, y_d[b, mc], y1[:, mc, :], [m], s_y)

            ys = [lambda mc=mc, half=half: y_step(mc, half) for mc in range(DC) for half in range(NH)]
            for k in range(2):
                late_ring.hold(k, (s_pe["proj"], s_pe["proj"].value), *m_weight[1].values())
            steps, qk_stored[1, b] = project_qk(1, b, y1, lambda: [state["y"], m_w2], w2, 1, 0, late_ring)

            def release():
                for i in range(2):
                    o_ring.hold(i, state["store"], (s_pe["proj"], s_pe["proj"].value))

            m_ystored[b] = state
            return ys + steps + [release]

        m_ystored = {}

        def add_residual(b):
            def step(mc, half):
                i, acc, mm = project_out(wo, (1, b), mc, half)
                o = xs(b)[:, mc, half * HALF:(half + 1) * HALF]
                m = do(dve, lambda e: e.scalar_tensor_tensor(
                    out=o, in0=acc[:], scalar=bcol[:, 5, mc:mc + 1], in1=o, op0=ALU.add, op1=ALU.add),
                    [mm], s_dve["resid"])
                bank_ring.hold(i, m)
                m_resid[b] = m

            return [lambda mc=mc, half=half: step(mc, half) for mc in range(DC) for half in range(NH)]

        def load_quad(n):
            att, b, q = JOBS[n]
            return load_stack(att, b, q, list(qk_stored[att, b].values()))

        def values_of(att, b):
            if att == 0:
                return project_v(0, lambda c: xs(b)[:, c], [m_x[b], m_w1], w1, 2)
            bufs = [prob_ring.take() for _ in range(DC)]
            loads = [dma(sp, buf, y_d[b, c], [m_ystored[b]["store"], *free], s_yload[c])
                     for c, (_, buf, free) in enumerate(bufs)]
            steps, marks = project_v(1, lambda c: bufs[c][1], [*loads, m_w2], w2, 2)

            def last():
                steps[-1]()
                for k, _, _ in bufs:
                    prob_ring.hold(k, marks["read"])

            return steps[:-1] + [last], marks

        steps, qk_stored[0, 0] = project_qk(0, 0, xs(0), lambda: [m_x[0], m_w1], w1, 0, 1, split_ring)
        for f in steps:
            f()
        quads = {0: load_quad(0)}
        for i in range(2):
            junk_ring.hold(i, m_hi, (s_dve["onehot"], s_dve["onehot"].value))
        max_steps, m_max = max_units(0, 0, *quads[0], m_bias[0])
        for t in range(NT):
            for _ in key_bias(0, t, [m_counted], m_bias[0]):
                pass
            for _ in range(NH):
                max_steps.pop(0)()
        quads[1] = load_quad(1)
        for k, f in enumerate(max_steps):
            f()
            if k % 6 == 5 and len(m_weight[0]) < NT:
                for _ in key_weight(0, len(m_weight[0]), [m_counted], m_weight[0]):
                    pass
        for i in range(N_PROB):
            prob_ring.hold(i, *m_tables, *m_weight[0].values(), *[u for us in split_ring.users for u in us])
        stack_ring.hold(2, *[u for us in split_ring.users for u in us])

        for k in range(2):
            middle_ring.hold(k, m_zero, *m_weight[0].values())
        one = v_aug[:, 0, 0, DH:DH + 1]
        extras, qk_stored[0, 1] = project_qk(0, 1, xs(1), lambda: [m_x[1], m_w1], w1, 0, 1, middle_ring)
        o_pair = []
        for n, (att, b, q) in enumerate(JOBS):
            causal = att == 1
            r, loaded = quads[n]
            m_rows = m_max["rows"]
            next_weights = (att, b, q) == (0, 0, NQ - 1)
            if next_weights:
                done_max = (s_dve["rowmax"], s_dve["rowmax"].value)
                tiles = [key_bias(1, t, [done_max], m_bias[1]) for t in range(NT)]
                for t in range(2):
                    next(tiles[t])
            if n + 2 < len(JOBS):
                quads[n + 2] = load_quad(n + 2)
            if q == 0:
                v_steps, m_v = values_of(att, b)
            steps = []
            if n + 1 < len(JOBS):
                steps, m_max = max_units(JOBS[n + 1][0], JOBS[n + 1][2], *quads[n + 1], m_bias[JOBS[n + 1][1]])
            if next_weights:
                maxima, steps = steps, []
                for t in range(NT):
                    steps.append(lambda t=t: next(tiles[t], None))
                    if t + 2 < NT:
                        steps.append(lambda t=t: next(tiles[t + 2]))
                    steps += maxima[NH * t:NH * (t + 1)]
                steps += maxima[NH * NT:]
                tab_w_ring.hold(0, (s_dve["norm"], s_dve["norm"].value), m_zero, *m_out.values())
            steps = weave(extras, steps)
            extras = []
            turn = steps.pop() if n + 1 < len(JOBS) else None
            n_steps, done, total = len(steps), 0, QUAD * NT - (SLACK[0] if causal else SLACK[1])
            _, pv, pvfree = pv_ring.take()

            def values(kt, ps):
                def step(lo, hi, end):
                    new, last = kt == 0 and lo % HALF == 0, kt == (hi // P - 1 if causal else NT - 1)
                    for g, (i, p, m) in enumerate(ps):
                        mm = do(pe, lambda e, g=g, p=p, lo=lo, hi=hi, new=new, last=last, q=q, pv=pv: e.matmul(
                            pv[g * HB:(g + 1) * HB, lo:hi], v_aug[:, kt, q * QUAD + g, :], p[:, lo:hi],
                            start=new, stop=last, skip_group_check=True), [m, m_v[kt], *pvfree],
                            s_pe["pv"] if g == QUAD - 1 else None)
                    if end:
                        for i, _, _ in ps:
                            prob_ring.hold(i, mm)
                    return mm

                first = kt * P if causal else 0
                return [lambda lo=lo: step(max(lo, first), lo + PIECE, lo + PIECE == S)
                        for lo in range(0, S, PIECE) if first < lo + PIECE]

            def weigh(kt, p, m):
                return do(dve, lambda e: e.scalar_tensor_tensor(
                    out=p, in0=p, scalar=HUGE, in1=weight[:, kt, :], op0=ALU.min, op1=ALU.mult),
                    [m, m_weight[b][kt]], s_dve["weigh"])

            waiting, ps, fresh, new, late_weight = [], [], None, None, None
            for u in range(QUAD * NT + 1):
                kt, g = divmod(u, QUAD)
                for _ in range(2 if u else 0):
                    if v_steps:
                        v_steps.pop(0)()
                while waiting and g == 0:
                    mm = waiting.pop(0)()
                if u < QUAD * NT:
                    first = kt * P if causal else 0
                    i, sc, free = score_ring.take()
                    for half in range(NH):
                        lo, hi = max(half * HALF, first), (half + 1) * HALF
                        if lo >= hi:
                            continue
                        diag = causal and lo == first
                        mm = do(pe, lambda e, sc=sc, lo=lo, hi=hi, g=g, kt=kt, diag=diag, r=r: e.matmul(
                            sc[:, lo:hi], stack_k[0:ROWS_M, r, g, kt * P:(kt + 1) * P],
                            stack_q[0:ROWS_M, r, g, lo:hi], start=True, stop=not diag),
                            [m_rows, m_krows, loaded, *free], s_pe["score"])
                        if diag:
                            mm = do(pe, lambda e, sc=sc, lo=lo: e.matmul(
                                sc[:, lo:lo + P], C["ident"], C["neg_kq"], start=False, stop=True),
                                [], s_pe["score"])
                    k, p, pfree = prob_ring.take()
                    to_pool = not causal and g in POOL_HEADS
                    if to_pool:
                        m = do(act, lambda e, p=p, sc=sc: e.activation(p, sc[:], ACT.Relu, scale=-1.0, bias=one),
                               [mm, m_ones, *pfree], s_act["exp"])
                        score_ring.hold(i, m)
                        m = do(act, lambda e, p=p: e.activation(p, p, ACT.Exp, scale=-1.0, bias=one), [m],
                               s_act["exp"])
                        m = do(pool, lambda e, p=p, kt=kt: e.tensor_tensor(p, p, weight[:, kt, :], ALU.mult),
                               [m, m_weight[b][kt]], s_pool["weigh"])
                    else:
                        m = do(act, lambda e, p=p, sc=sc, first=first: e.activation(
                            p[:, first:S], sc[:, first:S], ACT.Exp), [mm, *pfree], s_act["exp"])
                        score_ring.hold(i, m)
                    new = (kt, k, p, m, to_pool)
                due = (u + 1) * n_steps // total
                while done < min(due, n_steps):
                    steps[done]()
                    done += 1
                if fresh:
                    kt_f, k, p, m, weighed = fresh
                    if not causal and not weighed:
                        m = weigh(kt_f, p, m)
                    ps.append((k, p, m))
                    if len(ps) == QUAD:
                        ready, waiting, ps = ps, waiting + values(kt_f, ps), []
                        if next_weights:
                            late_weight = key_weight(1, kt_f, [m for _, _, m in ready], m_weight[1])
                            next(late_weight)
                fresh = new
                if next_weights and late_weight and (g == 3 or u == QUAD * NT):
                    next(late_weight, None)
                    late_weight = None
                if turn and u == QUAD * NT - (TURN[0] if causal else TURN[1]):
                    turn()
                for _ in range(PIECES_AT[g] if u < QUAD * NT else len(waiting)):
                    if waiting:
                        mm = waiting.pop(0)()
            stack_ring.hold(r, mm)
            oi, _, ofree = o_ring.take()
            m = do(act, lambda e, oi=oi, pv=pv: e.activation(o_raw[:, oi], pv[:], ACT.Copy), [mm, *ofree], s_act["o"])
            pv_ring.hold(0, m)
            o_pair.append((oi, m))
            if len(o_pair) == 2:
                extras += normalise_steps(q // 2, o_pair, (att, b))
                o_pair = []
            if (att, b, q) == (1, 0, 0):
                weights_read = [(s_dve["weigh"], s_dve["weigh"].value), (s_pool["weigh"], s_pool["weigh"].value)]
                load("mix", w_g[:], chunks(A["w_g"]), after=weights_read)
                load("mix", w_n1[:], chunks(A["w_n1"]))
                load("mix", w_n2[:], A["w_n2"])
                load("mix", w_soma[:], chunks(A["w_soma"]))
                load("mix", w_temp[:], chunks(A["w_temp"]))
                load("mix", w_out[:], chunks(A["w_out"]))
                load("mix", w_rt[:], chunks(A["w_router"]))
                load("mix", mcol[:], A["mix_cols"])
                load("mix", b_n1[:], A["b_n1"])
                load("mix", blend[:], A["blend"])
                load("mix", ln_rows[:], A["ln_rows"].partition_broadcast(P))
                load("mix", b_n2[:], A["b_n2"].partition_broadcast(P))
                m_mw = load("mix", taus[:], A["taus"].partition_broadcast(P))
            if (att, b, q) == (1, 0, 1):
                m_wo = load("w_causal_out", wo[:], chunks(A["w_proj"]), after=[m_out[0, 1]])
            if q == NQ - 1:
                v_ring.hold(0, mm)
                extras += add_residual(b) if causal else between(b)
        for f in extras:
            f()
        ph1.close()
        end1 = [(s, s.value) for s in all_sems if s.value]
        ph2 = ExitStack()

        def s2(name, shape, dt=F32):
            return sb(name, shape, dt, ph2)

        tiny = s2("tiny", [P, 8, 8])
        wsg = s2("sg", [P, DC, I_S])
        wsu = s2("su", [P, DC, I_S])
        wsd = s2("sd", [P, I_S // P, D])
        h_tok = s2("h_tok", [P, B * NT, D])
        y = h_tok
        big = s2("big", [P, 15 * S])

        def big_at(k, n):
            return big[:, k * S:(k + n) * S]

        ctxT, gated, tr0, tr1, soma, gate = (
            big_at(2 * k, 2).rearrange("p (c t) -> p c t", c=DC) for k in range(6))
        mod = big_at(12, 2).rearrange("p (c t) -> p c t", c=ND)
        h1 = big_at(14, 1)[0:HN]
        stats = s2("stats", [P, 4, 6])
        mean_var = s2("mean_var", [P, B * NT, 2])
        rstd = s2("rstd", [P, B * NT])
        ssq = s2("ssq", [P, B * NT])
        rms = s2("rms", [P, B * NT])
        best_f = s2("best_f", [P, B * NT, TOPK])
        lmax = s2("lmax", [P, B * NT])
        pick = s2("pick", [P, TOPK, B * NT, E])
        mask = s2("mask", [P, B * NT, E], BF16)
        before = s2("before", [P, B * NT + 1, E], BF16)
        far = s2("far", [P, B * NT, E])
        slot = s2("slot", [P, TOPK, B * NT])
        slot_w = s2("slot_w", [P, TOPK, B * NT], U32)
        slot_r = s2("slot_r", [P, TOPK, B * NT], U32)
        gain = s2("gain", [P, TOPK, B * NT])
        gsum = s2("gsum", [P, B * NT])
        sil = s2("sil", [P, 2, HALF])
        act_s = s2("act_s", [P, 3, HALF])
        xg = s2("xg", [P, 2, 3, D])
        xgT = s2("xgT", [P, 2, DC, CAP])
        act_e = big_at(12, 3)[:, 0:I_R // P * CAP].rearrange("p (i n) -> p i n", n=CAP)
        e_out = s2("e_out", [P, 2, 3, D])
        got = [w[:, c] for w in (w_soma, w_temp, w_g) for c in range(w.shape[1])]

        m_sg = load("sg", wsg[:], chunks(A["sg"]), after=end1)
        m_su = load("su", wsu[:], chunks(A["su"]))
        m_sd = load("sd", wsd[:], chunks(A["sd"]))

        sx = s_dve["mix"]
        alpha, ex, bmax, bw, bsum = (tiny[:, k] for k in range(5))
        m = do(act, lambda e: e.activation(ex[:, 0:3], taus[:], ACT.Exp), [m_mw, *end1], s_act["gate"])
        m = do(dve, lambda e: e.tensor_scalar(ex[:, 0:3], ex[:, 0:3], 1.0, None, ALU.add), [m, *end1], sx)
        m_alpha = do(dve, lambda e: e.reciprocal(alpha[:, 0:3], ex[:, 0:3]), [m], sx)
        m = do(dve, lambda e: e.tensor_tensor(bmax[:, 0:DC], blend[:, 0], blend[:, 1], ALU.max), [m_mw], sx)
        for d in range(ND):
            m = do(dve, lambda e, d=d: e.tensor_tensor(bw[:, d * DC:(d + 1) * DC], blend[:, d], bmax[:, 0:DC],
                                                       ALU.subtract), [m], sx)
        m = do(act, lambda e: e.activation(bw[:, 0:4], bw[:, 0:4], ACT.Exp), [m], s_act["gate"])
        m = do(dve, lambda e: e.tensor_tensor(bsum[:, 0:DC], bw[:, 0:DC], bw[:, DC:2 * DC], ALU.add), [m], sx)
        m = do(dve, lambda e: e.reciprocal(bmax[:, 0:DC], bsum[:, 0:DC]), [m], sx)
        for d in range(ND):
            m_bw = do(dve, lambda e, d=d: e.tensor_tensor(bw[:, d * DC:(d + 1) * DC], bw[:, d * DC:(d + 1) * DC],
                                                          bmax[:, 0:DC], ALU.mult), [m], sx)
            m = m_bw

        m_before = do(dve, lambda e: e.memset(before[:, 0, :], 0.0), [], s_dve["route"])

        def products(K, wt, srcs, after, use, rows=P):
            for h in range(NH):
                cols = slice(h * HALF, (h + 1) * HALF)
                i, acc, free = bank_ring.take()
                for k in range(K):
                    mm = do(pe, lambda e, k=k, acc=acc, cols=cols: e.matmul(
                        acc[0:rows], wt(k), srcs(k)[:, cols], start=(k == 0), stop=(k == K - 1)),
                        [*after, *free], s_pe["mix"] if k == K - 1 else None)
                m = use(cols, acc, mm)
                bank_ring.hold(i, m)
                yield
            return m

        def feature_cols(w, mc):
            return lambda k: w[:, k, mc * P:(mc + 1) * P]

        mix_free = []

        def mix(b):
            x = xs(b)
            sa, sd_ = s_act["gate"], s_dve["mix"]
            ready = [m_resid[b], m_mw]

            def activate(dst, fn, bias_, extra=()):
                return lambda cols, acc, mm: do(act, lambda e: e.activation(
                    dst[:, cols], acc[0:dst.shape[0]], fn, bias=bias_), [mm, *extra], sa)

            m_ctx = [do(dve, lambda e, c=c: e.tensor_tensor_scan(
                ctxT[:, c], alpha[:, 0:1].broadcast_to([P, S]), x[:, c], 0.0, ALU.mult, ALU.add),
                [*ready, m_alpha, *mix_free], s_dve["scan"]) for c in range(DC)][-1]
            m_h1 = yield from products(DC, lambda k: w_n1[:, k], lambda k: x[:, k], ready,
                                       activate(h1, ACT.Gelu, b_n1[:], mix_free), HN)
            for d in range(ND):
                m_mod = yield from products(1, lambda k, d=d: w_n2[:, d], lambda k: h1, [m_h1],
                                            activate(mod[:, d], ACT.Sigmoid, b_n2[:, d:d + 1]))
            m_gated = []
            for mc in range(DC):
                m = yield from products(2 * DC, feature_cols(w_g, mc),
                                        lambda k: x[:, k] if k < DC else ctxT[:, k - DC], [*ready, m_ctx],
                                        activate(gate[:, mc], ACT.Sigmoid, mcol[:, 0, mc:mc + 1]))
                m_gated.append(do(dve, lambda e, mc=mc: e.tensor_tensor(gated[:, mc], x[:, mc], gate[:, mc],
                                                                        ALU.mult), [m], sd_))
            m_temporal = []
            for c in range(DC):
                for d, tr in enumerate((tr0, tr1)):
                    m = do(dve, lambda e, c=c, d=d, tr=tr: e.scalar_tensor_tensor(
                        out=tr[:, c], in0=mod[:, d], scalar=0.5, in1=gated[:, c], op0=ALU.add, op1=ALU.mult),
                        [m_mod, m_gated[c]], sd_)
                    m = do(dve, lambda e, c=c, d=d, tr=tr: e.tensor_tensor_scan(
                        tr[:, c], alpha[:, 1 + d:2 + d].broadcast_to([P, S]), tr[:, c], 0.0, ALU.mult, ALU.add),
                        [m], s_dve["scan"])
                    yield
                    if d == 0:
                        m0 = do(dve, lambda e, c=c: e.tensor_scalar(tr0[:, c], tr0[:, c], bw[:, c:c + 1], None,
                                                                    ALU.mult), [m, m_bw], sd_)
                m_temporal.append(do(dve, lambda e, c=c: e.scalar_tensor_tensor(
                    out=tr0[:, c], in0=tr1[:, c], scalar=bw[:, DC + c:DC + c + 1], in1=tr0[:, c],
                    op0=ALU.mult, op1=ALU.add), [m, m0], sd_))
                yield
            for mc in range(DC):
                m_soma = yield from products(DC, feature_cols(w_soma, mc), lambda k: x[:, k], ready,
                                             activate(soma[:, mc], ACT.Gelu, mcol[:, 1, mc:mc + 1], mix_free))
            m_in = []
            for mc in range(DC):
                m = yield from products(DC, feature_cols(w_temp, mc), lambda k: tr0[:, k], m_temporal,
                                        activate(gate[:, mc], ACT.Sigmoid, mcol[:, 2, mc:mc + 1], [m_gated[mc]]))
                m_in.append(do(dve, lambda e, mc=mc: e.tensor_tensor(soma[:, mc], soma[:, mc], gate[:, mc],
                                                                     ALU.mult), [m, m_soma], sd_))
            return m_in

        def normalise(b, m_in):
            sl = s_dve["ln"]
            ts = slice(b * NT, (b + 1) * NT)
            stat_ring = Ring(list(range(4)))
            marks = []
            for t in range(NT):
                i, bk, free = bank_ring.take()
                for c in range(DC):
                    mm = do(pe, lambda e, bk=bk, c=c, t=t: e.matmul(
                        bk[:, 0:D], soma[:, c, t * P:(t + 1) * P], w_out[:, c], start=(c == 0), stop=(c == DC - 1)),
                        [*m_in, *free], s_pe["tok"] if c == DC - 1 else None)
                si_, _, sfree = stat_ring.take()
                m3 = do(act, lambda e, bk=bk, t=t: e.activation(h_tok[:, b * NT + t], bk[:, 0:D], ACT.Copy),
                        [mm], s_act["copy"])
                m1 = do(dve, lambda e, t=t, si_=si_: e.bn_stats(stats[:, si_], h_tok[:, b * NT + t]),
                        [m3, *sfree], sl)
                m2 = do(dve, lambda e, si_=si_, t=t: e.bn_aggr(mean_var[:, b * NT + t], stats[:, si_]), [m1], sl)
                stat_ring.hold(si_, m2)
                bank_ring.hold(i, m3)
                yield
            mix_free.clear()
            mix_free.append(mm)
            m = do(dve, lambda e: e.tensor_scalar(rstd[:, ts], mean_var[:, ts, 1], LN_EPS, None, ALU.add), [m2], sl)
            m = do(act, lambda e: e.activation(rstd[:, ts], rstd[:, ts], ACT.Sqrt), [m, m2], s_act["stat"])
            yield
            m = do(dve, lambda e: e.reciprocal(rstd[:, ts], rstd[:, ts]), [m], sl)
            for t in range(b * NT, (b + 1) * NT):
                mn = do(dve, lambda e, t=t: e.tensor_scalar(h_tok[:, t], h_tok[:, t], mean_var[:, t, 0:1],
                                                            rstd[:, t:t + 1], ALU.subtract, ALU.mult), [m, m3], sl)
            ht = h_tok[:, ts]
            m = do(dve, lambda e: e.tensor_tensor(ht, ht, ln_rows[:, 0:1].broadcast_to([P, NT, D]), ALU.mult),
                   [mn], sl)
            m_h = do(dve, lambda e: e.tensor_tensor(ht, ht, ln_rows[:, 1:2].broadcast_to([P, NT, D]), ALU.add),
                     [m], sl)
            yield
            for g in range(NT // 4):
                for c in range(DC):
                    i, bk, free = bank_ring.take()
                    for k in range(4):
                        mm = do(pe, lambda e, bk=bk, c=c, k=k, t=b * NT + 4 * g + k: e.transpose(
                            bk[:, k * P:(k + 1) * P], h_tok[:, t, c * P:(c + 1) * P], F["ident"]),
                            [m_h, *free], s_pe["hT"] if k == 3 else None)
                    m_hT = do(act, lambda e, bk=bk, c=c, o=b * S + g * HALF: e.activation(
                        hT[:, c, o:o + HALF], bk[:], ACT.Copy), [mm], s_act["copy"])
                    bank_ring.hold(i, m_hT)
                    yield
            scrap_ring = Ring([e_out[:, k, 0] for k in range(2)])
            for t in range(b * NT, (b + 1) * NT):
                k, sc, free = scrap_ring.take()
                m = do(act, lambda e, sc=sc, t=t: e.activation(sc, h_tok[:, t], ACT.Square,
                                                               accum_out=ssq[:, t:t + 1]), [m_h, *free], s_act["stat"])
                scrap_ring.hold(k, m)
            m = do(dve, lambda e: e.tensor_scalar(rms[:, ts], ssq[:, ts], 1.0 / D, RMS_EPS, ALU.mult, ALU.add),
                   [m], sl)
            m = do(act, lambda e: e.activation(rms[:, ts], rms[:, ts], ACT.Sqrt), [m], s_act["stat"])
            yield
            m_rms = do(dve, lambda e: e.reciprocal(rms[:, ts], rms[:, ts]), [m], sl)
            return m_h, m_hT, m_rms

        def route(b, m_h, m_hT, m_rms, last_before):
            sr = s_dve["route"]
            ts = slice(b * NT, (b + 1) * NT)
            i, bk, free = bank_ring.take()
            for t in range(NT):
                for c in range(DC):
                    mm = do(pe, lambda e, t=t, c=c: e.matmul(
                        bk[:, t * E:(t + 1) * E], hT[:, c, b * S + t * P:b * S + (t + 1) * P], w_rt[:, c],
                        start=(c == 0), stop=(c == DC - 1)), [m_hT, *free],
                        s_pe["logit"] if (t, c) == (NT - 1, DC - 1) else None)
            yield
            lg = logit[:, ts]
            m = do(dve, lambda e: e.tensor_tensor(lg, bk[:, 0:NT * E].rearrange("p (t x) -> p t x", t=NT),
                                                  rms[:, ts].unsqueeze(2).broadcast_to([P, NT, E]), ALU.mult),
                   [mm, m_rms], sr)
            bank_ring.hold(i, m)
            m = do(dve, lambda e: e.tensor_reduce(lmax[:, ts], lg, AX.X, ALU.max), [m], sr)
            m = do(dve, lambda e: e.tensor_tensor(lg, lg, lmax[:, ts].unsqueeze(2).broadcast_to([P, NT, E]),
                                                  ALU.subtract), [m], sr)
            m = do(act, lambda e: e.activation(lg, lg, ACT.Exp), [m], s_act["route"])
            yield
            for t in range(b * NT, (b + 1) * NT):
                m1 = do(dve, lambda e, t=t: e.max(out=top8[:, t], in_=logit[:, t]), [m], sr)
            m_top = m1
            for t in range(b * NT, (b + 1) * NT):
                m1 = do(dve, lambda e, t=t: e.max_index(out=best[:, t], in_max=top8[:, t], in_values=logit[:, t]),
                        [m_top], sr)
            m = do(dve, lambda e: e.tensor_copy(best_f[:, ts], best[:, ts, 0:TOPK]), [m1], sr)
            m2 = do(dve, lambda e: e.tensor_reduce(gsum[:, ts], top8[:, ts, 0:TOPK], AX.X, ALU.add), [m_top], sr)
            m2 = do(dve, lambda e: e.reciprocal(gsum[:, ts], gsum[:, ts]), [m2], sr)
            for k in range(TOPK):
                m_gain = do(dve, lambda e, k=k: e.tensor_tensor(gain[:, k, ts], top8[:, ts, k], gsum[:, ts],
                                                                ALU.mult), [m2], sr)
            marks = []
            for k in range(TOPK):
                marks.append(do(dve, lambda e, k=k: e.tensor_tensor(
                    pick[:, k, ts], F["iota_e"].unsqueeze(1).broadcast_to([P, NT, E]),
                    best_f[:, ts, k:k + 1].broadcast_to([P, NT, E]), ALU.is_equal), [m], sr))
            m = do(dve, lambda e: e.tensor_tensor(mask[:, ts], pick[:, 0, ts], pick[:, 1, ts], ALU.add), marks, sr)
            for t in range(b * NT, (b + 1) * NT):
                last_before = do(dve, lambda e, t=t: e.tensor_tensor(before[:, t + 1], before[:, t], mask[:, t],
                                                                     ALU.add), [m, last_before], sr)
            yield
            i, bk, free = bank_ring.take()
            for t in range(NT):
                do(pe, lambda e, t=t: e.matmul(bk[:, t * E:(t + 1) * E], C["ones"], before[:, b * NT + t],
                                               start=True, stop=False), [last_before, *free])
                mm = do(pe, lambda e, t=t: e.matmul(bk[:, t * E:(t + 1) * E], C["before"], mask[:, b * NT + t],
                                                    start=False, stop=True), [], s_pe["pos"])
            yield
            pos = bk[:, 0:NT * E].rearrange("p (t x) -> p t x", t=NT)
            m = do(dve, lambda e: e.tensor_scalar(far[:, ts], pos, float(CAP), FAR, ALU.is_ge, ALU.mult), [mm], sr)
            m1 = do(dve, lambda e: e.tensor_tensor(slot_map[:, ts], pos,
                                                   F["slot_e"].unsqueeze(1).broadcast_to([P, NT, E]), ALU.add), [mm], sr)
            bank_ring.hold(i, m1)
            m = do(dve, lambda e: e.tensor_tensor(slot_map[:, ts], slot_map[:, ts], far[:, ts], ALU.add), [m, m1], sr)
            for k in range(TOPK):
                m1 = do(dve, lambda e, k=k: e.tensor_tensor(pick[:, k, ts], pick[:, k, ts], slot_map[:, ts],
                                                            ALU.mult), [m], sr)
                m1 = do(dve, lambda e, k=k: e.tensor_reduce(slot[:, k, ts], pick[:, k, ts], AX.X, ALU.add), [m1], sr)
                m_w = do(dve, lambda e, k=k: e.tensor_copy(slot_w[:, k, ts], slot[:, k, ts]), [m1], sr)
                m_r = do(dve, lambda e, k=k: e.tensor_scalar(slot_r[:, k, ts], slot[:, k, ts], float(SLOTS), None,
                                                             ALU.min), [m1], sr)
            for t in range(b * NT, (b + 1) * NT):
                for k in range(TOPK):
                    m_sent = pool.add(lambda e, t=t, k=k: e.indirect_dma_start(
                        out=slots_in, out_offset=bass.IndirectOffsetOnAxis(ap=slot_w[:, k, t:t + 1], axis=0),
                        in_=h_tok[:, t], in_offset=None, bounds_check=SLOTS - 1, oob_is_err=False),
                        [m_w, m_h, m_zero], s_sent[b], 16)
            return last_before, m_sent, m_r, m_gain

        s_sent = [sem(f"tokens_sent{b}") for b in range(B)]
        sent = {}

        def normalised(b):
            m_h, m_hT, m_rms = yield from normalise(b, (yield from mix(b)))
            h_marks[b] = m_h, m_hT, m_rms

        def routed(b):
            sent[b] = yield from route(b, *h_marks[b], sent[b - 1][0] if b else m_before)

        h_marks = {}
        for _ in normalised(0):
            pass

        def rest():
            yield from routed(0)
            yield from normalised(1)
            yield from routed(1)

        def w_slot(k):
            o = 3 * 2 * S * k
            g, u, dn = (big[:, o + j * 2 * S:o + (j + 1) * 2 * S] for j in range(3))
            return (g.rearrange("p (c m) -> p c m", c=DC), u.rearrange("p (c m) -> p c m", c=DC),
                    dn.rearrange("p (i n) -> p i n", i=I_R // P))

        expert_ring = Ring([w_slot(0), w_slot(1)])
        s_we = [sem("load_expert0"), sem("load_expert1")]
        mixed = []
        expert_w = {}

        def load_expert(x):
            k, (g, u, dn), free = expert_ring.take()
            for dst, src in ((g, chunks(A["rg"][x])), (u, chunks(A["ru"][x])), (dn, chunks(A["rd"][x]))):
                m = dma(sp, dst, src, [*mixed, *free], s_we[k])
            expert_w[x] = (k, g, u, dn, m)

        gu_ring = Ring(wide[:2])
        acc_ring = Ring(wide[2:])
        sil_ring = Ring([sil[:, 0], sil[:, 1]])
        act_ring = Ring([act_s[:, k] for k in range(3)])
        def gate_up(n, wg_, wu_, col, src, ready, dst, dst_free):
            i, gu, free = gu_ring.take()
            for o, wt in ((0, wg_), (HALF, wu_)):
                for c in range(DC):
                    mm = do(pe, lambda e, o=o, wt=wt, c=c: e.matmul(
                        gu[:, o:o + n], wt[:, c, col:col + P], src(c), start=(c == 0), stop=(c == DC - 1)),
                        [*ready, *free], s_pe["gu"] if c == DC - 1 and o else None)
            k, sl_, sfree = sil_ring.take()
            m = do(act, lambda e: e.activation(sl_[:, 0:n], gu[:, 0:n], ACT.Silu), [mm, *sfree], s_act["silu"])
            m = do(dve, lambda e: e.tensor_tensor(dst, sl_[:, 0:n], gu[:, HALF:HALF + n], ALU.mult),
                   [m, *dst_free], s_dve["act"])
            gu_ring.hold(i, m)
            sil_ring.hold(k, m)
            return m

        def shared(tc, others=iter(())):
            n_i, tiles = I_S // P, HALF // P
            ai, acc, afree = acc_ring.take()
            def down(i, k, a, m):
                for t in range(tiles):
                    mm = do(pe, lambda e, t=t: e.matmul(
                        acc[:, t * D:(t + 1) * D], a[:, t * P:(t + 1) * P], wsd[:, i],
                        start=(i == 0 and t % 2 == 0), stop=False, skip_group_check=True),
                        [m, m_sd, *afree], s_pe["down"] if t == tiles - 1 else None)
                act_ring.hold(k, mm)
            late = None
            for i in range(n_i):
                k, a, free = act_ring.take()
                m = gate_up(HALF, wsg, wsu, i * P, lambda c: hT[:, c, tc * HALF:(tc + 1) * HALF],
                            [h_marks[tc * HALF // S][1], m_sg, m_su], a, free)
                if late:
                    down(*late)
                for _ in range(STEPS_PER_COLUMN):
                    next(others, None)
                late = (i, k, a, m)
            down(*late)
            for t in range(tiles):
                for c in range(DC):
                    mm = do(pe, lambda e, t=t, c=c: e.matmul(
                        acc[:, t * D + c * P:t * D + (c + 1) * P],
                        xT[:, c, tc * HALF + t * P:tc * HALF + (t + 1) * P], F["ident"],
                        start=False, stop=True, skip_group_check=True), [], s_pe["down"])
            yt = y[:, tc * tiles:(tc + 1) * tiles]
            for t in range(tiles):
                m = do(act, lambda e, t=t: e.activation(yt[:, t], acc[:, t * D:(t + 1) * D], ACT.Copy),
                       [mm, sent[tc * HALF // S][1]], s_act["copy"])
            acc_ring.hold(ai, m)
            return m

        second = rest()
        m_shared = {0: shared(0, second), 1: shared(1, second)}
        for _ in second:
            pass
        _, _, m_r, m_gain = sent[1]
        m_sent = [sent[b][1] for b in range(B)]
        mixed += [(s_, s_.value) for s_ in (s_pe["tok"], s_pe["mix"], s_dve["mix"], s_dve["scan"], s_act["stat"])]
        load_expert(0)
        load_expert(1)
        m_shared[2] = shared(2)

        xg_ring, xgT_ring, eo_ring = (Ring([0, 1]) for _ in range(3))
        s_xg = [sem("load_tokens0"), sem("load_tokens1")]
        s_eo = [sem("store_expert0"), sem("store_expert1")]
        act_e_ring = Ring([act_e])
        act_e_ring.hold(0, *mixed)
        for k in range(2):
            eo_ring.hold(k, *mixed)
        TILES = [(0, P), (P, P), (2 * P, CAP - 2 * P)]

        def fetch(x):
            k, _, free = xg_ring.take()
            rows = slots_in[x * CAP:(x + 1) * CAP, :]
            dma(sp, xg[:, k, 0:2], rows[0:2 * P, :].rearrange("(t p) n -> p t n", p=P), [*m_sent, *free], s_xg[k])
            m = dma(sp, xg[0:CAP - 2 * P, k, 2], rows[2 * P:CAP, :], [], s_xg[k])
            kt, _, tfree = xgT_ring.take()
            for c in range(DC):
                i, bk, bfree = bank_ring.take()
                for t, (o, n) in enumerate(TILES):
                    mm = do(pe, lambda e, c=c, t=t, o=o, n=n, bk=bk: e.transpose(
                        bk[:, o:o + n], xg[0:n, k, t, c * P:(c + 1) * P], F["ident"][0:n, 0:n]), [m, *bfree],
                        s_pe["xT"] if t == 2 else None)
                m2 = do(act, lambda e, c=c, bk=bk: e.activation(xgT[:, kt, c], bk[:, 0:CAP], ACT.Copy),
                        [mm, *tfree], s_act["copy"])
                bank_ring.hold(i, m2)
            xg_ring.hold(k, mm)
            return kt, m2

        fetched = {0: fetch(0)}
        stored_e = []
        for x in range(E):
            k, wg_, wu_, wd_, m_w = expert_w[x]
            kt, m_x_ = fetched[x]
            _, _, ae_free = act_e_ring.take()
            ai, acc, afree = acc_ring.take()

            def down_e(i, m, wd_=wd_, acc=acc, afree=afree):
                for t, (o, n) in enumerate(TILES):
                    mm = do(pe, lambda e, t=t, o=o, n=n: e.matmul(
                        acc[0:n, t * D:(t + 1) * D], act_e[:, i, o:o + n], wd_[:, i],
                        start=(i == 0 and t % 2 == 0), stop=(i == I_R // P - 1), skip_group_check=True),
                        [m, *afree], s_pe["down"] if t == len(TILES) - 1 else None)
                return mm

            late = None
            for i in range(I_R // P):
                m = gate_up(CAP, wg_, wu_, i * P, lambda c, kt=kt: xgT[:, kt, c], [m_w, m_x_], act_e[:, i], ae_free)
                if late:
                    down_e(*late)
                late = (i, m)
                if i == 3 and x + 1 < E:
                    fetched[x + 1] = fetch(x + 1)
            xgT_ring.hold(kt, (s_pe["gu"], s_pe["gu"].value))
            mm = down_e(*late)
            act_e_ring.hold(0, mm)
            expert_ring.hold(k, mm)
            if x + 2 < E:
                load_expert(x + 2)
            ko, _, ofree = eo_ring.take()
            do(dve, lambda e, ko=ko, acc=acc: e.tensor_copy(
                e_out[:, ko, 0:2], acc[:, 0:2 * D].rearrange("p (t n) -> p t n", t=2)), [mm, *ofree], s_dve["copy"])
            m = do(dve, lambda e, ko=ko, acc=acc: e.tensor_copy(e_out[0:CAP - 2 * P, ko, 2],
                                                                acc[0:CAP - 2 * P, 2 * D:3 * D]), [], s_dve["copy"])
            acc_ring.hold(ai, m)
            rows = slots_out[x * CAP:(x + 1) * CAP, :]
            dma(sp, rows[0:2 * P, :].rearrange("(t p) n -> p t n", p=P), e_out[:, ko, 0:2], [m], s_eo[ko])
            m = dma(sp, rows[2 * P:CAP, :], e_out[0:CAP - 2 * P, ko, 2], [], s_eo[ko])
            eo_ring.hold(ko, m)
            stored_e = (stored_e + [m])[-2:]

        got_ring = Ring(list(range(len(got))))
        for k in range(len(got)):
            got_ring.hold(k, *mixed)
        s_got = [sem(f"gather{k}") for k in range(len(got))]
        s_done = sem("store_out")
        gathered = {}

        def gather(t):
            for k in range(TOPK):
                g, _, free = got_ring.take()
                mg = pool.add(lambda e, g=g, k=k: e.indirect_dma_start(
                    out=got[g], out_offset=None, in_=slots_out,
                    in_offset=bass.IndirectOffsetOnAxis(ap=slot_r[:, k, t:t + 1], axis=0)),
                    [*stored_e, m_r, m_zero, *free], s_got[g], 16)
                gathered[t, k] = g, mg

        def combine(t):
            m = m_shared[t * P // HALF]
            for k in range(TOPK):
                g, mg = gathered[t, k]
                m = do(dve, lambda e, g=g, k=k: e.scalar_tensor_tensor(
                    out=y[:, t], in0=got[g], scalar=gain[:, k, t:t + 1], in1=y[:, t],
                    op0=ALU.mult, op1=ALU.add), [mg, m, m_gain], s_dve["comb"])
                got_ring.hold(g, m)
            return dma(sp, out[t * P:(t + 1) * P, :], y[:, t], [m], s_done)

        AHEAD = len(got) // TOPK
        last_chunk = B * NT - HALF // P

        def early():
            for t in range(AHEAD):
                gather(t)
            for _ in range(6):
                yield
            for t in range(last_chunk):
                combine(t)
                gather(t + AHEAD)
                yield

        others = early()
        m_shared[T // HALF - 1] = shared(T // HALF - 1, others)
        for _ in others:
            pass
        for t in range(last_chunk, B * NT):
            md = combine(t)
        ph2.close()
        sp.items.append(([md], None, None, 0))

        block = ctx.enter_context(nc.Block())

        @block.sync
        def _(e):
            sp.emit(e)

        @block.gpsimd
        def _(e):
            pool.emit(e)

        @block.scalar
        def _(e):
            act.emit(e)

        @block.vector
        def _(e):
            dve.emit(e)

        @block.tensor
        def _(e):
            pe.emit(e)




def constants():
    import numpy as np

    f = np.zeros((P, CF_W), np.float32)
    f[:, :P] = np.eye(P)
    for par in range(2):
        for g in range(QUAD):
            for d in range(DH):
                col = par * P + par * (P // 2) + g * DH + d
                f[g * HB + d, CF["sel_num"][0] + col] = 1
                f[g * HB + DH, CF["sel_den"][0] + col] = 1
    a = CF["iota_e"][0]
    f[:, a:a + E] = np.arange(E)
    f[:, a + E:a + 2 * E] = np.arange(E) * CAP
    r, c = np.arange(P)[:, None], np.arange(P)[None, :]
    b = np.concatenate([np.eye(P), np.where(c > r, NEG, 0), np.where(r > c, NEG, 0), r < c, np.ones((P, P)),
                        np.broadcast_to(c, (P, P))], 1)
    span = np.where(r // K_SPARSE == np.arange(SPANS * NT)[None, :] // NT, np.arange(SPANS * NT)[None, :] % NT, -1)
    return {"const_f32": f, "const_bf16": b.astype(mybir.dt.np(BF16)), "span_iota": span.astype(mybir.dt.np(BF16))}


def layout(inputs):
    import numpy as np

    i = {k: np.asarray(v) for k, v in inputs.items()}
    a = constants()
    a["xT"] = i["x"].reshape(T, D).T
    def by_span(m):
        return np.ascontiguousarray(m.reshape(SPANS, SPAN, K_SPARSE).transpose(0, 2, 1)).reshape(P, SPAN)

    a["idx"] = by_span(i["itok_Sx32_0_1023"])
    a["idx_mask"] = by_span(i["mask_Sx32_bk1"]).view(np.int32)
    a["prior"] = i["mask_SxS_bk0"].view(np.int32)
    a["priorT"] = i["mask_SxS_bk0"].T.copy().view(np.int32)
    a["u_prev"] = i["condB_uprev"]
    a["w_prior"] = np.concatenate([i[f"L0_cond_W{n}"].T for n in "qkv"], 1)
    a["w_causal"] = i["L0_attn_W_kqv"].T
    a["w_o"] = i["L0_cond_Wo"].T
    a["w_proj"] = i["L0_attn_W_proj"].T
    bk = i["L0_attn_b_kqv"]
    a["bias_cols"] = np.stack([i["L0_cond_bq"], i["L0_cond_bk"], bk[D:2 * D], bk[:D], i["L0_cond_bo"],
                               i["L0_attn_b_proj"]])
    a["bias_v"] = np.stack([i["L0_cond_bv"], bk[2 * D:]])
    c2 = "L0_cond2_"
    a["taus"] = np.concatenate([i[c2 + "tau_ctx"].reshape(1), i["condB_tauraws"]])
    a["w_g"] = i[c2 + "Wg"].T
    a["w_n1"] = i[c2 + "Wn1"].T
    a["w_n2"] = np.repeat(i["cond_256"].T[:, :, None], P, 2)
    a["b_n2"] = i["condB_bn2"]
    a["b_n1"] = i[c2 + "bn1"].reshape(HN, 1)
    a["blend"] = i["cond_1024"]
    a["w_soma"] = i[c2 + "Wsoma"].T
    a["w_temp"] = i[c2 + "Wtemp"].T
    a["w_out"] = i[c2 + "Wout"].T
    a["mix_cols"] = np.stack([i[c2 + "bg"], i[c2 + "bsoma"], i[c2 + "btemp"]])
    a["ln_rows"] = np.stack([i[c2 + "gamma"], i[c2 + "beta"]])
    a["w_router"] = i["L0_ffn_router_w"].T
    for n in ("rg", "ru", "rd", "sg", "su", "sd"):
        a[n] = i["L0_ffn_" + n]
    for n in ("bias_cols", "mix_cols", "blend"):
        a[n] = a[n].reshape(-1, DC, P).transpose(2, 0, 1)
    return {k: np.ascontiguousarray(v) for k, v in a.items()}


def kernel(**inputs):
    import concourse.bacc as bacc
    import numpy as np
    from concourse.bass_utils import run_bass_kernel_spmd

    arrays = layout(inputs)
    nc = bacc.Bacc("TRN2", target_bir_lowering=False, num_devices=1)
    A = {k: nc.dram_tensor(k, v.shape, mybir.dt.from_np(v.dtype), kind="ExternalInput").ap()
         for k, v in arrays.items()}
    out = nc.dram_tensor("out", (T, D), F32, kind="ExternalOutput").ap()
    build(nc, A, out)
    r = run_bass_kernel_spmd(nc, [arrays], core_ids=[0])
    return np.asarray(r.results[0]["out"]).reshape(B, S, D)
```
